# Optimizing a Trainium2 kernel written in Bass

```python
import numpy as np
import jax
import jax.numpy as jnp

def _softmax(x, axis=-1):
    return jax.nn.softmax(x, axis=axis)

def _gelu(x):
    return jax.nn.gelu(x, approximate=True)

def _silu(x):
    return jax.nn.silu(x)

def _sigmoid(x):
    return jax.nn.sigmoid(x)

def _layernorm(x, axis=-1, eps=1e-05):
    m = jnp.mean(x, axis=axis, keepdims=True)
    v = jnp.var(x, axis=axis, keepdims=True)
    return (x - m) / jnp.sqrt(v + eps)

def _scatter_add(tgt, idx, src, axis=0):
    return tgt.at[idx].add(src)

def _segment_sum(src, seg, n):
    return jax.ops.segment_sum(src, seg, n)
kernel_name = 'mk_gnn_resnorm_d2_gnn_r32_2c7373'

def setup_inputs(seed: int=0):
    np.random.seed(seed)
    _w = jnp.asarray

    def _rec_inputs():
        import jax
        import jax.numpy as jnp
        _gk = jax.random.key(seed)
        x = -0.0002117 + 1 * jax.random.normal(jax.random.fold_in(_gk, 1), (3125, 256), jnp.float32)
        src = jax.random.randint(jax.random.fold_in(_gk, 2), (50000,), 0, 3125, jnp.int32)
        dst = jnp.minimum((3125 * jax.random.uniform(jax.random.fold_in(_gk, 3), (50000,)) ** 2.0).astype(jnp.int32), 99999)
        _o = jnp.argsort(dst, stable=True)
        src = src[_o]
        dst = dst[_o]
        edge_attr_3 = -1.09012e-05 + 0.99985 * jax.random.normal(jax.random.fold_in(_gk, 12), (50000, 3), jnp.float32)
        edge_weight = jax.random.uniform(jax.random.fold_in(_gk, 14), (50000,), jnp.float32, 0.0, 1)
        return (x, src, dst, edge_attr_3, edge_weight)
    x, src, dst, edge_attr_3, edge_weight = _rec_inputs()

    def _L0_gnn_setup():
        import jax, jax.numpy as jnp
        import numpy as np
        N_NODES = 3125
        NNZ = 100000
        DIM = 256
        HOPS = 3
        key = jax.random.key(seed)
        ks = jax.random.split(key, 8)
        m = jax.random.normal(ks[0], (N_NODES, DIM), dtype=jnp.float32)
        vals = jax.random.uniform(ks[1], (NNZ,), dtype=jnp.float32)
        scale = 1.0 / np.sqrt(DIM)
        Wn = jax.random.normal(ks[2], (HOPS, DIM, DIM), dtype=jnp.float32) * scale
        bn = jax.random.normal(ks[3], (HOPS, DIM), dtype=jnp.float32) * 0.01
        Ws = jax.random.normal(ks[4], (HOPS, DIM, DIM), dtype=jnp.float32) * scale
        bs = jax.random.normal(ks[5], (HOPS, DIM), dtype=jnp.float32) * 0.01
        rows = jax.random.randint(ks[6], (NNZ,), 0, N_NODES, dtype=jnp.int64)
        cols = jax.random.randint(ks[7], (NNZ,), 0, N_NODES, dtype=jnp.int64)
        return {'m': m, 'vals': vals, 'Wn': Wn, 'bn': bn, 'Ws': Ws, 'bs': bs, 'rows': rows, 'cols': cols}
    _L0_gnn_all = _L0_gnn_setup()
    _L0_gnn_in = {k: v for k, v in _L0_gnn_all.items() if k in ('Wn', 'bn', 'Ws', 'bs')}
    del _L0_gnn_all

    def _L1_gnn_setup():
        import jax, jax.numpy as jnp
        import numpy as np
        N = 50000
        E = 12500
        IN = 256
        H = 8
        D = 32
        EF = 3
        key = jax.random.key(seed)
        ks = jax.random.split(key, 8)
        x = jax.random.normal(ks[0], (N, IN), dtype=jnp.float32)
        edge_index = jax.random.randint(ks[1], (2, E), 0, N, dtype=jnp.int64)
        edge_attr = jax.random.normal(ks[2], (E, EF), dtype=jnp.float32)
        W = jax.random.normal(ks[3], (H * D, IN), dtype=jnp.float32) * np.float32(np.sqrt(2.0 / (IN + H * D)))
        a_src = jax.random.normal(ks[4], (H, D), dtype=jnp.float32) * np.float32(np.sqrt(2.0 / (H + D)))
        a_dst = jax.random.normal(ks[5], (H, D), dtype=jnp.float32) * np.float32(np.sqrt(2.0 / (H + D)))
        edge_W = jax.random.normal(ks[6], (H * D, EF), dtype=jnp.float32) * np.float32(np.sqrt(2.0 / (EF + H * D)))
        edge_b = jnp.zeros((H * D,), dtype=jnp.float32)
        bias = jnp.zeros((H * D,), dtype=jnp.float32)
        return {'x': x, 'W': W, 'a_src': a_src, 'a_dst': a_dst, 'edge_W': edge_W, 'edge_b': edge_b, 'bias': bias, 'edge_attr': edge_attr, 'edge_index': edge_index}
    _L1_gnn_all = _L1_gnn_setup()
    _L1_gnn_in = {k: v for k, v in _L1_gnn_all.items() if k in ('W', 'a_src', 'a_dst', 'edge_W', 'edge_b', 'bias')}
    del _L1_gnn_all
    return {'x': x, 'src': src, 'dst': dst, 'edge_attr_3': edge_attr_3, 'edge_weight': edge_weight, 'L0_gnn_Wn': _L0_gnn_in['Wn'], 'L0_gnn_bn': _L0_gnn_in['bn'], 'L0_gnn_Ws': _L0_gnn_in['Ws'], 'L0_gnn_bs': _L0_gnn_in['bs'], 'L1_gnn_W': _L1_gnn_in['W'], 'L1_gnn_a_src': _L1_gnn_in['a_src'], 'L1_gnn_a_dst': _L1_gnn_in['a_dst'], 'L1_gnn_edge_W': _L1_gnn_in['edge_W'], 'L1_gnn_edge_b': _L1_gnn_in['edge_b'], 'L1_gnn_bias': _L1_gnn_in['bias']}

def reference(x, src, dst, edge_attr_3, edge_weight, L0_gnn_Wn, L0_gnn_bn, L0_gnn_Ws, L0_gnn_bs, L1_gnn_W, L1_gnn_a_src, L1_gnn_a_dst, L1_gnn_edge_W, L1_gnn_edge_b, L1_gnn_bias):
    import jax
    import jax.numpy as jnp

    def _L0_gnn_ref(m, vals, Wn, bn, Ws, bs, rows, cols):
        import jax, jax.numpy as jnp
        import numpy as np
        N_NODES = 3125
        NNZ = 100000
        DIM = 256
        HOPS = 3
        N = m.shape[0]
        hop_num = Wn.shape[0]
        H = m
        for i in range(hop_num):
            msg = H[cols] * vals[:, None]
            Hn = jax.ops.segment_sum(msg, rows, num_segments=N)
            Hn = Hn @ Wn[i].T + bn[i]
            Hs = H @ Ws[i].T + bs[i]
            H = Hn + Hs
            if i != hop_num - 1:
                H = jax.nn.elu(H)
        return H

    def _L1_gnn_ref(x, W, a_src, a_dst, edge_W, edge_b, bias, edge_attr, edge_index):
        import jax, jax.numpy as jnp
        import numpy as np
        N = 50000
        E = 12500
        IN = 256
        H = 8
        D = 32
        EF = 3
        n = x.shape[0]
        h = (x @ W.T).reshape(n, H, D)
        src, dst = (edge_index[0], edge_index[1])
        h_src = h[src]
        h_dst = h[dst]
        alpha = jnp.einsum('ehd,hd->eh', h_src, a_src) + jnp.einsum('ehd,hd->eh', h_dst, a_dst)
        enc = jax.nn.relu(edge_attr @ edge_W.T + edge_b).reshape(-1, H, D)
        alpha = alpha + jnp.sum(enc * h_dst, axis=-1)
        alpha = jnp.where(alpha >= 0, alpha, 0.2 * alpha)
        amax = jax.ops.segment_max(alpha, dst, num_segments=n)
        ex = jnp.exp(alpha - amax[dst])
        denom = jax.ops.segment_sum(ex, dst, num_segments=n)
        attn = ex / jnp.maximum(denom[dst], 1e-10)
        out = jax.ops.segment_sum(h_src * attn[..., None], dst, num_segments=n)
        return out.reshape(n, H * D) + bias
    edge_index = jnp.stack([src, dst])
    x = _layernorm(x + _L0_gnn_ref(x, edge_weight, L0_gnn_Wn, L0_gnn_bn, L0_gnn_Ws, L0_gnn_bs, src, dst), axis=-1)
    x = _layernorm(x + _L1_gnn_ref(x, L1_gnn_W, L1_gnn_a_src, L1_gnn_a_dst, L1_gnn_edge_W, L1_gnn_edge_b, L1_gnn_bias, edge_attr_3, edge_index), axis=-1)
    return x

_drawn_inputs = setup_inputs


def setup_inputs(seed=0):
    import zlib

    import numpy as np

    out = dict(_drawn_inputs(seed))
    spreads = {'L1_gnn_edge_b': (0.0, 0.8), 'L1_gnn_bias': (0.0, 0.1)}
    factors = {'edge_attr_3': 2.862,
     'L0_gnn_bn': 7.26,
     'L0_gnn_bs': 6.295,
     'L1_gnn_a_src': 3.332,
     'L1_gnn_a_dst': 8.0}
    for name, (base, spread) in spreads.items():
        noise = np.random.default_rng([zlib.crc32(name.encode()), seed]).standard_normal(out[name].shape)
        drawn = base * np.exp(spread * noise) if base else spread * noise
        out[name] = jnp.asarray(drawn.astype(out[name].dtype))
    for name, factor in factors.items():
        out[name] = (out[name] * factor).astype(out[name].dtype)
    return out
```

```python
from contextlib import ExitStack

import numpy as np
import concourse.bass as bass
from concourse import mybir

F32 = mybir.dt.float32
BF16 = mybir.dt.bfloat16
I32 = mybir.dt.int32
ALU = mybir.AluOpType
ACT = mybir.ActivationFunctionType
X = mybir.AxisListType.X

P = 128
SHIFT = 7
N = 3125
D = 256
E = 50000
HOPS = 3
HEADS = 8
HD = D // HEADS
EF = 3
NW = 26
HI = 32
USED = (N + P - 1) // P
EP = 125
EC = E // EP
U = 8
NC = 416
assert EP * EC == E and EC % U == 0 and NC % 16 == 0 and NC % U == 0 and NW % 2 == 0
assert NC >= (E + USED * (P - 1)) // P and NW * P >= N
REC = 8
HX = D + HEADS
NB = NC // 16
BIG = 1.0e38
EPS = 1e-5


def build(nc, x, src, dst, edge_attr, edge_weight, Wn, bn, Ws, bs, W, a_src, a_dst, edge_W, edge_b, bias, out,
          debug=()):
    dbg = dict(debug)
    with ExitStack() as ctx:
        def sb(name, shape, dt=F32, where=ctx):
            return where.enter_context(nc.sbuf_tensor(name, shape, dt))

        def sem(name):
            return ctx.enter_context(nc.semaphore(name))

        def dram(name, shape):
            return nc.dram_tensor(name, shape, F32, kind="Internal").ap()

        rows_dram = [dram("rows_by_src", [P * NC, REC]), dram("rows_by_dst", [P * NC, REC])]
        h_dram = [dram("h_even", [NW * P, D]), dram("h_odd", [NW * P, D])]
        hh_dram = dram("gat_h", [NW * P, D])
        ss_dram = dram("gat_s_src", [NW * P, HEADS])
        edge_dram = dram("chunk_ends", [P, NB * 4])
        carry_dram = dram("chunk_carries", [HEADS, 16 * NB * 2])

        identf = sb("identf", [P, P])
        identb = sb("identb", [P, P], BF16)
        tri = sb("tri", [P, P])
        triu = sb("triu", [P, P])
        ones = sb("ones", [P, P])
        iota_i = sb("iota_i", [P, NC], I32)
        iota_f = sb("iota_f", [P, NC])
        iota_b = sb("iota_b", [P, P], BF16)
        lane_i = sb("lane_i", [P, 1], I32)
        lane_f = sb("lane_f", [P, 1])
        win = [sb("win_src", [1, NC], I32), sb("win_dst", [1, NC], I32)]
        wT = sb("wT", [P, 2 * HOPS + 1, 2, D])
        bias2 = sb("bias2", [2, HOPS, D])
        ew4 = sb("ew4", [4, D])
        asrc_b = sb("asrc_b", [P, D])
        adst_b = sb("adst_b", [P, D])
        bias_b = sb("bias_b", [P, D])

        sort = ExitStack()
        src_i = sb("src_i", [P, EC], I32, sort)
        dst_i = sb("dst_i", [P, EC], I32, sort)
        w_in = sb("w_in", [P, EC], F32, sort)
        ea_in = sb("ea_in", [P, EC, EF], F32, sort)
        rec = sb("rec", [P, EC, REC], F32, sort)
        key_f = sb("key_f", [P, EC + U], F32, sort)
        kst = sb("kst", [P, U], F32, sort)
        lo_i = sb("lo_i", [P, EC], I32, sort)
        lo_f = sb("lo_f", [P, EC], F32, sort)
        hi_f = sb("hi_f", [P, EC], F32, sort)
        ohlo = sb("ohlo", [P, EC, P], BF16, sort)
        ohhi = sb("ohhi", [P, EC, HI], BF16, sort)
        ohhiT = sb("ohhiT", [HI, U, EP], F32, sort)
        hist = sb("hist", [HI, P], F32, sort)
        table0 = sb("table0", [HI, P], F32, sort)
        table = sb("table", [HI, 2, P], F32, sort)
        small = sb("small", [HI, 8], F32, sort)
        small_i = sb("small_i", [HI, 2], I32, sort)
        started = sb("started", [HI, NC], F32, sort)
        terms = sb("terms", [P, 2, 4, 2 * P], F32, sort)
        rank = sb("rank", [P, U], F32, sort)
        pos_i = sb("pos_i", [P, 3, U], I32, sort)
        leaving = sb("leaving", [P, 2, U, REC], F32, sort)
        place = sb("place", [P, 2, U], I32, sort)
        wraw = sb("wraw", [P, 2, D], F32, sort)
        sort.close()

        recs = [sb("recs_src", [P, NC + U, REC]), sb("recs_dst", [P, NC + U, REC])]
        fst = sb("fst", [P, U, REC])
        lo_s = sb("lo_s", [P, NC])
        lo_si = sb("lo_si", [P, NC], I32)
        acc = sb("acc", [P, NW, HX])
        hcur = sb("hcur", [P, NW, D])
        x0 = sb("x0", [P, NW, HX])
        stg = sb("stg", [P, 2, 2 * D])
        stgT = sb("stgT", [P, 2, 2 * D])
        elu = sb("elu", [P, 2, 2 * D])
        gath = sb("gath", [P, U, D])
        idx = sb("idx", [P, U], I32)
        onehot = sb("onehot", [P, 4, P])
        val = sb("val", [P, 4, HX])
        encr = stg[:, 0, :].rearrange("p (s d) -> p s d", s=2)
        prod = stg[:, 1, :].rearrange("p (s d) -> p s d", s=2)
        eaT = stgT[0:4, :, :]
        stat = sb("stat", [P, NW, 4])
        s_sb = sb("s_sb", [P, NC, HEADS])
        dot = sb("dot", [P, NC, HEADS])
        sde = sb("sde", [P, NC, HEADS])
        alT = recs[0][:, 0:NC, :].rearrange("p (b c) k -> p b (c k)", b=NB)
        ends = sb("ends", [P, NB, 4])
        brk = acc[:, :, :].rearrange("p w d -> p (w d)")[:, 0:NB * (P + 1)]
        x0f = x0[:, :, :].rearrange("p w d -> p (w d)")
        el = x0f[0:HEADS, 0:8 * NC].rearrange("h (k c) -> h k c", k=8)
        eh = x0f[0:HEADS, 8 * NC:12 * NC].rearrange("h (c b k) -> h c b k", c=16, k=4)
        eo = x0f[0:HEADS, 12 * NC:14 * NC].rearrange("h (c b k) -> h c b k", c=16, k=2)
        cin = sb("cin", [P, NB, 2])
        s_src = sb("s_src", [P, NW, HEADS])

        bank = [ctx.enter_context(nc.psum_tensor(f"bank{i}", [P, 512], F32)) for i in range(8)]

        s_const = sem("consts_made")
        s_lane = sem("iota_made")
        s_in = sem("edges_loaded")
        s_w = sem("weight_block_loaded")
        s_wT_pe = sem("weight_transposed")
        s_wT = sem("weight_stored")
        s_small = sem("small_weights_loaded")
        s_rec = sem("records_built")
        s_fill = sem("rows_prefilled")
        s_keys = sem("keys_split")
        s_oh = sem("onehots_built")
        s_hist = sem("histogram_done")
        s_d = sem("vector_step")
        s_hd = sem("histogram_step")
        s_cum = sem("window_starts_summed")
        s_base = sem("base_table_made")
        s_win = sem("windows_counted")
        s_seed = sem("table_seeded")
        s_hiT = sem("window_onehot_transposed")
        s_hiTs = sem("window_onehot_stored")
        s_row = sem("keys_broadcast")
        s_tab = sem("table_copied")
        s_look = sem("table_read")
        s_upd = sem("table_updated")
        s_rank = sem("ranks_taken")
        s_eq = sem("rank_terms_ready")
        s_pos = sem("positions_ready")
        s_scat = [sem("records_scattered_even"), sem("records_scattered_odd")]
        s_leave = sem("records_leaving")
        s_idx = sem("indices_staged")
        s_back = sem("records_read_back")
        s_lo = sem("los_ready")
        s_x = sem("x_loaded")
        s_lo7 = sem("lo_in_records")
        s_kst = sem("keys_staged")
        s_fst = sem("records_staged")
        s_x0z = sem("x_tail_cleared")
        s_clr = sem("acc_cleared")
        s_g = [sem(f"rows_gathered{i}") for i in range(U)]
        s_oneh = sem("onehot_made")
        s_mm = sem("chunk_summed")
        s_add = sem("chunk_added")
        s_stg = sem("window_staged")
        s_stT = sem("window_transposed")
        s_stTs = sem("window_transpose_stored")
        s_lin = sem("window_multiplied")
        s_ea = sem("elu_parts")
        s_em = sem("elu_min")
        s_new = sem("window_done")
        s_hst = sem("h_stored")
        s_ln = sem("layer_norm_step")
        s_sq = sem("layer_norm_root")
        s_ss = sem("s_gathered")
        s_eaT = sem("features_transposed")
        s_eaTs = sem("features_stored")
        s_lrow = sem("lo_broadcast")
        s_enc = sem("edge_encoded")
        s_relu = sem("encoding_clipped")
        s_hd_ = sem("h_dst_looked_up")
        s_sde = sem("s_dst_copied")
        s_dot = sem("dot_taken")
        s_al = sem("alpha_step")
        s_alT = sem("alpha_transposed")
        s_alTs = sem("alpha_transpose_stored")
        s_end = sem("chunk_ends_moved")
        s_mx = sem("max_ready")
        s_ex = sem("exp_done")
        s_exT = sem("exp_transposed")
        s_exs = sem("exp_stored")
        s_val = sem("values_scaled")
        s_vx = sem("exp_column_copied")
        s_out = sem("out_stored")
        s_dbg = sem("dbg")

        def nodes(t, cols=None):
            return t.rearrange("(w p) d -> p w d", p=P)

        groups = EC // U

        def turn(k):
            return k if k < HOPS else k + 1
        FULLW = N // P

        zero_tile = ohlo[:, 0:NC * REC * 2 // P, :].bitcast(F32).rearrange("p a b -> p (a b)")

        LN_STEPS = 6
        AL_ENDS = 6
        AL_CARRY = 17
        dotT = dot[:, :, :].rearrange("p (b c) h -> p b (c h)", b=NB)
        sdeT = sde[:, :, :].rearrange("p (b c) h -> p b (c h)", b=NB)
        brk3 = brk.rearrange("p (b e) -> p b e", b=NB)

        block = ctx.enter_context(nc.Block())

        @block.sync
        def _(sp):
            sp.dma_start(src_i[0:EP, :], src.rearrange("(p c) -> p c", c=EC)).then_inc(s_in, 16)
            sp.dma_start(dst_i[0:EP, :], dst.rearrange("(p c) -> p c", c=EC)).then_inc(s_in, 16)
            sp.dma_start(w_in[0:EP, :], edge_weight.rearrange("(p c) -> p c", c=EC)).then_inc(s_in, 16)
            sp.dma_start(ea_in[0:EP, :, :], edge_attr.rearrange("(p c) k -> p c k", c=EC)).then_inc(s_in, 16)
            for m in range(2 * HOPS + 1):
                if m >= 1:
                    sp.wait_ge(s_wT_pe, m)
                mat = W if m == 2 * HOPS else (Wn, Ws)[m % 2][m // 2]
                sp.dma_start(wraw[:, :, :], mat.rearrange("(a p) k -> p a k", p=P)).then_inc(s_w, 16)
            for k in range(HOPS):
                sp.dma_start(bias2[0:1, k, :], bn[k:k + 1, :]).then_inc(s_small, 16)
                sp.dma_start(bias2[1:2, k, :], bs[k:k + 1, :]).then_inc(s_small, 16)
            with nc.allow_non_contiguous_dma(reason="three short columns"):
                sp.dma_start(ew4[0:EF, :], edge_W.rearrange("o k -> k o")).then_inc(s_small, 16)
            sp.dma_start(ew4[EF:EF + 1, :], edge_b.rearrange("(a o) -> a o", a=1)).then_inc(s_small, 16)
            for t, v in ((asrc_b, a_src.rearrange("(a h) d -> a (h d)", a=1)),
                         (adst_b, a_dst.rearrange("(a h) d -> a (h d)", a=1)),
                         (bias_b, bias.rearrange("(a o) -> a o", a=1))):
                sp.dma_start(t[:, :], v.broadcast_to([P, D])).then_inc(s_small, 16)
            sp.wait_ge(s_fill, 1)
            for r in rows_dram:
                sp.dma_start(r.rearrange("(p c) k -> p (c k)", p=P), zero_tile).then_inc(s_fill, 16)

            for q in s_scat:
                sp.wait_ge(q, 16 * EC)
            sp.wait_ge(s_tab, 2 * EC + 2)
            for k in range(2):
                sp.dma_start(recs[k][:, 0:NC, :], rows_dram[k].rearrange("(p c) k -> p c k", p=P)).then_inc(s_back, 16)
            sp.wait_ge(s_x0z, 2)
            for t in (x0, hcur):
                sp.dma_start(t[:, 0:FULLW, 0:D], x[0:FULLW * P, :].rearrange("(w p) d -> p w d", p=P)).then_inc(s_x, 16)
                sp.dma_start(t[0:N - FULLW * P, FULLW, 0:D], x[FULLW * P:N, :]).then_inc(s_x, 16)
            for k in range(HOPS - 1):
                sp.wait_ge(s_new, NW * (k + 1))
                sp.dma_start(nodes(h_dram[k]), hcur[:, :, :]).then_inc(s_hst, 16)
            sp.wait_ge(s_new, NW * (HOPS + 1))
            sp.dma_start(nodes(hh_dram), x0[:, :, 0:D]).then_inc(s_hst, 16)
            sp.wait_ge(s_ln, LN_STEPS + 2)
            sp.dma_start(nodes(ss_dram), s_src[:, :, :]).then_inc(s_hst, 16)
            sp.wait_ge(s_al, AL_ENDS)
            sp.dma_start(edge_dram, ends[:, :, :].rearrange("p b k -> p (b k)")).then_inc(s_end, 16)
            sp.wait_ge(s_end, 16)
            sp.dma_start(eh[:, :, :, :].rearrange("h c b k -> h c (b k)"),
                         edge_dram.rearrange("(c h) k -> h c k", h=HEADS)).then_inc(s_end, 16)
            sp.wait_ge(s_al, AL_CARRY)
            sp.dma_start(carry_dram, eo[:, :, :, :].rearrange("h c b k -> h (c b k)")).then_inc(s_end, 16)
            sp.wait_ge(s_end, 48)
            for c in range(16):
                sp.dma_start(cin[c * HEADS:(c + 1) * HEADS, :, :].rearrange("p b k -> p (b k)"),
                             carry_dram[:, c * NB * 2:(c + 1) * NB * 2]).then_inc(s_end, 16)
            sp.wait_ge(s_ln, 2 * LN_STEPS + 6)
            sp.dma_start(out[0:FULLW * P, :].rearrange("(w p) d -> p w d", p=P), hcur[:, 0:FULLW, :]).then_inc(s_out, 16)
            sp.dma_start(out[FULLW * P:N, :], hcur[0:N - FULLW * P, FULLW, :]).then_inc(s_out, 16)
            sp.wait_ge(s_out, 32)


        @block.gpsimd
        def _(pool):
            pool.memset(identf[:, :], 0.0).then_inc(s_lane, 1)
            pool.memset(ones[:, :], 1.0).then_inc(s_lane, 1)
            pool.iota(iota_i[:, :], [[1, NC]], base=0, channel_multiplier=0).then_inc(s_lane, 1)
            pool.iota(lane_i[:, :], [[1, 1]], base=0, channel_multiplier=1).then_inc(s_lane, 1)
            pool.wait_ge(s_lane, 4)
            pool.affine_select(out=identf[:, :], in_=identf[:, :], compare_op=ALU.not_equal, fill=1.0, base=0,
                               pattern=[[-1, P]], channel_multiplier=1).then_inc(s_lane, 1)
            pool.affine_select(out=tri[:, :], in_=ones[:, :], compare_op=ALU.is_gt, fill=0.0, base=0,
                               pattern=[[-1, P]], channel_multiplier=1).then_inc(s_lane, 1)
            pool.affine_select(out=triu[:, :], in_=ones[:, :], compare_op=ALU.is_gt, fill=0.0, base=0,
                               pattern=[[1, P]], channel_multiplier=-1).then_inc(s_lane, 1)
            pool.wait_ge(s_fill, 1 + 32)
            pool.wait_ge(s_rec, 6)
            for k in range(2):
                with pool.Fori(0, groups // 2) as t:
                    for h in range(2):
                        g = 2 * t + h
                        pool.wait_ge(s_leave, g + groups * k + 1)
                        pool.wait_ge(s_pos, g + groups * k + 1)
                        pool.nop(nofuse=True)
                        for j in range(U):
                            pool.indirect_dma_start(
                                out=rows_dram[k],
                                in_=leaving[0:EP, h, j, :],
                                out_offset=bass.IndirectOffsetOnAxis(ap=place[0:EP, h, j:j + 1], axis=0),
                                in_offset=None).then_inc(s_scat[h], 16)

            def gather(p, t, table, ring, first):
                for j in range(U):
                    if ring is not None and not first:
                        pool.wait_ge(s_mm, ring * NC + (t - 1) * U + j + 1)
                        pool.nop(nofuse=True)
                    if j % 4 == 0:
                        pool.wait_ge(s_idx, p * (2 * NC // U + 2) + 2 * t + j // 4 + 1)
                        pool.nop(nofuse=True)
                    o = gath[:, j, :] if ring is not None else gath[:, j, 0:HEADS]
                    pool.indirect_dma_start(
                        out=o, out_offset=None, in_=table,
                        in_offset=bass.IndirectOffsetOnAxis(ap=idx[:, j:j + 1], axis=0)).then_inc(s_g[j], 16)

            for k in range(HOPS):
                if k >= 1:
                    pool.wait_ge(s_hst, 16 * k)
                gather(k, 0, x if k == 0 else h_dram[k - 1], k, k == 0)
                with pool.Fori(1, NC // U) as t:
                    gather(k, t, x if k == 0 else h_dram[k - 1], k, False)
            pool.wait_ge(s_hst, 16 * (HOPS + 1))
            pool.nop(nofuse=True)
            with pool.Fori(0, NC // U) as t:
                gather(HOPS, t, ss_dram, None, False)
            gather(HOPS + 1, 0, hh_dram, HOPS, False)
            with pool.Fori(1, NC // U) as t:
                gather(HOPS + 1, t, hh_dram, HOPS, False)

        @block.tensor
        def _(pe):
            pe.wait_ge(s_const, 4)
            for m in range(2 * HOPS + 1):
                pe.wait_ge(s_w, 16 * (m + 1))
                if m >= 2:
                    pe.wait_ge(s_wT, m - 1)
                for a in range(2):
                    for b in range(2):
                        i = pe.transpose(bank[m % 2][:, b * D + a * P:b * D + (a + 1) * P],
                                         wraw[:, a, b * P:(b + 1) * P], identf[:, :])
                i.then_inc(s_wT_pe, 1)

            for k in range(2):
                def count(t, start, stop):
                    for j in range(U):
                        c = t * U + j
                        if j == 0:
                            pe.wait_ge(s_oh, k * (groups + 1) + t + 2)
                        i = pe.matmul(bank[0][0:HI, 0:P], ohhi[0:EP, bass.ds(c, 1), :].rearrange("p c k -> p (c k)"),
                                      ohlo[0:EP, bass.ds(c, 1), :].rearrange("p c k -> p (c k)"),
                                      start=start and j == 0, stop=stop and j == U - 1, skip_group_check=True)
                    return i
                pe.wait_ge(s_wT, 2 * HOPS + 1)
                count(0, True, False)
                with pe.Fori(1, groups - 1) as t:
                    count(t, False, False)
                count(groups - 1, False, True).then_inc(s_hist, 1)
                pe.wait_ge(s_hd, 10 * k + 4)
                pe.matmul(bank[1][0:HI, 0:1], triu[0:HI, 0:HI], small[:, 2:3], start=True, stop=True).then_inc(s_cum, 1)
                pe.wait_ge(s_hd, 10 * k + 9)
                pe.matmul(bank[1][0:1, 0:NC], ones[0:USED, 0:1], started[0:USED, :], start=True,
                          stop=True).then_inc(s_win, 1)
                if k:
                    pe.wait_ge(s_tab, EC + 1)
                pe.matmul(bank[2][0:HI, 0:P], identf[0:HI, 0:HI], table0[:, :], start=True, stop=False,
                          skip_group_check=True).then_inc(s_seed, 1)

                def rank_step(t, first):
                    q0 = (2 * (groups * k + t))
                    for s in range(2):
                        h = bank[3 + s][0:HI, :]
                        r = bank[5 + s]
                        if not first:
                            pe.wait_ge(s_hiTs, q0 + s - 1)
                            pe.wait_ge(s_rank, q0 + s - 1)
                        for j in range(4):
                            c = t * U + 4 * s + j
                            pe.matmul(h[:, j * EP:(j + 1) * EP],
                                      ohhi[0:EP, bass.ds(c, 1), :].rearrange("p c k -> p (c k)"),
                                      identb[0:EP, 0:EP], start=True, stop=True, skip_group_check=True)
                        pe.wait_ge(s_kst, k * (2 * groups + 2) + 2 * t + s + 1)
                        for j in range(4):
                            i = pe.transpose(r[0:EP, j * EP:(j + 1) * EP],
                                             kst[0:EP, 4 * s + j:4 * s + j + 1].broadcast_to([EP, EP]),
                                             identf[0:EP, 0:EP])
                        i.then_inc(s_row, 1)
                    for j in range(U):
                        c = t * U + j
                        n = EC * k + c
                        if j % 4 == 0:
                            pe.wait_ge(s_hiTs, q0 + j // 4 + 1)
                        pe.wait_ge(s_tab, n + k + 1)
                        if not first and j % 4 == 0:
                            pe.wait_ge(s_rank, q0 + j // 4 - 1)
                        pe.matmul(bank[7 * (j // 4)][0:EP, (j % 4) * P:(j % 4 + 1) * P], ohhiT[:, j, :],
                                  table[:, j % 2, :], start=True, stop=True, skip_group_check=True).then_inc(s_look, 1)
                        pe.matmul(bank[2][0:HI, 0:P], ohhi[0:EP, bass.ds(c, 1), :].rearrange("p c k -> p (c k)"),
                                  ohlo[0:EP, bass.ds(c, 1), :].rearrange("p c k -> p (c k)"),
                                  start=False, stop=False, skip_group_check=True).then_inc(s_upd, 1)
                rank_step(0, k == 0)
                with pe.Fori(1, groups) as t:
                    rank_step(t, False)
            pe.wait_ge(s_rank, 4 * groups)

            def sum_chunks(k, t, first):
                for j in range(U):
                    n = k * NC + t * U + j
                    pe.wait_ge(s_g[j], 16 * (turn(k) * (NC // U) + t + 1))
                    pe.wait_ge(s_oneh, n + 1)
                    if not (first and j < 4):
                        pe.wait_ge(s_add, n - 3)
                    pe.matmul(bank[j % 4][:, 0:D], onehot[:, j % 4, :], gath[:, j, :], start=True,
                              stop=True).then_inc(s_mm, 1)

            def dense(k, t, first):
                parts = 4 if k < HOPS else 2
                for s in range(2):
                    n = k * NW + 2 * t + s
                    pe.wait_ge(s_stg, n + 1)
                    if not first:
                        pe.wait_ge(s_stTs, n - 1)
                    for q in range(parts):
                        i = pe.transpose(bank[4 + s][:, q * P:(q + 1) * P], stg[:, s, q * P:(q + 1) * P], identf[:, :])
                    i.then_inc(s_stT, 1)
                for s in range(2):
                    n = k * NW + 2 * t + s
                    pe.wait_ge(s_stTs, n + 1)
                    if not first:
                        pe.wait_ge(s_new, n - 1)
                    for q in range(parts):
                        i = pe.matmul(bank[6 + s][:, 0:D], stgT[:, s, q * P:(q + 1) * P],
                                      wT[:, 2 * k + q // 2, q % 2, :], start=q == 0, stop=k == HOPS and q == parts - 1)
                    if k < HOPS:
                        i = pe.matmul(bank[6 + s][:, 0:D], ones[0:2, :], bias2[:, k, :], start=False, stop=True)
                    i.then_inc(s_lin, 1)

            pe.wait_ge(s_small, 16 * (2 * HOPS + 5))
            for k in range(HOPS):
                sum_chunks(k, 0, k == 0)
                with pe.Fori(1, NC // U) as t:
                    sum_chunks(k, t, False)
                dense(k, 0, k == 0)
                with pe.Fori(1, NW // 2) as t:
                    dense(k, t, False)
            dense(HOPS, 0, False)
            with pe.Fori(1, NW // 2) as t:
                dense(HOPS, t, False)

            def score(t, first):
                for s in range(2):
                    g = 2 * t + s
                    pe.wait_ge(s_fst, g + 1)
                    if not first:
                        pe.wait_ge(s_eaTs, g - 1)
                    for j in range(4):
                        i = pe.transpose(bank[s][0:4, j * P:(j + 1) * P], fst[:, 4 * s + j, 3:7], identf[:, :])
                    i.then_inc(s_eaT, 1)
                for j in range(U):
                    n = t * U + j
                    if not (first and j < 2):
                        pe.wait_ge(s_oneh, HOPS * NC + n - 1)
                    pe.transpose(bank[2 + j % 2][:, 0:P], fst[:, j, 7:8].broadcast_to([P, P]),
                                 identf[:, :]).then_inc(s_lrow, 1)
                    if j % 4 == 0:
                        pe.wait_ge(s_eaTs, 2 * t + j // 4 + 1)
                    if not (first and j < 2):
                        pe.wait_ge(s_relu, n - 1)
                    pe.matmul(bank[4 + j % 2][:, 0:D], eaT[:, j // 4, (j % 4) * P:(j % 4 + 1) * P], ew4[:, :],
                              start=True, stop=True).then_inc(s_enc, 1)
                    pe.wait_ge(s_oneh, HOPS * NC + n + 1)
                    if not (first and j < 2):
                        pe.wait_ge(s_dot, n - 1)
                        pe.wait_ge(s_sde, n - 1)
                    w = pe.value_load(win[1][0:1, bass.ds(n, 1)], min_val=0, max_val=NW - 1)
                    pe.matmul(bank[6 + j % 2][:, 0:HX], onehot[:, j % 4, :],
                              x0[:, bass.ds(w, 1), :].rearrange("p c k -> p (c k)"), start=True, stop=True
                              ).then_inc(s_hd_, 1)
            pe.wait_ge(s_ln, LN_STEPS + 4)
            score(0, True)
            with pe.Fori(1, NC // U) as t:
                score(t, False)

            pe.wait_ge(s_al, 4)
            for i in range(2 * NB):
                if i >= 2:
                    pe.wait_ge(s_alTs, i - 1)
                a = (s_sb if i < NB else sde)[:, 16 * (i % NB):16 * (i % NB) + 16, :].rearrange("p c h -> p (c h)")
                pe.transpose(bank[i % 2][:, 0:P], a, identf[:, :]).then_inc(s_alT, 1)
            pe.wait_ge(s_ex, NB)
            for i in range(NB):
                if i >= 2:
                    pe.wait_ge(s_exs, i - 1)
                pe.transpose(bank[2 + i % 2][:, 0:P], alT[:, i, :], identf[:, :]).then_inc(s_exT, 1)

            def attend(t):
                for j in range(U):
                    n = HOPS * NC + t * U + j
                    pe.wait_ge(s_val, t * U + j + 1)
                    pe.wait_ge(s_vx, t * U + j + 1)
                    pe.wait_ge(s_oneh, NC + n + 1)
                    pe.wait_ge(s_add, n - 3)
                    pe.matmul(bank[4 + j % 4][:, 0:HX], onehot[:, j % 4, :], val[:, j % 4, :], start=True,
                              stop=True).then_inc(s_mm, 1)
            with pe.Fori(0, NC // U) as t:
                attend(t)

        @block.scalar
        def _(act):
            for m in range(2 * HOPS + 1):
                act.wait_ge(s_wT_pe, m + 1)
                nc.scalar.copy(wT[:, m, :, :].rearrange("p a o -> p (a o)"), bank[m % 2][:, :]).then_inc(s_wT, 1)
            for k in range(2):
                act.wait_ge(s_seed, k + 1)
                nc.scalar.copy(table[:, 0, :], bank[2][0:HI, 0:P]).then_inc(s_tab, 1)

                def stage(c, j):
                    nc.scalar.copy(kst[0:EP, j:j + 4], key_f[0:EP, bass.ds(c, 4)]).then_inc(s_kst, 1)

                stage(0, 0)
                stage(4, 4)

                def step(t):
                    for j in range(U):
                        n = EC * k + t * U + j
                        if j % 4 == 0:
                            g = 2 * (groups * k + t) + j // 4
                            act.wait_ge(s_row, g + 1)
                            if k > 0 or not isinstance(t, int):
                                act.wait_ge(s_look, n - 4)
                            nc.scalar.copy(ohhiT[:, j:j + 4, :],
                                           bank[3 + j // 4][0:HI, 0:4 * EP].rearrange("p (a e) -> p a e", a=4)).then_inc(s_hiTs, 1)
                        if j % 4 == 2:
                            act.wait_ge(s_eq, 5 * (2 * (groups * k + t) + j // 4) + 4)
                            act.nop(nofuse=True)
                            stage((t + 1) * U + j - 2, j - 2)
                        act.wait_ge(s_upd, n + 1)
                        nc.scalar.copy(table[:, (j + 1) % 2, :], bank[2][0:HI, 0:P]).then_inc(s_tab, 1)
                step(0)
                with act.Fori(1, groups) as t:
                    step(t)

            def dense(k, t):
                parts = 4 if k < HOPS else 2
                for s in range(2):
                    n = k * NW + 2 * t + s
                    act.wait_ge(s_stT, n + 1)
                    nc.scalar.copy(stgT[:, s, 0:parts * P], bank[4 + s][:, 0:parts * P]).then_inc(s_stTs, 1)
                if k < HOPS - 1:
                    for s in range(2):
                        n = k * NW + 2 * t + s
                        act.wait_ge(s_em, n + 1)
                        nc.scalar.activation(elu[:, s, 0:D], bank[6 + s][:, 0:D], ACT.Relu).then_inc(s_ea, 1)
                        nc.scalar.activation(elu[:, s, D:2 * D], elu[:, s, D:2 * D], ACT.Exp).then_inc(s_ea, 1)
            def stage_idx(p, t, h, first=False):
                if not (first and p == 0):
                    for j in range(4 * h, 4 * h + 4):
                        act.wait_ge(s_g[j], 16 * (p * (NC // U) + t))
                    act.nop(nofuse=True)
                if p == HOPS and not first:
                    nc.scalar.copy(s_sb[:, bass.ds((t - 1) * U + 4 * h, 4), :],
                                   gath[:, 4 * h:4 * h + 4, 0:HEADS]).then_inc(s_ss, 1)
                r, col = (recs[0], 1) if p < HOPS else (recs[1], 0)
                nc.scalar.copy(idx[:, 4 * h:4 * h + 4],
                               r[:, bass.ds(t * U + 4 * h, 4), col].bitcast(I32)).then_inc(s_idx, 1)

            act.wait_ge(s_back, 32)
            act.wait_ge(s_lo7, 2)
            for k in range(HOPS + 1):
                if k < HOPS:
                    stage_idx(k, 0, 0, True)
                    stage_idx(k, 0, 1, True)
                    with act.Fori(0, NC // U) as t:
                        stage_idx(k, t + 1, 0)
                        stage_idx(k, t + 1, 1)
                with act.Fori(0, NW // 2) as t:
                    dense(k, t)
                if k == HOPS - 1:
                    act.wait_ge(s_ln, 4)
                    nc.scalar.activation(stat[:, :, 2], stat[:, :, 1], ACT.Sqrt).then_inc(s_sq, 1)

            act.wait_ge(s_lo7, 3)

            def stage_recs(c, j):
                nc.scalar.copy(fst[:, j:j + 4, :], recs[1][:, bass.ds(c, 4), :]).then_inc(s_fst, 1)

            stage_recs(0, 0)
            stage_recs(4, 4)
            stage_idx(HOPS, 0, 0, True)
            stage_idx(HOPS, 0, 1, True)

            def score(t):
                for j in range(U):
                    n = t * U + j
                    if j % 4 == 0:
                        act.wait_ge(s_eaT, 2 * t + j // 4 + 1)
                        nc.scalar.copy(eaT[:, j // 4, :], bank[j // 4][0:4, :]).then_inc(s_eaTs, 1)
                    if j % 4 == 3:
                        act.wait_ge(s_lrow, n + 1)
                        act.nop(nofuse=True)
                        stage_recs((t + 1) * U + j - 3, j - 3)
                        stage_idx(HOPS, t + 1, j // 4)
                    act.wait_ge(s_enc, n + 1)
                    if not (isinstance(t, int) and j < 2):
                        act.wait_ge(s_dot, n - 1)
                    nc.scalar.activation(encr[:, j % 2, :], bank[4 + j % 2][:, 0:D], ACT.Relu).then_inc(s_relu, 1)
                    act.wait_ge(s_hd_, n + 1)
                    act.nop(nofuse=True)
                    nc.scalar.copy(sde[:, bass.ds(n, 1), :].rearrange("p c h -> p (c h)"),
                                   bank[6 + j % 2][:, D:HX]).then_inc(s_sde, 1)
            score(0)
            with act.Fori(1, NC // U) as t:
                score(t)
            for i in range(2 * NB):
                act.wait_ge(s_alT, i + 1)
                nc.scalar.copy((alT if i < NB else dotT)[:, i % NB, :], bank[i % 2][:, 0:P]).then_inc(s_alTs, 1)
            for b in range(NB):
                act.wait_ge(s_mx, b + 1)
                nc.scalar.activation(alT[:, b, :], alT[:, b, :], ACT.Exp).then_inc(s_ex, 1)
            for i in range(NB):
                act.wait_ge(s_exT, i + 1)
                nc.scalar.copy(s_sb[:, 16 * i:16 * i + 16, :].rearrange("p c h -> p (c h)"),
                               bank[2 + i % 2][:, 0:P]).then_inc(s_exs, 1)
            act.wait_ge(s_exs, NB)

            def attend(t):
                for j in range(U):
                    n = t * U + j
                    act.wait_ge(s_mm, HOPS * NC + n - 3)
                    act.nop(nofuse=True)
                    nc.scalar.copy(val[:, j % 4, D:HX], s_sb[:, bass.ds(n, 1), :].rearrange("p c h -> p (c h)")
                                   ).then_inc(s_vx, 1)
                    if j % 4 == 3:
                        stage_idx(HOPS + 1, t + 1, j // 4)
            stage_idx(HOPS + 1, 0, 0)
            stage_idx(HOPS + 1, 0, 1)
            attend(0)
            with act.Fori(1, NC // U) as t:
                attend(t)
            act.wait_ge(s_ln, LN_STEPS + 4 + 2 + 4)
            nc.scalar.activation(stat[:, :, 2], stat[:, :, 1], ACT.Sqrt).then_inc(s_sq, 1)


        @block.vector
        def _(dve):
            v = nc.vector
            v.memset(zero_tile, 0.0).then_inc(s_fill, 1)
            dve.wait_ge(s_lane, 7)
            v.tensor_copy(iota_f[:, :], iota_i[:, :]).then_inc(s_const, 1)
            v.tensor_copy(iota_b[:, :], iota_i[:, 0:P]).then_inc(s_const, 1)
            v.tensor_copy(lane_f[:, :], lane_i[:, :]).then_inc(s_const, 1)
            v.tensor_copy(identb[:, :], identf[:, :]).then_inc(s_const, 1)
            v.memset(key_f[0:EP, EC:EC + U], 0.0).then_inc(s_const, 1)
            dve.wait_ge(s_in, 64)
            rec_i = rec[:, :, :].bitcast(I32)
            v.tensor_copy(rec_i[0:EP, :, 0], src_i[0:EP, :]).then_inc(s_rec, 1)
            v.tensor_copy(rec_i[0:EP, :, 1], dst_i[0:EP, :]).then_inc(s_rec, 1)
            v.tensor_copy(rec[0:EP, :, 2], w_in[0:EP, :]).then_inc(s_rec, 1)
            v.tensor_copy(rec[0:EP, :, 3:6], ea_in[0:EP, :, :]).then_inc(s_rec, 1)
            v.memset(rec[0:EP, :, 6], 1.0).then_inc(s_rec, 1)
            v.memset(rec[0:EP, :, 7], 0.0).then_inc(s_rec, 1)

            dve.wait_ge(s_fill, 33)
            for k in range(2):
                key = (src_i, dst_i)[k]
                if k:
                    dve.wait_ge(s_upd, EC)
                    dve.wait_ge(s_row, 2 * groups)
                v.tensor_copy(key_f[0:EP, 0:EC], key[0:EP, :]).then_inc(s_keys, 1)
                v.tensor_scalar(lo_i[0:EP, :], key[0:EP, :], P - 1, None, ALU.bitwise_and).then_inc(s_keys, 1)
                dve.wait_ge(s_keys, 5 * k + 2)
                v.tensor_copy(lo_f[0:EP, :], lo_i[0:EP, :]).then_inc(s_keys, 1)
                dve.wait_ge(s_keys, 5 * k + 3)
                v.tensor_scalar(lo_i[0:EP, :], key[0:EP, :], SHIFT, None, ALU.logical_shift_right).then_inc(s_keys, 1)
                dve.wait_ge(s_keys, 5 * k + 4)
                v.tensor_copy(hi_f[0:EP, :], lo_i[0:EP, :]).then_inc(s_keys, 1)
                dve.wait_ge(s_keys, 5 * k + 5)
                v.tensor_tensor(ohhi[0:EP, :, :], hi_f[0:EP, :].unsqueeze(2).broadcast_to([EP, EC, HI]),
                                iota_f[0:EP, 0:HI].unsqueeze(1).broadcast_to([EP, EC, HI]),
                                ALU.is_equal).then_inc(s_oh, 1)
                with dve.Fori(0, groups) as t:
                    for j in range(U):
                        c = t * U + j
                        i = v.tensor_scalar(ohlo[0:EP, bass.ds(c, 1), :].rearrange("p c k -> p (c k)"),
                                            iota_b[0:EP, :], lo_f[0:EP, bass.ds(c, 1)], None, ALU.is_equal)
                    i.then_inc(s_oh, 1)
                q = 10 * k
                dve.wait_ge(s_hist, k + 1)
                v.tensor_copy(hist[:, :], bank[0][0:HI, 0:P]).then_inc(s_hd, 1)
                dve.wait_ge(s_hd, q + 1)
                v.tensor_reduce(small[:, 0:1], hist[:, :], X, ALU.add).then_inc(s_hd, 1)
                dve.wait_ge(s_hd, q + 2)
                v.tensor_scalar(small_i[:, 0:1], small[:, 0:1], float(P - 1), None, ALU.add).then_inc(s_hd, 1)
                dve.wait_ge(s_hd, q + 3)
                v.tensor_scalar(small_i[:, 1:2], small_i[:, 0:1], SHIFT, None,
                                ALU.logical_shift_right).then_inc(s_base, 1)
                dve.wait_ge(s_base, 2 * k + 1)
                v.tensor_copy(small[:, 2:3], small_i[:, 1:2]).then_inc(s_hd, 1)
                dve.wait_ge(s_cum, k + 1)
                v.tensor_copy(small[:, 3:4], bank[1][0:HI, 0:1]).then_inc(s_hd, 1)
                dve.wait_ge(s_hd, q + 5)
                v.tensor_scalar(small[:, 4:5], small[:, 3:4], float(P), None, ALU.mult).then_inc(s_hd, 1)
                dve.wait_ge(s_hd, q + 6)
                v.tensor_tensor_scan(table0[:, :], ones[0:HI, :], hist[:, :], small[:, 4:5], ALU.mult,
                                     ALU.add).then_inc(s_hd, 1)
                dve.wait_ge(s_hd, q + 7)
                v.tensor_tensor(table0[:, :], table0[:, :], hist[:, :], ALU.subtract).then_inc(s_hd, 1)
                v.tensor_scalar(started[:, :], iota_f[0:HI, :], small[:, 3:4], None, ALU.is_ge).then_inc(s_hd, 1)
                dve.wait_ge(s_win, k + 1)
                v.tensor_scalar(win[k][:, :], bank[1][0:1, 0:NC], -1.0, None, ALU.add).then_inc(s_base, 1)
                dve.wait_ge(s_base, 2 * k + 2)
                v.tensor_copy(small[0:1, 5:6], small[0:1, 3:4]).then_inc(s_hd, 1)

                def ranks(pair, h, first):
                    t = 2 * pair + h
                    g = groups * k + t
                    for q in range(2):
                        tm = terms[0:EP, q, :, :]
                        dve.wait_ge(s_row, 2 * g + q + 1)
                        for j in range(4):
                            v.scalar_tensor_tensor(out=tm[:, j, 0:EP], in0=bank[5 + q][0:EP, j * EP:(j + 1) * EP],
                                                   scalar=kst[0:EP, 4 * q + j:4 * q + j + 1], in1=tri[0:EP, 0:EP],
                                                   op0=ALU.is_equal, op1=ALU.mult).then_inc(s_eq, 1)
                        dve.wait_ge(s_look, EC * k + t * U + 4 * q + 4)
                        v.tensor_tensor(tm[:, :, EP:EP + P],
                                        bank[7 * q][0:EP, :].rearrange("p (c n) -> p c n", c=4),
                                        ohlo[0:EP, bass.ds(t * U + 4 * q, 4), :], ALU.mult).then_inc(s_eq, 1)
                        dve.wait_ge(s_eq, 5 * (2 * g + q + 1))
                        v.tensor_reduce(rank[0:EP, 4 * q:4 * q + 4], tm[:, :, 0:EP + P], X,
                                        ALU.add).then_inc(s_rank, 1)
                    dve.wait_ge(s_rank, 2 * g + 2)
                    v.tensor_copy(pos_i[0:EP, 0, :], rank[0:EP, :]).then_inc(s_d, 1)
                    dve.wait_ge(s_d, 3 * g + 1)
                    v.tensor_scalar(pos_i[0:EP, 1, :], pos_i[0:EP, 0, :], P - 1, None,
                                    ALU.bitwise_and).then_inc(s_d, 1)
                    v.tensor_scalar(pos_i[0:EP, 2, :], pos_i[0:EP, 0, :], SHIFT, None,
                                    ALU.logical_shift_right).then_inc(s_d, 1)
                    dve.wait_ge(s_d, 3 * g + 3)
                    if not first:
                        dve.wait_ge(s_scat[h], 16 * U * (groups // 2 * k + pair))
                    v.tensor_copy(leaving[0:EP, h, :, :], rec[0:EP, bass.ds(t * U, U), :]).then_inc(s_leave, 1)
                    v.scalar_tensor_tensor(out=place[0:EP, h, :], in0=pos_i[0:EP, 1, :], scalar=float(NC),
                                           in1=pos_i[0:EP, 2, :], op0=ALU.mult, op1=ALU.add).then_inc(s_pos, 1)
                ranks(0, 0, k == 0)
                ranks(0, 1, k == 0)
                with dve.Fori(1, groups // 2) as t:
                    ranks(t, 0, False)
                    ranks(t, 1, False)

            def los(k):
                dve.wait_ge(s_back, 32)
                ri = recs[k][:, 0:NC, :].bitcast(I32)
                q = 4 * k
                v.tensor_scalar(lo_si[:, :], ri[:, :, k], P - 1, None, ALU.bitwise_and).then_inc(s_lo, 1)
                dve.wait_ge(s_lo, q + 1)
                v.tensor_copy(lo_s[:, :], lo_si[:, :]).then_inc(s_lo, 1)
                dve.wait_ge(s_lo, q + 2)
                v.scalar_tensor_tensor(out=lo_s[:, :], in0=lo_s[:, :], scalar=1.0, in1=recs[k][:, 0:NC, 6],
                                       op0=ALU.add, op1=ALU.mult).then_inc(s_lo, 1)
                dve.wait_ge(s_lo, q + 3)
                v.tensor_scalar(lo_s[:, :], lo_s[:, :], -1.0, None, ALU.add).then_inc(s_lo, 1)
                dve.wait_ge(s_lo, q + 4)

            for q in s_scat:
                dve.wait_ge(q, 16 * EC)
            dve.wait_ge(s_tab, 2 * EC + 2)
            for k in range(2):
                v.memset(recs[k][:, NC:NC + U, :], 0.0).then_inc(s_lo7, 1)
            v.memset(x0[:, FULLW:NW, :], 0.0).then_inc(s_x0z, 1)
            v.memset(hcur[:, FULLW:NW, :], 0.0).then_inc(s_x0z, 1)
            los(0)

            def sum_chunks(k, t):
                for j in range(U):
                    n = k * NC + t * U + j
                    c = t * U + j
                    cold = isinstance(t, int) and k == 0
                    m = n if k < HOPS else n + NC
                    if not (cold and j < 4):
                        dve.wait_ge(s_mm, n - 3)
                    if k < HOPS:
                        v.tensor_scalar(onehot[:, j % 4, :], iota_f[:, 0:P], lo_s[:, bass.ds(c, 1)],
                                        recs[0][:, bass.ds(c, 1), 2], ALU.is_equal, ALU.mult).then_inc(s_oneh, 1)
                    else:
                        v.tensor_scalar(onehot[:, j % 4, :], iota_f[:, 0:P], lo_s[:, bass.ds(c, 1)], None,
                                        ALU.is_equal).then_inc(s_oneh, 1)
                        dve.wait_ge(s_g[j], 16 * (turn(k) * (NC // U) + t + 1))
                        v.tensor_tensor(val[:, j % 4, 0:D].rearrange("p (h d) -> p h d", h=HEADS),
                                        gath[:, j, :].rearrange("p (h d) -> p h d", h=HEADS),
                                        s_sb[:, bass.ds(c, 1), :].rearrange("p c h -> p (c h)").unsqueeze(2)
                                        .broadcast_to([P, HEADS, HD]), ALU.mult).then_inc(s_val, 1)
                    if not (isinstance(t, int) and j < 2):
                        add(k, n - 2, (j - 2) % U)

            def add(k, n, j):
                wide = D if k < HOPS else HX
                b = bank[j % 4] if k < HOPS else bank[4 + j % 4]
                dve.wait_ge(s_mm, n + 1)
                dve.wait_ge(s_add, n) if not (isinstance(n, int) and n == 0) else None
                w = dve.value_load(win[0 if k < HOPS else 1][0:1, bass.ds(n - k * NC, 1)], min_val=0, max_val=NW - 1)
                a = acc[:, bass.ds(w, 1), 0:wide].rearrange("p c d -> p (c d)")
                v.tensor_tensor(a, a, b[:, 0:wide], ALU.add).then_inc(s_add, 1)

            def dense(k, t, first):
                parts = 2 if k < HOPS else 1
                for s in range(2):
                    w = 2 * t + s
                    n = k * NW + w
                    if not first:
                        dve.wait_ge(s_stT, n - 1)
                    if k < HOPS:
                        v.tensor_copy(stg[:, s, 0:D], acc[:, bass.ds(w, 1), 0:D].rearrange("p c d -> p (c d)")
                                      ).then_inc(s_d, 1)
                        v.tensor_copy(stg[:, s, D:2 * D], hcur[:, bass.ds(w, 1), :].rearrange("p c d -> p (c d)")
                                      ).then_inc(s_stg, 1)
                    else:
                        v.tensor_copy(stg[:, s, 0:D], hcur[:, bass.ds(w, 1), :].rearrange("p c d -> p (c d)")
                                      ).then_inc(s_stg, 1)
                for s in range(2):
                    w = 2 * t + s
                    n = k * NW + w
                    h = hcur[:, bass.ds(w, 1), :].rearrange("p c d -> p (c d)")
                    y = bank[6 + s][:, 0:D]
                    xw = x0[:, bass.ds(w, 1), 0:D].rearrange("p c d -> p (c d)")
                    dve.wait_ge(s_lin, n + 1)
                    if k < HOPS - 1:
                        if not first:
                            dve.wait_ge(s_new, n - 1)
                        v.tensor_scalar(elu[:, s, D:2 * D], y, 0.0, None, ALU.min).then_inc(s_em, 1)
                    elif k == HOPS - 1:
                        v.tensor_tensor(h, xw, y, ALU.add).then_inc(s_new, 1)
                    else:
                        v.tensor_copy(xw, y).then_inc(s_new, 1)
                if k < HOPS - 1:
                    for s in range(2):
                        w = 2 * t + s
                        n = k * NW + w
                        dve.wait_ge(s_ea, 2 * n + 2)
                        v.scalar_tensor_tensor(out=hcur[:, bass.ds(w, 1), :].rearrange("p c d -> p (c d)"),
                                               in0=elu[:, s, D:2 * D], scalar=-1.0, in1=elu[:, s, 0:D],
                                               op0=ALU.add, op1=ALU.add).then_inc(s_new, 1)

            def layer_norm(q, r):
                sq = acc[:, :, 0:D]
                mean, var, root, inv = (stat[:, :, i] for i in range(4))
                v.tensor_reduce(mean, hcur[:, :, :], X, ALU.add).then_inc(s_ln, 1)
                dve.wait_ge(s_ln, q + 1)
                v.tensor_scalar(mean, mean, 1.0 / D, None, ALU.mult).then_inc(s_ln, 1)
                dve.wait_ge(s_ln, q + 2)
                mb = mean.unsqueeze(2).broadcast_to([P, NW, D])
                v.tensor_tensor(hcur[:, :, :], hcur[:, :, :], mb, ALU.subtract).then_inc(s_d, 1)
                dve.wait_ge(s_d, r + 1)
                v.tensor_tensor(sq, hcur[:, :, :], hcur[:, :, :], ALU.mult).then_inc(s_d, 1)
                dve.wait_ge(s_d, r + 2)
                v.tensor_reduce(var, sq, X, ALU.add).then_inc(s_ln, 1)
                dve.wait_ge(s_ln, q + 3)
                v.tensor_scalar(var, var, 1.0 / D, EPS, ALU.mult, ALU.add).then_inc(s_ln, 1)
                dve.wait_ge(s_sq, 1 if q == 0 else 2)
                v.reciprocal(inv, root).then_inc(s_ln, 1)
                dve.wait_ge(s_ln, q + 5)
                v.tensor_tensor(hcur[:, :, :], hcur[:, :, :], inv.unsqueeze(2).broadcast_to([P, NW, D]),
                                ALU.mult).then_inc(s_ln, 1)
                dve.wait_ge(s_ln, q + 6)

            dve.wait_ge(s_x, 64)
            for k in range(HOPS):
                if k:
                    dve.wait_ge(s_hst, 16 * k)
                v.memset(acc[:, :, :], 0.0).then_inc(s_clr, 1)
                dve.wait_ge(s_clr, k + 1)
                sum_chunks(k, 0)
                with dve.Fori(1, NC // U) as t:
                    sum_chunks(k, t)
                for n in range(2):
                    add(k, k * NC + NC - 2 + n, U - 2 + n)
                dve.wait_ge(s_add, NC * (k + 1))
                dense(k, 0, k == 0)
                with dve.Fori(1, NW // 2) as t:
                    dense(k, t, False)
            dve.wait_ge(s_new, HOPS * NW)
            R = 3 * 2 * groups + HOPS * NW
            layer_norm(0, R)
            R += 2
            dense(HOPS, 0, False)
            with dve.Fori(1, NW // 2) as t:
                dense(HOPS, t, False)
            dve.wait_ge(s_new, (HOPS + 1) * NW)
            h4 = x0[:, :, 0:D]
            pr = acc[:, :, 0:D]
            for i, (a, o) in enumerate(((asrc_b, s_src[:, :, :]), (adst_b, x0[:, :, D:HX]))):
                for w in range(2):
                    half = slice(w * NW // 2, (w + 1) * NW // 2)
                    v.tensor_tensor(pr[:, half, :], h4[:, half, :],
                                    a[:, :].unsqueeze(1).broadcast_to([P, NW // 2, D]), ALU.mult).then_inc(s_d, 1)
                    R += 1
                    dve.wait_ge(s_d, R)
                    for ww in range(w * NW // 2, (w + 1) * NW // 2):
                        ins = v.tensor_reduce(o[:, ww, :], pr[:, ww, :].rearrange("p (h d) -> p h d", h=HEADS),
                                              X, ALU.add)
                    ins.then_inc(s_ln, 1)
                    dve.wait_ge(s_ln, LN_STEPS + 2 * i + w + 1)
            los(1)
            v.tensor_copy(recs[1][:, 0:NC, 7], lo_s[:, :]).then_inc(s_lo7, 1)

            def score(t):
                for j in range(U):
                    n = t * U + j
                    dve.wait_ge(s_lrow, n + 1)
                    cold = isinstance(t, int)
                    if not (cold and j < 4):
                        dve.wait_ge(s_hd_, n - 3)
                    v.tensor_scalar(onehot[:, j % 4, :], bank[2 + j % 2][:, 0:P], lane_f[:, 0:1], None,
                                    ALU.is_equal).then_inc(s_oneh, 1)
                    if not (cold and j < 1):
                        take_dot(n - 1, (j - 1) % U)

            def take_dot(n, j):
                dve.wait_ge(s_relu, n + 1)
                dve.wait_ge(s_sde, n + 1)
                v.tensor_tensor(prod[:, j % 2, :], encr[:, j % 2, :], bank[6 + j % 2][:, 0:D],
                                ALU.mult).then_inc(s_em, 1)
                dve.wait_ge(s_em, (HOPS - 1) * NW + n + 1)
                v.tensor_reduce(dot[:, bass.ds(n, 1), :].rearrange("p c h -> p (c h)"),
                                prod[:, j % 2, :].rearrange("p (h d) -> p h d", h=HEADS), X, ALU.add).then_inc(s_dot, 1)

            score(0)
            with dve.Fori(1, NC // U) as t:
                score(t)
            take_dot(NC - 1, U - 1)

            dve.wait_ge(s_dot, NC)
            dve.wait_ge(s_sde, NC)
            dve.wait_ge(s_ss, 2 * NC // U)
            al, do, sd = (z[:, :, :].rearrange("p c h -> p (c h)") for z in (s_sb, dot, sde))
            v.tensor_tensor(al, al, sd, ALU.add).then_inc(s_al, 1)
            dve.wait_ge(s_al, 1)
            v.tensor_tensor(al, al, do, ALU.add).then_inc(s_al, 1)
            dve.wait_ge(s_al, 2)
            v.scalar_tensor_tensor(out=al, in0=al, scalar=0.2, in1=al, op0=ALU.mult, op1=ALU.max).then_inc(s_al, 1)
            v.tensor_copy(lo_s[:, :], recs[1][:, 0:NC, :].bitcast(I32)[:, :, 1]).then_inc(s_lo, 1)
            dve.wait_ge(s_lo, 9)
            v.scalar_tensor_tensor(out=lo_si[:, :].bitcast(F32), in0=lo_s[:, :], scalar=1.0, in1=recs[1][:, 0:NC, 6],
                                   op0=ALU.add, op1=ALU.mult).then_inc(s_lo, 1)
            dve.wait_ge(s_lo, 10)
            v.tensor_copy(sde[:, :, :], lo_si[:, :].bitcast(F32).unsqueeze(2).broadcast_to([P, NC, HEADS])).then_inc(s_al, 1)

            dve.wait_ge(s_alTs, 2 * NB)
            K = dotT
            v.memset(brk, 0.0).then_inc(s_lo, 1)
            dve.wait_ge(s_lo, 11)
            v.tensor_tensor(brk3[:, :, 1:P], K[:, :, 1:P], K[:, :, 0:P - 1], ALU.not_equal).then_inc(s_lo, 1)
            dve.wait_ge(s_lo, 12)
            v.tensor_scalar(brk, brk, -BIG, None, ALU.mult).then_inc(s_lo, 1)
            dve.wait_ge(s_lo, 13)
            for b in range(NB):
                ins = v.tensor_tensor_scan(sdeT[:, b, :], brk3[:, b, 0:P], alT[:, b, :], -BIG, ALU.add, ALU.max)
            ins.then_inc(s_lo, 1)
            dve.wait_ge(s_lo, 14)
            v.tensor_copy(ends[:, :, 0], sdeT[:, :, P - 1]).then_inc(s_lo, 1)
            v.tensor_copy(ends[:, :, 2], K[:, :, 0]).then_inc(s_lo, 1)
            v.tensor_copy(ends[:, :, 3], K[:, :, P - 1]).then_inc(s_lo, 1)
            dve.wait_ge(s_lo, 17)
            for b in range(NB):
                ins = v.tensor_tensor_scan(dotT[:, b, ::-1], brk3[:, b, 1:P + 1][:, ::-1], sdeT[:, b, ::-1], -BIG,
                                           ALU.add, ALU.max)
            ins.then_inc(s_al, 1)
            dve.wait_ge(s_al, 5)
            v.tensor_copy(ends[:, :, 1], dotT[:, :, 0]).then_inc(s_al, 1)
            dve.wait_ge(s_end, 32)
            for i in range(4):
                ins = v.tensor_copy(el[:, i, :].rearrange("h (b c) -> h c b", c=16), eh[:, :, :, i])
            ins.then_inc(s_al, 1)
            dve.wait_ge(s_al, 7)
            last, firstm, k0, k1, cont, sing, p_, o_ = (el[:, i, :] for i in range(8))
            v.memset(cont, 1.0).then_inc(s_al, 1)
            dve.wait_ge(s_al, 8)
            v.tensor_tensor(cont[:, 1:NC], k0[:, 1:NC], k1[:, 0:NC - 1], ALU.not_equal).then_inc(s_al, 1)
            v.tensor_tensor(sing, k0, k1, ALU.not_equal).then_inc(s_al, 1)
            dve.wait_ge(s_al, 10)
            v.tensor_tensor(p_, cont, sing, ALU.max).then_inc(s_al, 1)
            dve.wait_ge(s_al, 11)
            v.tensor_scalar(p_, p_, -BIG, None, ALU.mult).then_inc(s_al, 1)
            dve.wait_ge(s_al, 12)
            v.tensor_tensor_scan(o_, p_, last, -BIG, ALU.add, ALU.max).then_inc(s_al, 1)
            v.memset(k0, 1.0).then_inc(s_al, 1)
            dve.wait_ge(s_al, 14)
            v.tensor_copy(k0[:, 0:NC - 1], cont[:, 1:NC]).then_inc(s_al, 1)
            dve.wait_ge(s_al, 15)
            v.tensor_tensor(k1, k0, sing, ALU.max).then_inc(s_x0z, 1)
            dve.wait_ge(s_x0z, 3)
            v.tensor_scalar(k1, k1, -BIG, None, ALU.mult).then_inc(s_x0z, 1)
            dve.wait_ge(s_x0z, 4)
            v.tensor_tensor_scan(sing[:, ::-1], k1[:, ::-1], firstm[:, ::-1], -BIG, ALU.add, ALU.max).then_inc(s_x0z, 1)
            v.tensor_scalar(cont, cont, -BIG, None, ALU.mult).then_inc(s_x0z, 1)
            v.tensor_scalar(k0, k0, -BIG, None, ALU.mult).then_inc(s_x0z, 1)
            v.memset(last, 0.0).then_inc(s_x0z, 1)
            dve.wait_ge(s_x0z, 8)
            v.tensor_tensor(last[:, 1:NC], cont[:, 1:NC], o_[:, 0:NC - 1], ALU.add).then_inc(s_x0z, 1)
            v.tensor_scalar(last[:, 0:1], cont[:, 0:1], 1.0, None, ALU.mult).then_inc(s_x0z, 1)
            v.tensor_tensor(p_[:, 0:NC - 1], k0[:, 0:NC - 1], sing[:, 1:NC], ALU.add).then_inc(s_x0z, 1)
            v.tensor_scalar(p_[:, NC - 1:NC], k0[:, NC - 1:NC], 1.0, None, ALU.mult).then_inc(s_x0z, 1)
            dve.wait_ge(s_x0z, 12)
            v.tensor_copy(eo[:, :, :, 0], last.rearrange("h (b c) -> h c b", c=16)).then_inc(s_al, 1)
            v.tensor_copy(eo[:, :, :, 1], p_.rearrange("h (b c) -> h c b", c=16)).then_inc(s_al, 1)
            dve.wait_ge(s_end, 16 * (3 + 16))
            for b in range(NB):
                ins = v.tensor_tensor_scan(sdeT[:, b, :], brk3[:, b, 0:P], alT[:, b, :], cin[:, b, 0:1],
                                           ALU.add, ALU.max)
            ins.then_inc(s_lo, 1)
            dve.wait_ge(s_lo, 18)
            for b in range(NB):
                ins = v.tensor_tensor_scan(dotT[:, b, ::-1], brk3[:, b, 1:P + 1][:, ::-1], sdeT[:, b, ::-1],
                                           cin[:, b, 1:2], ALU.add, ALU.max)
            ins.then_inc(s_lo, 1)
            dve.wait_ge(s_lo, 19)
            for b in range(NB):
                v.tensor_tensor(alT[:, b, :], alT[:, b, :], dotT[:, b, :], ALU.subtract).then_inc(s_mx, 1)

            v.tensor_scalar(lo_si[:, :], recs[1][:, 0:NC, :].bitcast(I32)[:, :, 1], P - 1, None,
                            ALU.bitwise_and).then_inc(s_lo, 1)
            dve.wait_ge(s_lo, 20)
            v.tensor_copy(lo_s[:, :], lo_si[:, :]).then_inc(s_lo, 1)
            dve.wait_ge(s_lo, 21)
            v.scalar_tensor_tensor(out=lo_s[:, :], in0=lo_s[:, :], scalar=1.0, in1=recs[1][:, 0:NC, 6],
                                   op0=ALU.add, op1=ALU.mult).then_inc(s_lo, 1)
            dve.wait_ge(s_lo, 22)
            v.tensor_scalar(lo_s[:, :], lo_s[:, :], -1.0, None, ALU.add).then_inc(s_lo, 1)
            dve.wait_ge(s_lo, 23)
            v.memset(acc[:, :, :], 0.0).then_inc(s_clr, 1)
            dve.wait_ge(s_clr, HOPS + 1)
            dve.wait_ge(s_exs, NB)
            sum_chunks(HOPS, 0)
            with dve.Fori(1, NC // U) as t:
                sum_chunks(HOPS, t)
            for n in range(2):
                add(HOPS, HOPS * NC + NC - 2 + n, U - 2 + n)
            dve.wait_ge(s_add, NC * (HOPS + 1))
            q = LN_STEPS + 4
            v.tensor_scalar(x0[:, :, D:HX], acc[:, :, D:HX], 1e-10, None, ALU.max).then_inc(s_ln, 1)
            dve.wait_ge(s_ln, q + 1)
            v.reciprocal(s_src[:, :, :], x0[:, :, D:HX]).then_inc(s_ln, 1)
            dve.wait_ge(s_ln, q + 2)
            for w in range(NW):
                ins = v.tensor_tensor(acc[:, w, 0:D].rearrange("p (h d) -> p h d", h=HEADS),
                                      acc[:, w, 0:D].rearrange("p (h d) -> p h d", h=HEADS),
                                      s_src[:, w, :].unsqueeze(2).broadcast_to([P, HEADS, HD]), ALU.mult)
            ins.then_inc(s_d, 1)
            R += 1
            dve.wait_ge(s_d, R)
            v.tensor_tensor(acc[:, :, 0:D], acc[:, :, 0:D], bias_b[:, :].unsqueeze(1).broadcast_to([P, NW, D]),
                            ALU.add).then_inc(s_d, 1)
            R += 1
            dve.wait_ge(s_d, R)
            v.tensor_tensor(hcur[:, :, :], hcur[:, :, :], acc[:, :, 0:D], ALU.add).then_inc(s_d, 1)
            R += 1
            dve.wait_ge(s_d, R)
            layer_norm(q + 2, R)


_INS = ['x', 'src', 'dst', 'edge_attr_3', 'edge_weight', 'L0_gnn_Wn', 'L0_gnn_bn', 'L0_gnn_Ws', 'L0_gnn_bs',
        'L1_gnn_W', 'L1_gnn_a_src', 'L1_gnn_a_dst', 'L1_gnn_edge_W', 'L1_gnn_edge_b', 'L1_gnn_bias']


def kernel(**inputs):
    import concourse.bacc as bacc
    from concourse.bass_utils import run_bass_kernel_spmd

    nc = bacc.Bacc("TRN2", target_bir_lowering=False, num_devices=1)
    arrays, args = {}, []
    for name in _INS:
        a = np.ascontiguousarray(inputs[name])
        arrays[f"in_{name}"] = a
        args.append(nc.dram_tensor(f"in_{name}", a.shape, mybir.dt.from_np(a.dtype), kind="ExternalInput").ap())
    out = nc.dram_tensor("out_0", (N, D), F32, kind="ExternalOutput").ap()
    build(nc, *args, out)
    r = run_bass_kernel_spmd(nc, [arrays], core_ids=[0])
    return r.results[0]["out_0"]
```

```python
from contextlib import ExitStack

import numpy as np
import concourse.bass as bass
from concourse import mybir

F32 = mybir.dt.float32
BF16 = mybir.dt.bfloat16
I32 = mybir.dt.int32
ALU = mybir.AluOpType
ACT = mybir.ActivationFunctionType
X = mybir.AxisListType.X

P = 128
SHIFT = 7
N = 3125
D = 256
E = 50000
HOPS = 3
HEADS = 8
HD = D // HEADS
EF = 3
NW = 26
HI = 32
USED = (N + P - 1) // P
EP = 125
EC = E // EP
U = 8
NC = 416
assert EP * EC == E and EC % U == 0 and NC % 16 == 0 and NC % U == 0 and NW % 2 == 0
assert NC >= (E + USED * (P - 1)) // P and NW * P >= N
REC = 8
HX = D + HEADS
NB = NC // 16
LAG = 2
BIG = 1.0e38
EPS = 1e-5


def build(nc, x, src, dst, edge_attr, edge_weight, Wn, bn, Ws, bs, W, a_src, a_dst, edge_W, edge_b, bias, out,
          debug=()):
    dbg = dict(debug)
    with ExitStack() as ctx:
        def sb(name, shape, dt=F32, where=ctx):
            return where.enter_context(nc.sbuf_tensor(name, shape, dt))

        def sem(name):
            return ctx.enter_context(nc.semaphore(name))

        def dram(name, shape):
            return nc.dram_tensor(name, shape, F32, kind="Internal").ap()

        rows_dram = [dram("rows_by_src", [P * NC, REC]), dram("rows_by_dst", [P * NC, REC])]
        h_dram = [dram("h_even", [NW * P, D]), dram("h_odd", [NW * P, D])]
        hh_dram = dram("gat_h", [NW * P, D])
        ss_dram = dram("gat_s_src", [NW * P, HEADS])
        edge_dram = dram("chunk_ends", [P, NB * 4])
        carry_dram = dram("chunk_carries", [HEADS, 16 * NB * 2])

        identf = sb("identf", [P, P])
        identb = sb("identb", [P, P], BF16)
        tri = sb("tri", [P, P])
        triu = sb("triu", [P, P])
        ones = sb("ones", [P, P])
        iota_f = sb("iota_f", [P, NC])
        iota_b = sb("iota_b", [P, P], BF16)
        lane_i = sb("lane_i", [P, 1], I32)
        lane_f = sb("lane_f", [P, 1])
        win_late = [sb(f"win_{key}_late", [1, NC + U], I32) for key in ("src", "dst")]
        win_next = sb("win_dst_next", [1, NC + U], I32)
        wT = sb("wT", [P, 2 * HOPS + 1, 2, D])
        bias6 = sb("bias6", [6, HOPS, D], BF16)
        ew36 = sb("ew36", [36, D], BF16)
        onesb = sb("onesb", [6, P], BF16)
        asrc_b = sb("asrc_b", [P, D])
        adst_b = sb("adst_b", [P, D])
        bias_b = sb("bias_b", [P, D])

        sort = ExitStack()
        src_i = sb("src_i", [P, EC], I32, sort)
        dst_i = sb("dst_i", [P, EC], I32, sort)
        loads = sb("loads", [P, EC * (1 + EF)], F32, sort)
        w_in = loads[:, 0:EC]
        ea_in = loads[:, EC:].rearrange("p (c k) -> p c k", k=EF)
        TERMS = 2 * EP + P + 1
        assert 4 * TERMS <= EC * (1 + EF)
        terms = loads[:, 0:4 * TERMS].rearrange("p (c n) -> p c n", c=4)
        rec = sb("rec", [P, EC, REC], F32, sort)
        key_f = sb("key_f", [P, EC + U], F32, sort)
        earlier = sb("earlier", [P, 2 * EP], F32, sort)
        kst = sb("kst", [P, U], F32, sort)
        lo_i = sb("lo_i", [P, EC], I32, sort)
        lo_f = sb("lo_f", [P, EC], F32, sort)
        hi_f = sb("hi_f", [P, EC], F32, sort)
        ohlo = sb("ohlo", [P, EC, P], BF16, sort)
        early = ohlo[:, EC // 2:, :].rearrange("p c n -> p (c n)")
        BW = HOPS * D
        bias2 = early[0:2, 0:2 * BW].bitcast(F32).rearrange("p (k o) -> p k o", k=HOPS)
        b_parts = early[0:2, 2 * BW:5 * BW].rearrange("p (a k o) -> p a k o", a=3, k=HOPS)
        ew4 = early[0:4, 5 * BW:5 * BW + 2 * D].bitcast(F32)
        ew_parts = early[0:4, 5 * BW + 2 * D:5 * BW + 5 * D].rearrange("p (a o) -> p a o", a=3)
        iota_i = early[:, 5 * BW + 5 * D:5 * BW + 5 * D + 2 * NC].bitcast(I32)
        ohhi = sb("ohhi", [P, EC, HI], BF16, sort)
        ohhiT = sb("ohhiT", [HI, U, EP], F32, sort)
        blocks = sb("blocks", [P, P], F32, sort)
        fold = sb("fold", [P, HI], F32, sort)
        hist = sb("hist", [HI, P], F32, sort)
        table0 = sb("table0", [HI, P], F32, sort)
        table = sb("table", [HI, 2, P], F32, sort)
        small = sb("small", [HI, 8], F32, sort)
        small_i = sb("small_i", [HI, 2], I32, sort)
        started = sb("started", [HI, NC], F32, sort)
        rank = sb("rank", [P, U], F32, sort)
        pos_i = sb("pos_i", [P, 3, U], I32, sort)
        leaving = sb("leaving", [P, 2, U, REC], F32, sort)
        place = sb("place", [P, 2, U], I32, sort)
        wraw = sb("wraw", [P, 2, D], F32, sort)
        sort.close()

        recs = [sb("recs_src", [P, NC + 2 * U, REC]), sb("recs_dst", [P, NC + U, REC])]
        fst = sb("fst", [P, U, 40], BF16)
        lo_s = sb("lo_s", [P, NC + U])
        lo_si = sb("lo_si", [P, NC], I32)
        acc = sb("acc", [P, NW, HX])
        hcur = sb("hcur", [P, NW, D])
        x0 = sb("x0", [P, NW, HX])
        stg = sb("stg", [P, 2, 2 * D])
        stgT = sb("stgT", [P, 2, 2 * D])
        elu = sb("elu", [P, 2, 2 * D])
        gath = sb("gath", [P, U, D])
        idx = sb("idx", [P, U], I32)
        onehot = sb("onehot", [P, 4, P])
        val = sb("val", [P, 4, HX])
        parts12 = acc[:, :, :].rearrange("p w d -> p (w d)").bitcast(BF16)
        h_parts = [parts12[:, i * NW * HX:(i + 1) * NW * HX].rearrange("p (w d) -> p w d", w=NW) for i in range(2)]
        h_parts.append(recs[0][:, :, :].rearrange("p c k -> p (c k)").bitcast(BF16)[:, 0:NW * HX]
                       .rearrange("p (w d) -> p w d", w=NW))
        encr = elu[:, :, :].rearrange("p a (s d) -> p (a s) d", s=2)
        prod = stg[:, :, :].rearrange("p a (s d) -> p (a s) d", s=2)
        eaT = stgT[0:36, :, :].rearrange("p s d -> p (s d)").bitcast(BF16)[:, 0:8 * P].rearrange("p (s d) -> p s d", s=2)
        onehotb = sb("onehotb", [P, 4, P], BF16)
        stat = sb("stat", [P, NW, 4])
        s_sb = sb("s_sb", [P, NC, HEADS])
        dot = sb("dot", [P, NC, HEADS])
        sde = sb("sde", [P, NC, HEADS])
        alT = recs[0][:, 0:NC, :].rearrange("p (b c) k -> p b (c k)", b=NB)
        ends = sb("ends", [P, NB, 4])
        brk = acc[:, :, :].rearrange("p w d -> p (w d)")[:, 0:NB * (P + 1)]
        x0f = x0[:, :, :].rearrange("p w d -> p (w d)")
        el = x0f[0:HEADS, 0:8 * NC].rearrange("h (k c) -> h k c", k=8)
        eh = x0f[0:HEADS, 8 * NC:12 * NC].rearrange("h (c b k) -> h c b k", c=16, k=4)
        eo = x0f[0:HEADS, 12 * NC:14 * NC].rearrange("h (c b k) -> h c b k", c=16, k=2)
        cin = sb("cin", [P, NB, 2])
        s_src = sb("s_src", [P, NW, HEADS])

        bank = [ctx.enter_context(nc.psum_tensor(f"bank{i}", [P, 512], F32)) for i in range(8)]

        s_const = sem("consts_made")
        s_lane = sem("iota_made")
        s_in = sem("edges_loaded")
        s_w = sem("weight_block_loaded")
        s_wT_pe = sem("weight_transposed")
        s_wT = sem("weight_stored")
        s_small = sem("small_weights_loaded")
        s_rec = sem("records_built")
        s_fill = sem("rows_prefilled")
        s_keys = sem("keys_split")
        s_oh = sem("onehots_built")
        s_hist = sem("histogram_done")
        s_part = sem("histogram_blocks_copied")
        s_sum = sem("histogram_blocks_summed")
        s_d = sem("vector_step")
        s_hd = sem("histogram_step")
        s_cum = sem("window_starts_summed")
        s_base = sem("base_table_made")
        s_win = sem("windows_counted")
        s_seed = sem("table_seeded")
        s_hiT = sem("window_onehot_transposed")
        s_hiTs = sem("window_onehot_stored")
        s_row = sem("keys_broadcast")
        s_tab = sem("table_copied")
        s_look = sem("table_read")
        s_upd = sem("table_updated")
        s_rank = sem("ranks_taken")
        s_eq = sem("rank_terms_ready")
        s_pos = sem("positions_ready")
        s_scat = [sem("records_scattered_even"), sem("records_scattered_odd")]
        s_leave = sem("records_leaving")
        s_idx = sem("indices_staged")
        s_back = sem("records_read_back")
        s_lo = sem("los_ready")
        s_x = sem("x_loaded")
        s_lo7 = sem("lo_in_records")
        s_split = sem("parts_split")
        s_kst = sem("keys_staged")
        s_fst = sem("records_staged")
        s_fsl = sem("lo_staged")
        s_x0z = sem("x_tail_cleared")
        s_clr = sem("acc_cleared")
        s_g = [sem(f"rows_gathered{i}") for i in range(U)]
        s_oneh = sem("onehot_made")
        s_mm = sem("chunk_summed")
        s_add = sem("chunk_added")
        s_stg = sem("window_staged")
        s_stT = sem("window_transposed")
        s_stTs = sem("window_transpose_stored")
        s_lin = sem("window_multiplied")
        s_ea = sem("elu_parts")
        s_em = sem("elu_min")
        s_new = sem("window_done")
        s_hst = sem("h_stored")
        s_ln = sem("layer_norm_step")
        s_sq = sem("layer_norm_root")
        s_ss = sem("s_gathered")
        s_eaT = sem("features_transposed")
        s_eaTs = sem("features_stored")
        s_lrow = sem("lo_broadcast")
        s_enc = sem("edge_encoded")
        s_relu = sem("encoding_clipped")
        s_hd_ = sem("h_dst_looked_up")
        s_sde = sem("s_dst_copied")
        s_dot = sem("dot_taken")
        s_al = sem("alpha_step")
        s_alT = sem("alpha_transposed")
        s_alTs = sem("alpha_transpose_stored")
        s_end = sem("chunk_ends_moved")
        s_mx = sem("max_ready")
        s_ex = sem("exp_done")
        s_exT = sem("exp_transposed")
        s_exs = sem("exp_stored")
        s_val = sem("values_scaled")
        s_vx = sem("exp_column_copied")
        s_out = sem("out_stored")
        s_dbg = sem("dbg")

        def nodes(t, cols=None):
            return t.rearrange("(w p) d -> p w d", p=P)

        def windows(engine, row, c, n):
            return nc.values_load_multi_w_load_instructions(
                row[0:1, bass.ds(c, n)], engines=(engine,), min_val=0, max_val=NW - 1,
                skip_runtime_bounds_check_because="a count of the USED windows, less one")[1]

        groups = EC // U

        def split(eng, parts, full, sem_, q):
            for i in range(3):
                nc.vector.tensor_copy(parts[i], full).then_inc(sem_, 1)
                eng.wait_ge(sem_, q + 2 * i + 1)
                if i < 2:
                    nc.vector.tensor_tensor(full, full, parts[i], ALU.subtract).then_inc(sem_, 1)
                    eng.wait_ge(sem_, q + 2 * i + 2)

        def turn(k):
            return k if k < HOPS else k + 1
        FULLW = N // P

        zero_tile = ohlo[:, 0:NC * REC * 2 // P, :].bitcast(F32).rearrange("p a b -> p (a b)")

        LN_STEPS = 6
        AL_ENDS = 6
        AL_CARRY = 17
        dotT = dot[:, :, :].rearrange("p (b c) h -> p b (c h)", b=NB)
        sdeT = sde[:, :, :].rearrange("p (b c) h -> p b (c h)", b=NB)
        brk3 = brk.rearrange("p (b e) -> p b e", b=NB)

        block = ctx.enter_context(nc.Block())

        @block.sync
        def _(sp):
            sp.dma_start(src_i[0:EP, :], src.rearrange("(p c) -> p c", c=EC)).then_inc(s_in, 16)
            sp.dma_start(dst_i[0:EP, :], dst.rearrange("(p c) -> p c", c=EC)).then_inc(s_in, 16)
            sp.dma_start(w_in[0:EP, :], edge_weight.rearrange("(p c) -> p c", c=EC)).then_inc(s_in, 16)
            sp.dma_start(ea_in[0:EP, :, :], edge_attr.rearrange("(p c) k -> p c k", c=EC)).then_inc(s_in, 16)
            sp.wait_ge(s_fill, 1)
            for r in rows_dram:
                sp.dma_start(r.rearrange("(p c) k -> p (c k)", p=P), zero_tile).then_inc(s_fill, 16)
            for k in range(HOPS):
                sp.dma_start(bias2[0:1, k, :], bn[k:k + 1, :]).then_inc(s_small, 16)
                sp.dma_start(bias2[1:2, k, :], bs[k:k + 1, :]).then_inc(s_small, 16)
            with nc.allow_non_contiguous_dma(reason="three short columns"):
                sp.dma_start(ew4[0:EF, :], edge_W.rearrange("o k -> k o")).then_inc(s_small, 16)
            sp.dma_start(ew4[EF:EF + 1, :], edge_b.rearrange("(a o) -> a o", a=1)).then_inc(s_small, 16)
            for t, v in ((asrc_b, a_src.rearrange("(a h) d -> a (h d)", a=1)),
                         (adst_b, a_dst.rearrange("(a h) d -> a (h d)", a=1)),
                         (bias_b, bias.rearrange("(a o) -> a o", a=1))):
                sp.dma_start(t[:, :], v.broadcast_to([P, D])).then_inc(s_small, 16)
            sp.wait_ge(s_split, 6)
            for a in range(3):
                sp.dma_start(bias6[2 * a:2 * a + 2, :, :], b_parts[:, a, :, :]).then_inc(s_small, 16)
            sp.wait_ge(s_split, 11)
            for a in range(3):
                for b in range(3):
                    r0 = 4 * (3 * a + b)
                    sp.dma_start(ew36[r0:r0 + 4, :], ew_parts[:, b, :]).then_inc(s_small, 16)
            for m in range(2 * HOPS + 1):
                if m >= 1:
                    sp.wait_ge(s_wT_pe, m)
                mat = W if m == 2 * HOPS else (Wn, Ws)[m % 2][m // 2]
                sp.dma_start(wraw[:, :, :], mat.rearrange("(a p) k -> p a k", p=P)).then_inc(s_w, 16)

            for q in s_scat:
                sp.wait_ge(q, 16 * EC)
            sp.wait_ge(s_tab, EC + 2)
            for k in range(2):
                sp.dma_start(recs[k][:, 0:NC, :], rows_dram[k].rearrange("(p c) k -> p c k", p=P)).then_inc(s_back, 16)
            sp.wait_ge(s_x0z, 2)
            for t in (x0, hcur):
                sp.dma_start(t[:, 0:FULLW, 0:D], x[0:FULLW * P, :].rearrange("(w p) d -> p w d", p=P)).then_inc(s_x, 16)
                sp.dma_start(t[0:N - FULLW * P, FULLW, 0:D], x[FULLW * P:N, :]).then_inc(s_x, 16)
            for k in range(HOPS - 1):
                sp.wait_ge(s_new, NW * (k + 1))
                sp.dma_start(nodes(h_dram[k]), hcur[:, :, :]).then_inc(s_hst, 16)
            sp.wait_ge(s_new, NW * (HOPS + 1))
            sp.dma_start(nodes(hh_dram), x0[:, :, 0:D]).then_inc(s_hst, 16)
            sp.wait_ge(s_ln, LN_STEPS + 2)
            sp.dma_start(nodes(ss_dram), s_src[:, :, :]).then_inc(s_hst, 16)
            sp.wait_ge(s_al, AL_ENDS)
            sp.dma_start(edge_dram, ends[:, :, :].rearrange("p b k -> p (b k)")).then_inc(s_end, 16)
            sp.wait_ge(s_end, 16)
            sp.dma_start(eh[:, :, :, :].rearrange("h c b k -> h c (b k)"),
                         edge_dram.rearrange("(c h) k -> h c k", h=HEADS)).then_inc(s_end, 16)
            sp.wait_ge(s_al, AL_CARRY)
            sp.dma_start(carry_dram, eo[:, :, :, :].rearrange("h c b k -> h (c b k)")).then_inc(s_end, 16)
            sp.wait_ge(s_end, 48)
            for c in range(16):
                sp.dma_start(cin[c * HEADS:(c + 1) * HEADS, :, :].rearrange("p b k -> p (b k)"),
                             carry_dram[:, c * NB * 2:(c + 1) * NB * 2]).then_inc(s_end, 16)
            sp.wait_ge(s_ln, 2 * LN_STEPS + 6)
            sp.dma_start(out[0:FULLW * P, :].rearrange("(w p) d -> p w d", p=P), hcur[:, 0:FULLW, :]).then_inc(s_out, 16)
            sp.dma_start(out[FULLW * P:N, :], hcur[0:N - FULLW * P, FULLW, :]).then_inc(s_out, 16)
            sp.wait_ge(s_out, 32)


        @block.gpsimd
        def _(pool):
            pool.memset(identf[:, :], 0.0).then_inc(s_lane, 1)
            pool.memset(ones[:, :], 1.0).then_inc(s_lane, 1)
            pool.iota(iota_i[:, :], [[1, NC]], base=0, channel_multiplier=0).then_inc(s_lane, 1)
            pool.iota(lane_i[:, :], [[1, 1]], base=0, channel_multiplier=1).then_inc(s_lane, 1)
            pool.wait_ge(s_lane, 4)
            pool.affine_select(out=identf[:, :], in_=identf[:, :], compare_op=ALU.not_equal, fill=1.0, base=0,
                               pattern=[[-1, P]], channel_multiplier=1).then_inc(s_lane, 1)
            pool.affine_select(out=tri[:, :], in_=ones[:, :], compare_op=ALU.is_gt, fill=0.0, base=0,
                               pattern=[[-1, P]], channel_multiplier=1).then_inc(s_lane, 1)
            pool.affine_select(out=triu[:, :], in_=ones[:, :], compare_op=ALU.is_gt, fill=0.0, base=0,
                               pattern=[[1, P]], channel_multiplier=-1).then_inc(s_lane, 1)
            pool.wait_ge(s_fill, 1 + 32)
            pool.wait_ge(s_rec, 6)
            for k in range(2):
                with pool.Fori(0, groups // 2) as t:
                    for h in range(2):
                        g = 2 * t + h
                        pool.wait_ge(s_leave, g + groups * k + 1)
                        pool.wait_ge(s_pos, g + groups * k + 1)
                        pool.nop(nofuse=True)
                        for j in range(U):
                            pool.indirect_dma_start(
                                out=rows_dram[k],
                                in_=leaving[0:EP, h, j, :],
                                out_offset=bass.IndirectOffsetOnAxis(ap=place[0:EP, h, j:j + 1], axis=0),
                                in_offset=None).then_inc(s_scat[h], 16)

            def gather(p, t, table, ring, first):
                for j in range(U):
                    if ring is not None and not first:
                        pool.wait_ge(s_mm, ring * NC + (t - 1) * U + j + 1)
                        pool.nop(nofuse=True)
                    if j % 4 == 0:
                        pool.wait_ge(s_idx, p * (2 * NC // U + 2) + 2 * t + j // 4 + 1)
                        pool.nop(nofuse=True)
                    o = gath[:, j, :] if ring is not None else gath[:, j, 0:HEADS]
                    pool.indirect_dma_start(
                        out=o, out_offset=None, in_=table,
                        in_offset=bass.IndirectOffsetOnAxis(ap=idx[:, j:j + 1], axis=0)).then_inc(s_g[j], 16)

            for k in range(HOPS):
                if k >= 1:
                    pool.wait_ge(s_hst, 16 * k)
                gather(k, 0, x if k == 0 else h_dram[k - 1], k, k == 0)
                with pool.Fori(1, NC // U) as t:
                    gather(k, t, x if k == 0 else h_dram[k - 1], k, False)
            pool.wait_ge(s_hst, 16 * (HOPS + 1))
            pool.nop(nofuse=True)
            with pool.Fori(0, NC // U) as t:
                gather(HOPS, t, ss_dram, None, False)
            gather(HOPS + 1, 0, hh_dram, HOPS, False)
            with pool.Fori(1, NC // U) as t:
                gather(HOPS + 1, t, hh_dram, HOPS, False)

        @block.tensor
        def _(pe):
            pe.wait_ge(s_const, 4)
            for m in range(2 * HOPS + 1):
                pe.wait_ge(s_w, 16 * (m + 1))
                if m >= 2:
                    pe.wait_ge(s_wT, m - 1)
                for a in range(2):
                    for b in range(2):
                        i = pe.transpose(bank[m % 2][:, b * D + a * P:b * D + (a + 1) * P],
                                         wraw[:, a, b * P:(b + 1) * P], identf[:, :])
                i.then_inc(s_wT_pe, 1)

            for k in range(2):
                def count(t, start, stop):
                    pe.wait_ge(s_oh, k * (groups + 1) + t + 2)
                    for j in range(0, U, 4):
                        i = pe.matmul(bank[0][:, :], ohhi[0:EP, bass.ds(t * U + j, 4), :].rearrange("p c k -> p (c k)"),
                                      ohlo[0:EP, bass.ds(t * U + j, 4), :].rearrange("p c k -> p (c k)"),
                                      start=start and j == 0, stop=stop and j == U - 4, skip_group_check=True)
                    return i
                pe.wait_ge(s_wT, 2 * HOPS + 1)
                count(0, True, False)
                with pe.Fori(1, groups - 1) as t:
                    count(t, False, False)
                count(groups - 1, False, True).then_inc(s_hist, 1)
                pe.wait_ge(s_part, 4 * k + 4)
                pe.matmul(bank[1][0:HI, 0:P], fold[:, :], blocks[:, :], start=True, stop=True).then_inc(s_sum, 1)
                pe.wait_ge(s_hd, 10 * k + 4)
                pe.matmul(bank[1][0:HI, 0:1], triu[0:HI, 0:HI], small[:, 2:3], start=True, stop=True).then_inc(s_cum, 1)
                pe.wait_ge(s_hd, 10 * k + 9)
                pe.matmul(bank[1][0:1, 0:NC], ones[0:USED, 0:1], started[0:USED, :], start=True,
                          stop=True).then_inc(s_win, 1)
                if k:
                    pe.wait_ge(s_tab, EC // 2 + 1)
                pe.matmul(bank[2][0:HI, 0:P], identf[0:HI, 0:HI], table0[:, :], start=True, stop=False,
                          skip_group_check=True).then_inc(s_seed, 1)

                def spread(t, s, n, cold):
                    h, rows = bank[3 + s][0:HI, :], bank[5 + s]
                    if not cold:
                        pe.wait_ge(s_hiTs, n - 1)
                    for j in range(4):
                        i = pe.matmul(h[:, j * EP:(j + 1) * EP],
                                      ohhi[0:EP, bass.ds(t * U + 4 * s + j, 1), :].rearrange("p c k -> p (c k)"),
                                      identb[0:EP, 0:EP], start=True, stop=True, skip_group_check=True)
                    i.then_inc(s_hiT, 1)
                    yield
                    if not cold:
                        pe.wait_ge(s_rank, n - 1)
                    pe.wait_ge(s_kst, n + 2 * k + 1)
                    for j in range(4):
                        i = pe.transpose(rows[0:EP, j * EP:(j + 1) * EP],
                                         kst[0:EP, 4 * s + j:4 * s + j + 1].broadcast_to([EP, EP]),
                                         identf[0:EP, 0:EP])
                    i.then_inc(s_row, 1)
                    yield

                def rank_step(t, first, last=False):
                    for s in range(2):
                        n = 2 * (groups * k + t) + s
                        pe.wait_ge(s_hiTs, n + 1)
                        if not first:
                            pe.wait_ge(s_rank, n - 1)
                        ahead = iter(()) if last and s else spread(t + s, 1 - s, n + 1, first and s == 0)
                        for half in range(2):
                            pe.wait_ge(s_tab, (EC // 2 + 1) * k + U // 2 * t + 2 * s + half + 1)
                            for j in (2 * half, 2 * half + 1):
                                pe.matmul(bank[7 * s][0:EP, j * P:(j + 1) * P], ohhiT[:, 4 * s + j, :],
                                          table[:, half, :], start=True, stop=True,
                                          skip_group_check=True).then_inc(s_look, 1)
                            for j in (2 * half, 2 * half + 1):
                                c = t * U + 4 * s + j
                                i = pe.matmul(bank[2][0:HI, 0:P],
                                              ohhi[0:EP, bass.ds(c, 1), :].rearrange("p c k -> p (c k)"),
                                              ohlo[0:EP, bass.ds(c, 1), :].rearrange("p c k -> p (c k)"),
                                              start=False, stop=False, skip_group_check=True)
                            i.then_inc(s_upd, 1)
                            next(ahead, None)

                for _ in spread(0, 0, 2 * groups * k, k == 0):
                    pass
                rank_step(0, k == 0)
                with pe.Fori(1, groups - 1) as t:
                    rank_step(t, False)
                rank_step(groups - 1, False, True)
            pe.wait_ge(s_rank, 4 * groups)

            def sum_chunks(k, t, first):
                for j in range(U):
                    n = k * NC + t * U + j
                    pe.wait_ge(s_g[j], 16 * (turn(k) * (NC // U) + t + 1))
                    pe.wait_ge(s_oneh, n + 1)
                    if not (first and j < 4):
                        pe.wait_ge(s_add, n - 3)
                    pe.matmul(bank[j % 4][:, 0:D], onehot[:, j % 4, :], gath[:, j, :], start=True,
                              stop=True).then_inc(s_mm, 1)

            def dense(k, t, first):
                parts = 4 if k < HOPS else 2
                for s in range(2):
                    n = k * NW + 2 * t + s
                    pe.wait_ge(s_stg, n + 1)
                    if not first:
                        pe.wait_ge(s_stTs, n - 1)
                    for q in range(parts):
                        i = pe.transpose(bank[4 + s][:, q * P:(q + 1) * P], stg[:, s, q * P:(q + 1) * P], identf[:, :])
                    i.then_inc(s_stT, 1)
                for s in range(2):
                    n = k * NW + 2 * t + s
                    pe.wait_ge(s_stTs, n + 1)
                    if not first:
                        pe.wait_ge(s_new, n - 1)
                    for q in range(parts):
                        i = pe.matmul(bank[6 + s][:, 0:D], stgT[:, s, q * P:(q + 1) * P],
                                      wT[:, 2 * k + q // 2, q % 2, :], start=q == 0, stop=k == HOPS and q == parts - 1)
                    if k < HOPS:
                        i = pe.matmul(bank[6 + s][:, 0:D], onesb[:, :], bias6[:, k, :], start=False, stop=True)
                    i.then_inc(s_lin, 1)

            pe.wait_ge(s_small, 16 * (2 * HOPS + 5 + 12))
            for k in range(HOPS):
                sum_chunks(k, 0, k == 0)
                with pe.Fori(1, NC // U) as t:
                    sum_chunks(k, t, False)
                dense(k, 0, k == 0)
                with pe.Fori(1, NW // 2) as t:
                    dense(k, t, False)
            dense(HOPS, 0, False)
            with pe.Fori(1, NW // 2) as t:
                dense(HOPS, t, False)

            def transpose_features(g, s):
                pe.wait_ge(s_fst, g + 1)
                pe.wait_ge(s_fsl, g + 1)
                pe.nop(nofuse=True)
                for j in range(4):
                    i = pe.transpose(bank[s][0:36, 0:2 * P].bitcast(BF16)[:, j * P:(j + 1) * P], fst[:, 4 * s + j, 0:36],
                                     identb[:, :])
                i.then_inc(s_eaT, 1)

            def score(t, first):
                ws = windows(mybir.EngineType.PE, win_next, t * U, U) if not first else (
                    (None, *windows(mybir.EngineType.PE, win_next, 1, U - 1)))
                for j in range(U):
                    n = t * U + j
                    if not (first and j < 2):
                        pe.wait_ge(s_oneh, HOPS * NC + n - 1)
                    pe.transpose(bank[2 + j % 2][:, 0:P // 2].bitcast(BF16), fst[:, j, 36:37].broadcast_to([P, P]),
                                 identb[:, :]).then_inc(s_lrow, 1)
                    if j % 4 == 0:
                        pe.wait_ge(s_eaTs, 2 * t + j // 4 + 1)
                    if not (first and j < 2):
                        pe.wait_ge(s_relu, n - 1)
                    pe.matmul(bank[4 + j % 2][:, 0:D], eaT[:, j // 4, (j % 4) * P:(j % 4 + 1) * P], ew36[:, :],
                              start=True, stop=True).then_inc(s_enc, 1)
                    if not (first and j == 0):
                        look_up(n - 1, (j - 1) % U, ws[j], first and 1 <= j < 3)
                    if j % 4 == 1:
                        transpose_features(2 * t + j // 4 + 1, 1 - j // 4)

            def look_up(n, j, w, cold):
                pe.wait_ge(s_oneh, HOPS * NC + n + 1)
                if not cold:
                    pe.wait_ge(s_em, (HOPS - 1) * NW + n - 1)
                    pe.wait_ge(s_sde, n - 1)
                for i in range(3):
                    mm = pe.matmul(bank[6 + j % 2][:, 0:HX], onehotb[:, j % 4, :],
                                   h_parts[i][:, bass.ds(w, 1), :].rearrange("p c k -> p (c k)"),
                                   start=i == 0, stop=i == 2)
                mm.then_inc(s_hd_, 1)
            pe.wait_ge(s_split, 22)
            transpose_features(0, 0)
            score(0, True)
            with pe.Fori(1, NC // U) as t:
                score(t, False)
            look_up(NC - 1, U - 1, windows(mybir.EngineType.PE, win_next, NC, 1)[0], False)

            pe.wait_ge(s_al, 4)
            for i in range(2 * NB):
                if i >= 2:
                    pe.wait_ge(s_alTs, i - 1)
                a = (s_sb if i < NB else sde)[:, 16 * (i % NB):16 * (i % NB) + 16, :].rearrange("p c h -> p (c h)")
                pe.transpose(bank[i % 2][:, 0:P], a, identf[:, :]).then_inc(s_alT, 1)
            pe.wait_ge(s_ex, NB)
            for i in range(NB):
                if i >= 2:
                    pe.wait_ge(s_exs, i - 1)
                pe.transpose(bank[2 + i % 2][:, 0:P], alT[:, i, :], identf[:, :]).then_inc(s_exT, 1)

            def attend(t):
                for j in range(U):
                    n = HOPS * NC + t * U + j
                    pe.wait_ge(s_val, t * U + j + 1)
                    pe.wait_ge(s_vx, t * U + j + 1)
                    pe.wait_ge(s_oneh, NC + n + 1)
                    pe.wait_ge(s_add, n - 3)
                    pe.matmul(bank[4 + j % 4][:, 0:HX], onehot[:, j % 4, :], val[:, j % 4, :], start=True,
                              stop=True).then_inc(s_mm, 1)
            with pe.Fori(0, NC // U) as t:
                attend(t)

        @block.scalar
        def _(act):
            for m in range(2 * HOPS + 1):
                act.wait_ge(s_wT_pe, m + 1)
                nc.scalar.copy(wT[:, m, :, :].rearrange("p a o -> p (a o)"), bank[m % 2][:, :]).then_inc(s_wT, 1)
            for k in range(2):
                act.wait_ge(s_seed, k + 1)
                nc.scalar.copy(table[:, 0, :], bank[2][0:HI, 0:P]).then_inc(s_tab, 1)

                def stage(c, j):
                    nc.scalar.copy(kst[0:EP, j:j + 4], key_f[0:EP, bass.ds(c, 4)]).then_inc(s_kst, 1)

                stage(0, 0)
                stage(4, 4)

                def store_hiT(g, s):
                    act.wait_ge(s_hiT, g + 1)
                    nc.scalar.copy(ohhiT[:, 4 * s:4 * s + 4, :],
                                   bank[3 + s][0:HI, 0:4 * EP].rearrange("p (a e) -> p a e", a=4)).then_inc(s_hiTs, 1)

                def step(t, last=False):
                    for j in range(U):
                        if j % 4 == 2:
                            act.wait_ge(s_eq, 5 * (2 * (groups * k + t) + j // 4) + 4)
                            act.nop(nofuse=True)
                            stage((t + 1) * U + j - 2, j - 2)
                        if j % 2:
                            act.wait_ge(s_upd, EC // 2 * k + U // 2 * t + j // 2 + 1)
                            nc.scalar.copy(table[:, (j // 2 + 1) % 2, :], bank[2][0:HI, 0:P]).then_inc(s_tab, 1)
                        if j % 4 == 1 and not (last and j == 5):
                            store_hiT(2 * (groups * k + t) + j // 4 + 1, 1 - j // 4)
                store_hiT(2 * groups * k, 0)
                step(0)
                with act.Fori(1, groups - 1) as t:
                    step(t)
                step(groups - 1, True)

            def dense(k, t):
                parts = 4 if k < HOPS else 2
                for s in range(2):
                    n = k * NW + 2 * t + s
                    act.wait_ge(s_stT, n + 1)
                    nc.scalar.copy(stgT[:, s, 0:parts * P], bank[4 + s][:, 0:parts * P]).then_inc(s_stTs, 1)
                if k < HOPS - 1:
                    for s in range(2):
                        n = k * NW + 2 * t + s
                        act.wait_ge(s_em, n + 1)
                        nc.scalar.activation(elu[:, s, 0:D], bank[6 + s][:, 0:D], ACT.Relu).then_inc(s_ea, 1)
                        nc.scalar.activation(elu[:, s, D:2 * D], elu[:, s, D:2 * D], ACT.Exp).then_inc(s_ea, 1)
            def stage_idx(p, t, h, first=False):
                if not (first and p == 0):
                    for j in range(4 * h, 4 * h + 4):
                        act.wait_ge(s_g[j], 16 * (p * (NC // U) + t))
                    act.nop(nofuse=True)
                if p == HOPS and not first:
                    nc.scalar.copy(s_sb[:, bass.ds((t - 1) * U + 4 * h, 4), :],
                                   gath[:, 4 * h:4 * h + 4, 0:HEADS]).then_inc(s_ss, 1)
                r, col = (recs[0], 1) if p < HOPS else (recs[1], 0)
                nc.scalar.copy(idx[:, 4 * h:4 * h + 4],
                               r[:, bass.ds(t * U + 4 * h, 4), col].bitcast(I32)).then_inc(s_idx, 1)

            act.wait_ge(s_back, 32)
            act.wait_ge(s_lo7, 2)
            for k in range(HOPS + 1):
                if k < HOPS:
                    stage_idx(k, 0, 0, True)
                    stage_idx(k, 0, 1, True)
                    with act.Fori(0, NC // U) as t:
                        stage_idx(k, t + 1, 0)
                        stage_idx(k, t + 1, 1)
                with act.Fori(0, NW // 2) as t:
                    dense(k, t)
                if k == HOPS - 1:
                    act.wait_ge(s_ln, 4)
                    nc.scalar.activation(stat[:, :, 2], stat[:, :, 1], ACT.Sqrt).then_inc(s_sq, 1)

            act.wait_ge(s_lo7, 3)

            def stage_recs(c, j):
                e = recs[1][:, bass.ds(c, 4), 2:8].bitcast(BF16)
                nc.scalar.copy(fst[:, j:j + 4, 36], lo_s[:, bass.ds(c, 4)]).then_inc(s_fsl, 1)
                for a in range(3):
                    i = nc.scalar.copy(fst[:, j:j + 4, 12 * a:12 * a + 12].rearrange("p c (b f) -> p c b f", b=3),
                                       e[:, :, 4 * a:4 * a + 4].unsqueeze(2).broadcast_to([P, 4, 3, 4]))
                i.then_inc(s_fst, 1)

            stage_recs(0, 0)
            stage_recs(4, 4)
            stage_idx(HOPS, 0, 0, True)
            stage_idx(HOPS, 0, 1, True)

            def keep_s_dst(n, j):
                act.wait_ge(s_hd_, n + 1)
                act.nop(nofuse=True)
                nc.scalar.copy(sde[:, bass.ds(n, 1), :].rearrange("p c h -> p (c h)"),
                               bank[6 + j % 2][:, D:HX]).then_inc(s_sde, 1)

            def store_features(g, s):
                act.wait_ge(s_eaT, g + 1)
                nc.scalar.copy(eaT[:, s, :], bank[s][0:36, 0:2 * P].bitcast(BF16)).then_inc(s_eaTs, 1)

            def score(t):
                for j in range(U):
                    n = t * U + j
                    act.wait_ge(s_enc, n + 1)
                    if not (isinstance(t, int) and j < 4):
                        act.wait_ge(s_em, (HOPS - 1) * NW + n - 3)
                    nc.scalar.activation(encr[:, j % 4, :], bank[4 + j % 2][:, 0:D], ACT.Relu).then_inc(s_relu, 1)
                    if not (isinstance(t, int) and j == 0):
                        keep_s_dst(n - 1, (j - 1) % U)
                    if j % 4 == 2:
                        store_features(2 * t + j // 4 + 1, 1 - j // 4)
                    if j % 4 == 3:
                        stage_recs((t + 1) * U + j - 3, j - 3)
                        stage_idx(HOPS, t + 1, j // 4)
            store_features(0, 0)
            score(0)
            with act.Fori(1, NC // U) as t:
                score(t)
            keep_s_dst(NC - 1, U - 1)
            for i in range(2 * NB):
                act.wait_ge(s_alT, i + 1)
                nc.scalar.copy((alT if i < NB else dotT)[:, i % NB, :], bank[i % 2][:, 0:P]).then_inc(s_alTs, 1)
            for b in range(NB):
                act.wait_ge(s_mx, b + 1)
                nc.scalar.activation(alT[:, b, :], alT[:, b, :], ACT.Exp).then_inc(s_ex, 1)
            for i in range(NB):
                act.wait_ge(s_exT, i + 1)
                nc.scalar.copy(s_sb[:, 16 * i:16 * i + 16, :].rearrange("p c h -> p (c h)"),
                               bank[2 + i % 2][:, 0:P]).then_inc(s_exs, 1)
            act.wait_ge(s_exs, NB)

            def attend(t):
                for j in range(U):
                    n = t * U + j
                    act.wait_ge(s_mm, HOPS * NC + n - 3)
                    act.nop(nofuse=True)
                    nc.scalar.copy(val[:, j % 4, D:HX], s_sb[:, bass.ds(n, 1), :].rearrange("p c h -> p (c h)")
                                   ).then_inc(s_vx, 1)
                    if j % 4 == 3:
                        stage_idx(HOPS + 1, t + 1, j // 4)
            stage_idx(HOPS + 1, 0, 0)
            stage_idx(HOPS + 1, 0, 1)
            attend(0)
            with act.Fori(1, NC // U) as t:
                attend(t)
            act.wait_ge(s_ln, LN_STEPS + 4 + 2 + 4)
            nc.scalar.activation(stat[:, :, 2], stat[:, :, 1], ACT.Sqrt).then_inc(s_sq, 1)


        @block.vector
        def _(dve):
            v = nc.vector
            v.memset(zero_tile, 0.0).then_inc(s_fill, 1)
            dve.wait_ge(s_lane, 7)
            v.tensor_copy(iota_f[:, :], iota_i[:, :]).then_inc(s_const, 1)
            v.tensor_copy(iota_b[:, :], iota_i[:, 0:P]).then_inc(s_const, 1)
            v.tensor_copy(lane_f[:, :], lane_i[:, :]).then_inc(s_const, 1)
            v.tensor_copy(identb[:, :], identf[:, :]).then_inc(s_const, 1)
            v.memset(key_f[0:EP, EC:EC + U], 0.0).then_inc(s_const, 1)
            v.tensor_reduce(fold[:, :], identf[:, :].rearrange("p (b i) -> p i b", i=HI), X, ALU.add).then_inc(s_const, 1)
            v.memset(earlier[0:EP, 0:EP], 1.0).then_inc(s_const, 1)
            v.tensor_copy(earlier[0:EP, EP:2 * EP], tri[0:EP, 0:EP]).then_inc(s_const, 1)
            dve.wait_ge(s_small, 16 * (2 * HOPS + 5))
            split(dve, [b_parts[:, i, :, :] for i in range(3)], bias2, s_split, 0)
            v.memset(onesb[:, :], 1.0).then_inc(s_split, 1)
            split(dve, [ew_parts[:, i, :] for i in range(3)], ew4, s_split, 6)
            dve.wait_ge(s_in, 64)
            rec_i = rec[:, :, :].bitcast(I32)
            v.tensor_copy(rec_i[0:EP, :, 0], src_i[0:EP, :]).then_inc(s_rec, 1)
            v.tensor_copy(rec_i[0:EP, :, 1], dst_i[0:EP, :]).then_inc(s_rec, 1)
            v.tensor_copy(rec[0:EP, :, 2], w_in[0:EP, :]).then_inc(s_rec, 1)
            v.tensor_copy(rec[0:EP, :, 3:6], ea_in[0:EP, :, :]).then_inc(s_rec, 1)
            v.memset(rec[0:EP, :, 6], 1.0).then_inc(s_rec, 1)
            v.memset(rec[0:EP, :, 7], 0.0).then_inc(s_rec, 1)
            dve.wait_ge(s_rec, 6)

            for k in range(2):
                key = (src_i, dst_i)[k]
                if k:
                    dve.wait_ge(s_upd, EC // 2)
                    dve.wait_ge(s_row, 2 * groups)
                v.tensor_copy(key_f[0:EP, 0:EC], key[0:EP, :]).then_inc(s_keys, 1)
                v.tensor_scalar(lo_i[0:EP, :], key[0:EP, :], P - 1, None, ALU.bitwise_and).then_inc(s_keys, 1)
                dve.wait_ge(s_keys, 5 * k + 2)
                v.tensor_copy(lo_f[0:EP, :], lo_i[0:EP, :]).then_inc(s_keys, 1)
                dve.wait_ge(s_keys, 5 * k + 3)
                v.tensor_scalar(lo_i[0:EP, :], key[0:EP, :], SHIFT, None, ALU.logical_shift_right).then_inc(s_keys, 1)
                dve.wait_ge(s_keys, 5 * k + 4)
                v.tensor_copy(hi_f[0:EP, :], lo_i[0:EP, :]).then_inc(s_keys, 1)
                dve.wait_ge(s_keys, 5 * k + 5)
                v.tensor_tensor(ohhi[0:EP, :, :], hi_f[0:EP, :].unsqueeze(2).broadcast_to([EP, EC, HI]),
                                iota_f[0:EP, 0:HI].unsqueeze(1).broadcast_to([EP, EC, HI]),
                                ALU.is_equal).then_inc(s_oh, 1)
                if k == 0:
                    dve.wait_ge(s_fill, 33)
                    dve.wait_ge(s_small, 16 * (2 * HOPS + 5 + 12))
                with dve.Fori(0, groups) as t:
                    v.tensor_tensor(ohlo[0:EP, bass.ds(t * U, U), :],
                                    lo_f[0:EP, bass.ds(t * U, U)].unsqueeze(2).broadcast_to([EP, U, P]),
                                    iota_b[0:EP, :].unsqueeze(1).broadcast_to([EP, U, P]),
                                    ALU.is_equal).then_inc(s_oh, 1)
                q = 10 * k
                dve.wait_ge(s_hist, k + 1)
                for j in range(4):
                    v.tensor_copy(blocks[j * HI:(j + 1) * HI, :],
                                  bank[0][j * HI:(j + 1) * HI, j * P:(j + 1) * P]).then_inc(s_part, 1)
                dve.wait_ge(s_sum, k + 1)
                v.tensor_copy(hist[:, :], bank[1][0:HI, 0:P]).then_inc(s_hd, 1)
                dve.wait_ge(s_hd, q + 1)
                v.tensor_reduce(small[:, 0:1], hist[:, :], X, ALU.add).then_inc(s_hd, 1)
                dve.wait_ge(s_hd, q + 2)
                v.tensor_scalar(small_i[:, 0:1], small[:, 0:1], float(P - 1), None, ALU.add).then_inc(s_hd, 1)
                dve.wait_ge(s_hd, q + 3)
                v.tensor_scalar(small_i[:, 1:2], small_i[:, 0:1], SHIFT, None,
                                ALU.logical_shift_right).then_inc(s_base, 1)
                dve.wait_ge(s_base, k + 1)
                v.tensor_copy(small[:, 2:3], small_i[:, 1:2]).then_inc(s_hd, 1)
                dve.wait_ge(s_cum, k + 1)
                v.tensor_copy(small[:, 3:4], bank[1][0:HI, 0:1]).then_inc(s_hd, 1)
                dve.wait_ge(s_hd, q + 5)
                v.tensor_scalar(small[:, 4:5], small[:, 3:4], float(P), None, ALU.mult).then_inc(s_hd, 1)
                dve.wait_ge(s_hd, q + 6)
                v.tensor_tensor_scan(table0[:, :], ones[0:HI, :], hist[:, :], small[:, 4:5], ALU.mult,
                                     ALU.add).then_inc(s_hd, 1)
                dve.wait_ge(s_hd, q + 7)
                v.tensor_tensor(table0[:, :], table0[:, :], hist[:, :], ALU.subtract).then_inc(s_hd, 1)
                v.tensor_scalar(started[:, :], iota_f[0:HI, :], small[:, 3:4], None, ALU.is_ge).then_inc(s_hd, 1)
                dve.wait_ge(s_win, k + 1)
                if k:
                    v.tensor_scalar(win_next[:, 1:NC + 1], bank[1][0:1, 0:NC], -1.0, None, ALU.add).then_inc(s_base, 1)
                v.tensor_scalar(win_late[k][:, LAG:NC + LAG], bank[1][0:1, 0:NC], -1.0, None,
                                ALU.add).then_inc(s_hd, 1)

                def ranks(pair, h, first):
                    t = 2 * pair + h
                    g = groups * k + t
                    for q in range(2):
                        tm = terms[0:EP, :, :]
                        if not (first and h == 0 and q == 0):
                            dve.wait_ge(s_rank, 2 * g + q)
                        dve.wait_ge(s_row, 2 * g + q + 1)
                        for j in range(4):
                            wide = (j % 2 + 1) * EP
                            v.scalar_tensor_tensor(out=tm[:, j, 0:wide],
                                                   in0=bank[5 + q][0:EP, j // 2 * 2 * EP:j // 2 * 2 * EP + wide],
                                                   scalar=kst[0:EP, 4 * q + j:4 * q + j + 1],
                                                   in1=earlier[0:EP, 2 * EP - wide:2 * EP], op0=ALU.is_equal, op1=ALU.mult,
                                                   accum_out=tm[:, j, TERMS - 1:TERMS]).then_inc(s_eq, 1)
                        dve.wait_ge(s_look, EC * k + t * U + 4 * q + 4)
                        v.tensor_tensor(tm[:, :, 2 * EP:2 * EP + P],
                                        bank[7 * q][0:EP, :].rearrange("p (c n) -> p c n", c=4),
                                        ohlo[0:EP, bass.ds(t * U + 4 * q, 4), :], ALU.mult).then_inc(s_eq, 1)
                        dve.wait_ge(s_eq, 5 * (2 * g + q + 1))
                        v.tensor_reduce(rank[0:EP, 4 * q:4 * q + 4], tm[:, :, 2 * EP:TERMS], X,
                                        ALU.add).then_inc(s_rank, 1)
                    dve.wait_ge(s_rank, 2 * g + 2)
                    v.tensor_copy(pos_i[0:EP, 0, :], rank[0:EP, :]).then_inc(s_d, 1)
                    dve.wait_ge(s_d, 3 * g + 1)
                    v.tensor_scalar(pos_i[0:EP, 1, :], pos_i[0:EP, 0, :], P - 1, None,
                                    ALU.bitwise_and).then_inc(s_d, 1)
                    v.tensor_scalar(pos_i[0:EP, 2, :], pos_i[0:EP, 0, :], SHIFT, None,
                                    ALU.logical_shift_right).then_inc(s_d, 1)
                    dve.wait_ge(s_d, 3 * g + 3)
                    if not first:
                        dve.wait_ge(s_scat[h], 16 * U * (groups // 2 * k + pair))
                    v.tensor_copy(leaving[0:EP, h, :, :], rec[0:EP, bass.ds(t * U, U), :]).then_inc(s_leave, 1)
                    v.scalar_tensor_tensor(out=place[0:EP, h, :], in0=pos_i[0:EP, 1, :], scalar=float(NC),
                                           in1=pos_i[0:EP, 2, :], op0=ALU.mult, op1=ALU.add).then_inc(s_pos, 1)
                ranks(0, 0, k == 0)
                ranks(0, 1, k == 0)
                with dve.Fori(1, groups // 2) as t:
                    ranks(t, 0, False)
                    ranks(t, 1, False)

            def los(k):
                dve.wait_ge(s_back, 32)
                ri = recs[k][:, 0:NC, :].bitcast(I32)
                q = 4 * k
                v.tensor_scalar(lo_si[:, :], ri[:, :, k], P - 1, None, ALU.bitwise_and).then_inc(s_lo, 1)
                dve.wait_ge(s_lo, q + 1)
                v.tensor_copy(lo_s[:, 0:NC], lo_si[:, :]).then_inc(s_lo, 1)
                dve.wait_ge(s_lo, q + 2)
                v.scalar_tensor_tensor(out=lo_s[:, 0:NC], in0=lo_s[:, 0:NC], scalar=1.0, in1=recs[k][:, 0:NC, 6],
                                       op0=ALU.add, op1=ALU.mult).then_inc(s_lo, 1)
                dve.wait_ge(s_lo, q + 3)
                v.tensor_scalar(lo_s[:, 0:NC], lo_s[:, 0:NC], -1.0, None, ALU.add).then_inc(s_lo, 1)
                dve.wait_ge(s_lo, q + 4)

            for q in s_scat:
                dve.wait_ge(q, 16 * EC)
            dve.wait_ge(s_tab, EC + 2)
            for k in range(2):
                v.memset(recs[k][:, NC:NC + U, :], 0.0).then_inc(s_lo7, 1)
            v.memset(x0[:, FULLW:NW, :], 0.0).then_inc(s_x0z, 1)
            v.memset(hcur[:, FULLW:NW, :], 0.0).then_inc(s_x0z, 1)
            los(0)

            def sum_chunks(k, t):
                row = win_late[0 if k < HOPS else 1]
                if isinstance(t, int):
                    ws = [None] * LAG + list(windows(mybir.EngineType.DVE, row, LAG, U - LAG))
                else:
                    ws = windows(mybir.EngineType.DVE, row, t * U, U)
                for j in range(U):
                    n = k * NC + t * U + j
                    c = t * U + j
                    cold = isinstance(t, int) and k == 0
                    m = n if k < HOPS else n + NC
                    if not (cold and j < 4):
                        dve.wait_ge(s_mm, n - 3)
                    if k < HOPS:
                        v.tensor_scalar(onehot[:, j % 4, :], iota_f[:, 0:P], lo_s[:, bass.ds(c, 1)],
                                        recs[0][:, bass.ds(c, 1), 2], ALU.is_equal, ALU.mult).then_inc(s_oneh, 1)
                    else:
                        v.tensor_scalar(onehot[:, j % 4, :], iota_f[:, 0:P], lo_s[:, bass.ds(c, 1)], None,
                                        ALU.is_equal).then_inc(s_oneh, 1)
                        dve.wait_ge(s_g[j], 16 * (turn(k) * (NC // U) + t + 1))
                        v.tensor_tensor(val[:, j % 4, 0:D].rearrange("p (h d) -> p h d", h=HEADS),
                                        gath[:, j, :].rearrange("p (h d) -> p h d", h=HEADS),
                                        s_sb[:, bass.ds(c, 1), :].rearrange("p c h -> p (c h)").unsqueeze(2)
                                        .broadcast_to([P, HEADS, HD]), ALU.mult).then_inc(s_val, 1)
                    if not (isinstance(t, int) and j < LAG):
                        add(k, n - LAG, (j - LAG) % U, ws[j])

            def add(k, n, j, w):
                wide = D if k < HOPS else HX
                b = bank[j % 4] if k < HOPS else bank[4 + j % 4]
                dve.wait_ge(s_mm, n + 1)
                dve.wait_ge(s_add, n) if not (isinstance(n, int) and n == 0) else None
                a = acc[:, bass.ds(w, 1), 0:wide].rearrange("p c d -> p (c d)")
                v.tensor_tensor(a, a, b[:, 0:wide], ALU.add).then_inc(s_add, 1)

            def dense(k, t, first):
                parts = 2 if k < HOPS else 1
                for s in range(2):
                    w = 2 * t + s
                    n = k * NW + w
                    if not first:
                        dve.wait_ge(s_stT, n - 1)
                    if k < HOPS:
                        v.tensor_copy(stg[:, s, 0:D], acc[:, bass.ds(w, 1), 0:D].rearrange("p c d -> p (c d)")
                                      ).then_inc(s_d, 1)
                        v.tensor_copy(stg[:, s, D:2 * D], hcur[:, bass.ds(w, 1), :].rearrange("p c d -> p (c d)")
                                      ).then_inc(s_stg, 1)
                    else:
                        v.tensor_copy(stg[:, s, 0:D], hcur[:, bass.ds(w, 1), :].rearrange("p c d -> p (c d)")
                                      ).then_inc(s_stg, 1)
                for s in range(2):
                    w = 2 * t + s
                    n = k * NW + w
                    h = hcur[:, bass.ds(w, 1), :].rearrange("p c d -> p (c d)")
                    y = bank[6 + s][:, 0:D]
                    xw = x0[:, bass.ds(w, 1), 0:D].rearrange("p c d -> p (c d)")
                    dve.wait_ge(s_lin, n + 1)
                    if k < HOPS - 1:
                        if not first:
                            dve.wait_ge(s_new, n - 1)
                        v.tensor_scalar(elu[:, s, D:2 * D], y, 0.0, None, ALU.min).then_inc(s_em, 1)
                    elif k == HOPS - 1:
                        v.tensor_tensor(h, xw, y, ALU.add).then_inc(s_new, 1)
                    else:
                        v.tensor_copy(xw, y).then_inc(s_new, 1)
                if k < HOPS - 1:
                    for s in range(2):
                        w = 2 * t + s
                        n = k * NW + w
                        dve.wait_ge(s_ea, 2 * n + 2)
                        v.scalar_tensor_tensor(out=hcur[:, bass.ds(w, 1), :].rearrange("p c d -> p (c d)"),
                                               in0=elu[:, s, D:2 * D], scalar=-1.0, in1=elu[:, s, 0:D],
                                               op0=ALU.add, op1=ALU.add).then_inc(s_new, 1)

            def layer_norm(q, r):
                sq = acc[:, :, 0:D]
                mean, var, root, inv = (stat[:, :, i] for i in range(4))
                v.tensor_reduce(mean, hcur[:, :, :], X, ALU.add).then_inc(s_ln, 1)
                dve.wait_ge(s_ln, q + 1)
                v.tensor_scalar(mean, mean, 1.0 / D, None, ALU.mult).then_inc(s_ln, 1)
                dve.wait_ge(s_ln, q + 2)
                mb = mean.unsqueeze(2).broadcast_to([P, NW, D])
                v.tensor_tensor(hcur[:, :, :], hcur[:, :, :], mb, ALU.subtract).then_inc(s_d, 1)
                dve.wait_ge(s_d, r + 1)
                v.tensor_tensor(sq, hcur[:, :, :], hcur[:, :, :], ALU.mult).then_inc(s_d, 1)
                dve.wait_ge(s_d, r + 2)
                v.tensor_reduce(var, sq, X, ALU.add).then_inc(s_ln, 1)
                dve.wait_ge(s_ln, q + 3)
                v.tensor_scalar(var, var, 1.0 / D, EPS, ALU.mult, ALU.add).then_inc(s_ln, 1)
                dve.wait_ge(s_sq, 1 if q == 0 else 2)
                v.reciprocal(inv, root).then_inc(s_ln, 1)
                dve.wait_ge(s_ln, q + 5)
                v.tensor_tensor(hcur[:, :, :], hcur[:, :, :], inv.unsqueeze(2).broadcast_to([P, NW, D]),
                                ALU.mult).then_inc(s_ln, 1)
                dve.wait_ge(s_ln, q + 6)

            dve.wait_ge(s_x, 64)
            for k in range(HOPS):
                v.memset(acc[:, :, :], 0.0).then_inc(s_clr, 1)
                dve.wait_ge(s_clr, k + 1)
                sum_chunks(k, 0)
                with dve.Fori(1, NC // U) as t:
                    sum_chunks(k, t)
                ws = windows(mybir.EngineType.DVE, win_late[0], NC, LAG)
                for n in range(LAG):
                    add(k, k * NC + NC - LAG + n, U - LAG + n, ws[n])
                dve.wait_ge(s_add, NC * (k + 1))
                if k:
                    dve.wait_ge(s_hst, 16 * k)
                dense(k, 0, k == 0)
                with dve.Fori(1, NW // 2) as t:
                    dense(k, t, False)
            dve.wait_ge(s_new, HOPS * NW)
            R = 3 * 2 * groups + HOPS * NW
            layer_norm(0, R)
            R += 2
            dense(HOPS, 0, False)
            with dve.Fori(1, NW // 2) as t:
                dense(HOPS, t, False)
            dve.wait_ge(s_new, (HOPS + 1) * NW)
            h4 = x0[:, :, 0:D]
            pr = acc[:, :, 0:D]
            for i, (a, o) in enumerate(((asrc_b, s_src[:, :, :]), (adst_b, x0[:, :, D:HX]))):
                for w in range(2):
                    half = slice(w * NW // 2, (w + 1) * NW // 2)
                    v.tensor_tensor(pr[:, half, :], h4[:, half, :],
                                    a[:, :].unsqueeze(1).broadcast_to([P, NW // 2, D]), ALU.mult).then_inc(s_d, 1)
                    R += 1
                    dve.wait_ge(s_d, R)
                    for ww in range(w * NW // 2, (w + 1) * NW // 2):
                        ins = v.tensor_reduce(o[:, ww, :], pr[:, ww, :].rearrange("p (h d) -> p h d", h=HEADS),
                                              X, ALU.add)
                    ins.then_inc(s_ln, 1)
                    dve.wait_ge(s_ln, LN_STEPS + 2 * i + w + 1)
            los(1)
            full = dot[:, 0:NC // 2, :].rearrange("p c (a f) -> p (c a) f", f=4)
            v.tensor_copy(full, recs[1][:, 0:NC, 3:7]).then_inc(s_split, 1)
            dve.wait_ge(s_split, 12)
            rb = recs[1][:, 0:NC, 2:8].bitcast(BF16)
            split(dve, [rb[:, :, 4 * i:4 * i + 4] for i in range(3)], full, s_split, 12)
            v.tensor_copy(lo_s[:, NC:NC + U], lo_s[:, NC - U:NC]).then_inc(s_lo7, 1)
            dve.wait_ge(s_lo7, 3)
            dve.wait_ge(s_hst, 16 * (HOPS + 1))
            split(dve, [h_parts[i][:, :, :] for i in range(3)], x0[:, :, :], s_split, 17)

            def score(t):
                for j in range(U):
                    n = t * U + j
                    cold = isinstance(t, int)
                    dve.wait_ge(s_lrow, n + 1)
                    if not (cold and j < 4):
                        dve.wait_ge(s_hd_, n - 3)
                    v.tensor_scalar(onehotb[:, j % 4, :], bank[2 + j % 2][:, 0:P // 2].bitcast(BF16), lane_f[:, 0:1], None,
                                    ALU.is_equal).then_inc(s_oneh, 1)
                    if not (cold and j < 2):
                        multiply(n - 2, (j - 2) % U)
                    if not (cold and j < 3):
                        take_dot(n - 3, (j - 3) % U)

            def multiply(n, j):
                dve.wait_ge(s_relu, n + 1)
                dve.wait_ge(s_sde, n + 1)
                v.tensor_tensor(prod[:, j % 4, :], encr[:, j % 4, :], bank[6 + j % 2][:, 0:D],
                                ALU.mult).then_inc(s_em, 1)

            def take_dot(n, j):
                dve.wait_ge(s_em, (HOPS - 1) * NW + n + 1)
                v.tensor_reduce(dot[:, bass.ds(n, 1), :].rearrange("p c h -> p (c h)"),
                                prod[:, j % 4, :].rearrange("p (h d) -> p h d", h=HEADS), X, ALU.add).then_inc(s_dot, 1)

            score(0)
            with dve.Fori(1, NC // U) as t:
                score(t)
            take_dot(NC - 3, (NC - 3) % U)
            for n in range(NC - 2, NC):
                multiply(n, n % U)
                take_dot(n, n % U)

            dve.wait_ge(s_dot, NC)
            dve.wait_ge(s_sde, NC)
            dve.wait_ge(s_ss, 2 * NC // U)
            al, do, sd = (z[:, :, :].rearrange("p c h -> p (c h)") for z in (s_sb, dot, sde))
            v.tensor_tensor(al, al, sd, ALU.add).then_inc(s_al, 1)
            dve.wait_ge(s_al, 1)
            v.tensor_tensor(al, al, do, ALU.add).then_inc(s_al, 1)
            dve.wait_ge(s_al, 2)
            v.scalar_tensor_tensor(out=al, in0=al, scalar=0.2, in1=al, op0=ALU.mult, op1=ALU.max).then_inc(s_al, 1)
            v.tensor_copy(lo_s[:, 0:NC], recs[1][:, 0:NC, :].bitcast(I32)[:, :, 1]).then_inc(s_lo, 1)
            dve.wait_ge(s_lo, 9)
            v.scalar_tensor_tensor(out=lo_si[:, :].bitcast(F32), in0=lo_s[:, 0:NC], scalar=1.0, in1=recs[1][:, 0:NC, 3:4].bitcast(BF16)[:, :, 1],
                                   op0=ALU.add, op1=ALU.mult).then_inc(s_lo, 1)
            dve.wait_ge(s_lo, 10)
            v.tensor_copy(sde[:, :, :], lo_si[:, :].bitcast(F32).unsqueeze(2).broadcast_to([P, NC, HEADS])).then_inc(s_al, 1)

            dve.wait_ge(s_alTs, 2 * NB)
            K = dotT
            v.memset(brk, 0.0).then_inc(s_lo, 1)
            dve.wait_ge(s_lo, 11)
            v.tensor_tensor(brk3[:, :, 1:P], K[:, :, 1:P], K[:, :, 0:P - 1], ALU.not_equal).then_inc(s_lo, 1)
            dve.wait_ge(s_lo, 12)
            v.tensor_scalar(brk, brk, -BIG, None, ALU.mult).then_inc(s_lo, 1)
            dve.wait_ge(s_lo, 13)
            for b in range(NB):
                ins = v.tensor_tensor_scan(sdeT[:, b, :], brk3[:, b, 0:P], alT[:, b, :], -BIG, ALU.add, ALU.max)
            ins.then_inc(s_lo, 1)
            dve.wait_ge(s_lo, 14)
            v.tensor_copy(ends[:, :, 0], sdeT[:, :, P - 1]).then_inc(s_lo, 1)
            v.tensor_copy(ends[:, :, 2], K[:, :, 0]).then_inc(s_lo, 1)
            v.tensor_copy(ends[:, :, 3], K[:, :, P - 1]).then_inc(s_lo, 1)
            dve.wait_ge(s_lo, 17)
            for b in range(NB):
                ins = v.tensor_tensor_scan(dotT[:, b, ::-1], brk3[:, b, 1:P + 1][:, ::-1], sdeT[:, b, ::-1], -BIG,
                                           ALU.add, ALU.max)
            ins.then_inc(s_al, 1)
            dve.wait_ge(s_al, 5)
            v.tensor_copy(ends[:, :, 1], dotT[:, :, 0]).then_inc(s_al, 1)
            dve.wait_ge(s_end, 32)
            for i in range(4):
                ins = v.tensor_copy(el[:, i, :].rearrange("h (b c) -> h c b", c=16), eh[:, :, :, i])
            ins.then_inc(s_al, 1)
            dve.wait_ge(s_al, 7)
            last, firstm, k0, k1, cont, sing, p_, o_ = (el[:, i, :] for i in range(8))
            v.memset(cont, 1.0).then_inc(s_al, 1)
            dve.wait_ge(s_al, 8)
            v.tensor_tensor(cont[:, 1:NC], k0[:, 1:NC], k1[:, 0:NC - 1], ALU.not_equal).then_inc(s_al, 1)
            v.tensor_tensor(sing, k0, k1, ALU.not_equal).then_inc(s_al, 1)
            dve.wait_ge(s_al, 10)
            v.tensor_tensor(p_, cont, sing, ALU.max).then_inc(s_al, 1)
            dve.wait_ge(s_al, 11)
            v.tensor_scalar(p_, p_, -BIG, None, ALU.mult).then_inc(s_al, 1)
            dve.wait_ge(s_al, 12)
            v.tensor_tensor_scan(o_, p_, last, -BIG, ALU.add, ALU.max).then_inc(s_al, 1)
            v.memset(k0, 1.0).then_inc(s_al, 1)
            dve.wait_ge(s_al, 14)
            v.tensor_copy(k0[:, 0:NC - 1], cont[:, 1:NC]).then_inc(s_al, 1)
            dve.wait_ge(s_al, 15)
            v.tensor_tensor(k1, k0, sing, ALU.max).then_inc(s_x0z, 1)
            dve.wait_ge(s_x0z, 3)
            v.tensor_scalar(k1, k1, -BIG, None, ALU.mult).then_inc(s_x0z, 1)
            dve.wait_ge(s_x0z, 4)
            v.tensor_tensor_scan(sing[:, ::-1], k1[:, ::-1], firstm[:, ::-1], -BIG, ALU.add, ALU.max).then_inc(s_x0z, 1)
            v.tensor_scalar(cont, cont, -BIG, None, ALU.mult).then_inc(s_x0z, 1)
            v.tensor_scalar(k0, k0, -BIG, None, ALU.mult).then_inc(s_x0z, 1)
            v.memset(last, 0.0).then_inc(s_x0z, 1)
            dve.wait_ge(s_x0z, 8)
            v.tensor_tensor(last[:, 1:NC], cont[:, 1:NC], o_[:, 0:NC - 1], ALU.add).then_inc(s_x0z, 1)
            v.tensor_scalar(last[:, 0:1], cont[:, 0:1], 1.0, None, ALU.mult).then_inc(s_x0z, 1)
            v.tensor_tensor(p_[:, 0:NC - 1], k0[:, 0:NC - 1], sing[:, 1:NC], ALU.add).then_inc(s_x0z, 1)
            v.tensor_scalar(p_[:, NC - 1:NC], k0[:, NC - 1:NC], 1.0, None, ALU.mult).then_inc(s_x0z, 1)
            dve.wait_ge(s_x0z, 12)
            v.tensor_copy(eo[:, :, :, 0], last.rearrange("h (b c) -> h c b", c=16)).then_inc(s_al, 1)
            v.tensor_copy(eo[:, :, :, 1], p_.rearrange("h (b c) -> h c b", c=16)).then_inc(s_al, 1)
            dve.wait_ge(s_end, 16 * (3 + 16))
            for b in range(NB):
                ins = v.tensor_tensor_scan(sdeT[:, b, :], brk3[:, b, 0:P], alT[:, b, :], cin[:, b, 0:1],
                                           ALU.add, ALU.max)
            ins.then_inc(s_lo, 1)
            dve.wait_ge(s_lo, 18)
            for b in range(NB):
                ins = v.tensor_tensor_scan(dotT[:, b, ::-1], brk3[:, b, 1:P + 1][:, ::-1], sdeT[:, b, ::-1],
                                           cin[:, b, 1:2], ALU.add, ALU.max)
            ins.then_inc(s_lo, 1)
            dve.wait_ge(s_lo, 19)
            for b in range(NB):
                v.tensor_tensor(alT[:, b, :], alT[:, b, :], dotT[:, b, :], ALU.subtract).then_inc(s_mx, 1)

            v.tensor_scalar(lo_si[:, :], recs[1][:, 0:NC, :].bitcast(I32)[:, :, 1], P - 1, None,
                            ALU.bitwise_and).then_inc(s_lo, 1)
            dve.wait_ge(s_lo, 20)
            v.tensor_copy(lo_s[:, 0:NC], lo_si[:, :]).then_inc(s_lo, 1)
            dve.wait_ge(s_lo, 21)
            v.scalar_tensor_tensor(out=lo_s[:, 0:NC], in0=lo_s[:, 0:NC], scalar=1.0, in1=recs[1][:, 0:NC, 3:4].bitcast(BF16)[:, :, 1],
                                   op0=ALU.add, op1=ALU.mult).then_inc(s_lo, 1)
            dve.wait_ge(s_lo, 22)
            v.tensor_scalar(lo_s[:, 0:NC], lo_s[:, 0:NC], -1.0, None, ALU.add).then_inc(s_lo, 1)
            dve.wait_ge(s_lo, 23)
            v.memset(acc[:, :, :], 0.0).then_inc(s_clr, 1)
            dve.wait_ge(s_clr, HOPS + 1)
            dve.wait_ge(s_exs, NB)
            sum_chunks(HOPS, 0)
            with dve.Fori(1, NC // U) as t:
                sum_chunks(HOPS, t)
            ws = windows(mybir.EngineType.DVE, win_late[1], NC, LAG)
            for n in range(LAG):
                add(HOPS, HOPS * NC + NC - LAG + n, U - LAG + n, ws[n])
            dve.wait_ge(s_add, NC * (HOPS + 1))
            q = LN_STEPS + 4
            v.tensor_scalar(x0[:, :, D:HX], acc[:, :, D:HX], 1e-10, None, ALU.max).then_inc(s_ln, 1)
            dve.wait_ge(s_ln, q + 1)
            v.reciprocal(s_src[:, :, :], x0[:, :, D:HX]).then_inc(s_ln, 1)
            dve.wait_ge(s_ln, q + 2)
            for w in range(NW):
                ins = v.tensor_tensor(acc[:, w, 0:D].rearrange("p (h d) -> p h d", h=HEADS),
                                      acc[:, w, 0:D].rearrange("p (h d) -> p h d", h=HEADS),
                                      s_src[:, w, :].unsqueeze(2).broadcast_to([P, HEADS, HD]), ALU.mult)
            ins.then_inc(s_d, 1)
            R += 1
            dve.wait_ge(s_d, R)
            v.tensor_tensor(acc[:, :, 0:D], acc[:, :, 0:D], bias_b[:, :].unsqueeze(1).broadcast_to([P, NW, D]),
                            ALU.add).then_inc(s_d, 1)
            R += 1
            dve.wait_ge(s_d, R)
            v.tensor_tensor(hcur[:, :, :], hcur[:, :, :], acc[:, :, 0:D], ALU.add).then_inc(s_d, 1)
            R += 1
            dve.wait_ge(s_d, R)
            layer_norm(q + 2, R)


_INS = ['x', 'src', 'dst', 'edge_attr_3', 'edge_weight', 'L0_gnn_Wn', 'L0_gnn_bn', 'L0_gnn_Ws', 'L0_gnn_bs',
        'L1_gnn_W', 'L1_gnn_a_src', 'L1_gnn_a_dst', 'L1_gnn_edge_W', 'L1_gnn_edge_b', 'L1_gnn_bias']


def kernel(**inputs):
    import concourse.bacc as bacc
    from concourse.bass_utils import run_bass_kernel_spmd

    nc = bacc.Bacc("TRN2", target_bir_lowering=False, num_devices=1)
    arrays, args = {}, []
    for name in _INS:
        a = np.ascontiguousarray(inputs[name])
        arrays[f"in_{name}"] = a
        args.append(nc.dram_tensor(f"in_{name}", a.shape, mybir.dt.from_np(a.dtype), kind="ExternalInput").ap())
    out = nc.dram_tensor("out_0", (N, D), F32, kind="ExternalOutput").ap()
    build(nc, *args, out)
    r = run_bass_kernel_spmd(nc, [arrays], core_ids=[0])
    return r.results[0]["out_0"]
```

```python
from contextlib import ExitStack

import numpy as np
import concourse.bass as bass
from concourse import mybir

F32 = mybir.dt.float32
BF16 = mybir.dt.bfloat16
I32 = mybir.dt.int32
ALU = mybir.AluOpType
ACT = mybir.ActivationFunctionType
X = mybir.AxisListType.X

P = 128
SHIFT = 7
N = 3125
D = 256
E = 50000
HOPS = 3
HEADS = 8
HD = D // HEADS
EF = 3
NW = 26
HI = 32
USED = (N + P - 1) // P
EP = 125
EC = E // EP
U = 8
NC = 416
assert EP * EC == E and EC % U == 0 and NC % 16 == 0 and NC % U == 0 and NW % 2 == 0
assert NC >= (E + USED * (P - 1)) // P and NW * P >= N
REC = 8
HX = D + HEADS
NB = NC // 16
LAG = 2
BIG = 1.0e38
EPS = 1e-5


def build(nc, x, src, dst, edge_attr, edge_weight, Wn, bn, Ws, bs, W, a_src, a_dst, edge_W, edge_b, bias, out):
    with ExitStack() as ctx:
        def sb(name, shape, dt=F32, where=ctx):
            return where.enter_context(nc.sbuf_tensor(name, shape, dt))

        def sem(name):
            return ctx.enter_context(nc.semaphore(name))

        def dram(name, shape):
            return nc.dram_tensor(name, shape, F32, kind="Internal").ap()

        rows_dram = [dram("rows_by_src", [P * NC, REC]), dram("rows_by_dst", [P * NC, REC])]
        h_dram = [dram("h_even", [NW * P, D]), dram("h_odd", [NW * P, D])]
        hh_dram = dram("gat_h", [NW * P, D])
        ss_dram = dram("gat_s_src", [NW * P, HEADS])
        edge_dram = dram("chunk_ends", [P, NB * 4])
        carry_dram = dram("chunk_carries", [P, NB * 2])

        identf = sb("identf", [P, P])
        identb = sb("identb", [P, P], BF16)
        tri = sb("tri", [P, P])
        triu = sb("triu", [P, P])
        ones = sb("ones", [P, P])
        iota_f = sb("iota_f", [P, NC])
        iota_b = sb("iota_b", [P, P], BF16)
        lane_i = sb("lane_i", [P, 1], I32)
        lane_f = sb("lane_f", [P, 1])
        win_late = [sb(f"win_{key}_late", [1, NC + U], I32) for key in ("src", "dst")]
        win_next = sb("win_dst_next", [1, NC + U], I32)
        wT = sb("wT", [P, 2 * HOPS, 2, D])
        w1T = sb("w1T", [P, 2, D + 2 * HEADS])
        bias6 = sb("bias6", [6, HOPS, D], BF16)
        ew36 = sb("ew36", [36, D], BF16)
        onesb = sb("onesb", [6, P], BF16)
        bias_b = sb("bias_b", [P, D])

        sort = ExitStack()
        src_i = sb("src_i", [P, EC], I32, sort)
        dst_i = sb("dst_i", [P, EC], I32, sort)
        loads = sb("loads", [P, EC * (1 + EF)], F32, sort)
        w_in = loads[:, 0:EC]
        ea_in = loads[:, EC:].rearrange("p (c k) -> p c k", k=EF)
        TERMS = 2 * EP + P + 1
        assert 4 * TERMS <= EC * (1 + EF)
        terms = loads[:, 0:4 * TERMS].rearrange("p (c n) -> p c n", c=4)
        rec = sb("rec", [P, EC, REC], F32, sort)
        key_f = sb("key_f", [P, EC + U], F32, sort)
        earlier = sb("earlier", [P, 2 * EP], F32, sort)
        kst = sb("kst", [P, U], F32, sort)
        lo_i = sb("lo_i", [P, EC], I32, sort)
        lo_f = sb("lo_f", [P, EC], F32, sort)
        hi_f = sb("hi_f", [P, EC], F32, sort)
        ohlo = sb("ohlo", [P, EC, P], BF16, sort)
        early = ohlo[:, EC // 2:, :].rearrange("p c n -> p (c n)")
        BW = HOPS * D
        bias2 = early[0:2, 0:2 * BW].bitcast(F32).rearrange("p (k o) -> p k o", k=HOPS)
        b_parts = early[0:2, 2 * BW:5 * BW].rearrange("p (a k o) -> p a k o", a=3, k=HOPS)
        ew4 = early[0:4, 5 * BW:5 * BW + 2 * D].bitcast(F32)
        ew_parts = early[0:4, 5 * BW + 2 * D:5 * BW + 5 * D].rearrange("p (a o) -> p a o", a=3)
        iota_i = early[:, 5 * BW + 5 * D:5 * BW + 5 * D + 2 * NC].bitcast(I32)
        ohhi = sb("ohhi", [P, EC, HI], BF16, sort)
        ohhiT = sb("ohhiT", [HI, U, EP], F32, sort)
        blocks = sb("blocks", [P, P], F32, sort)
        fold = sb("fold", [P, HI], F32, sort)
        hist = sb("hist", [HI, P], F32, sort)
        table0 = sb("table0", [HI, P], F32, sort)
        table = sb("table", [HI, 2, P], F32, sort)
        small = sb("small", [HI, 8], F32, sort)
        small_i = sb("small_i", [HI, 2], I32, sort)
        started = sb("started", [HI, NC], F32, sort)
        rank = sb("rank", [P, U], F32, sort)
        pos_i = sb("pos_i", [P, 3, U], I32, sort)
        leaving = sb("leaving", [P, 2, U, REC], F32, sort)
        place = sb("place", [P, 2, U], I32, sort)
        wraw = sb("wraw", [P, 2, D], F32, sort)
        a_cols = sb("a_cols", [P, 2, 2], F32, sort)
        headmask = sb("headmask", [P, P // HD], F32, sort)
        a_blocks = sb("a_blocks", [P, 2, 2 * HEADS], F32, sort)
        sort.close()

        recs = [sb("recs_src", [P, NC + 2 * U, REC]), sb("recs_dst", [P, NC + U, REC])]
        fst = sb("fst", [P, U, 40], BF16)
        lo_s = sb("lo_s", [P, NC + U])
        lo_si = sb("lo_si", [P, NC], I32)
        acc = sb("acc", [P, NW, HX])
        hcur = sb("hcur", [P, NW, D])
        x0 = sb("x0", [P, NW, HX])
        stg = sb("stg", [P, 2, 2 * D])
        stgT = sb("stgT", [P, 2, 2 * D])
        elu = sb("elu", [P, 2, 2 * D])
        gath = sb("gath", [P, U, D])
        idx = sb("idx", [P, U], I32)
        onehot = sb("onehot", [P, 4, P])
        val = sb("val", [P, 4, HX])
        parts12 = acc[:, :, :].rearrange("p w d -> p (w d)").bitcast(BF16)
        h_parts = [parts12[:, i * NW * HX:(i + 1) * NW * HX].rearrange("p (w d) -> p w d", w=NW) for i in range(2)]
        h_parts.append(recs[0][:, :, :].rearrange("p c k -> p (c k)").bitcast(BF16)[:, 0:NW * HX]
                       .rearrange("p (w d) -> p w d", w=NW))
        encr = elu[:, :, :].rearrange("p a (s d) -> p (a s) d", s=2)
        prod = stg[:, :, :].rearrange("p a (s d) -> p (a s) d", s=2)
        eaT = stgT[0:36, :, :].rearrange("p s d -> p (s d)").bitcast(BF16)[:, 0:8 * P].rearrange("p (s d) -> p s d", s=2)
        onehotb = sb("onehotb", [P, 4, P], BF16)
        stat = sb("stat", [P, NW, 4])
        s_sb = sb("s_sb", [P, NC, HEADS])
        dot = sb("dot", [P, NC, HEADS])
        sde = sb("sde", [P, NC, HEADS])
        alT = recs[0][:, 0:NC, :].rearrange("p (b c) k -> p b (c k)", b=NB)
        ends = sb("ends", [P, NB, 4])
        brk = acc[:, :, :].rearrange("p w d -> p (w d)")[:, 0:NB * (P + 1)]
        x0f = x0[:, :, :].rearrange("p w d -> p (w d)")
        el = x0f[0:HEADS, 0:8 * NC].rearrange("h (k c) -> h k c", k=8)
        eh = x0f[0:HEADS, 8 * NC:12 * NC].rearrange("h (c b k) -> h c b k", c=16, k=4)
        eo = x0f[0:HEADS, 12 * NC:14 * NC].rearrange("h (c b k) -> h c b k", c=16, k=2)
        cin = sb("cin", [P, NB, 2])
        s_src = sb("s_src", [P, NW, HEADS])

        bank = [ctx.enter_context(nc.psum_tensor(f"bank{i}", [P, 512], F32)) for i in range(8)]

        s_const = sem("consts_made")
        s_lane = sem("iota_made")
        s_in = sem("edges_loaded")
        s_w = sem("weight_block_loaded")
        s_wT_pe = sem("weight_transposed")
        s_wT = sem("weight_stored")
        s_small = sem("small_weights_loaded")
        s_rec = sem("records_built")
        s_fill = sem("rows_prefilled")
        s_keys = sem("keys_split")
        s_oh = sem("onehots_built")
        s_hist = sem("histogram_done")
        s_part = sem("histogram_blocks_copied")
        s_sum = sem("histogram_blocks_summed")
        s_d = sem("vector_step")
        s_hd = sem("histogram_step")
        s_cum = sem("window_starts_summed")
        s_base = sem("base_table_made")
        s_win = sem("windows_counted")
        s_seed = sem("table_seeded")
        s_hiT = sem("window_onehot_transposed")
        s_hiTs = sem("window_onehot_stored")
        s_row = sem("keys_broadcast")
        s_tab = sem("table_copied")
        s_look = sem("table_read")
        s_upd = sem("table_updated")
        s_rank = sem("ranks_taken")
        s_eq = sem("rank_terms_ready")
        s_pos = sem("positions_ready")
        s_scat = [sem("records_scattered_even"), sem("records_scattered_odd")]
        s_leave = sem("records_leaving")
        s_idx = sem("indices_staged")
        s_back = [sem("records_by_src_read_back"), sem("records_by_dst_read_back")]
        s_lo = sem("los_ready")
        s_x = sem("x_loaded")
        s_lo7 = sem("lo_in_records")
        s_split = sem("parts_split")
        s_blk = sem("a_blocks_made")
        s_bn = sem("window_statistics")
        s_nrm = sem("window_normalised")
        s_p0 = sem("h_part_0_made")
        s_kept = sem("h_kept")
        s_p1 = sem("h_part_1_made")
        s_r1 = sem("h_rest_of_part_0_made")
        s_r2 = sem("h_rest_of_part_1_made")
        s_p2 = sem("h_part_2_made")
        s_bias = sem("bias_added")
        s_div = sem("window_divided")
        s_res = sem("residual_added")
        s_fin = sem("output_window_done")
        s_kst = sem("keys_staged")
        s_fst = sem("records_staged")
        s_fsl = sem("lo_staged")
        s_x0z = sem("x_tail_cleared")
        s_clr = sem("acc_cleared")
        s_g = [sem(f"rows_gathered{i}") for i in range(U)]
        s_oneh = sem("onehot_made")
        s_mm = sem("chunk_summed")
        s_add = sem("chunk_added")
        s_ostg = sem("own_staged")
        s_oT = sem("own_transposed")
        s_oTs = sem("own_transpose_stored")
        s_oL = sem("own_multiplied")
        s_own = sem("own_stored")
        s_z = sem("window_summed")
        s_stg = sem("window_staged")
        s_stT = sem("window_transposed")
        s_stTs = sem("window_transpose_stored")
        s_lin = sem("window_multiplied")
        s_ea = sem("elu_parts")
        s_em = sem("elu_exp_less_1")
        s_new = sem("window_done")
        s_hst = sem("h_stored")
        s_ln = sem("layer_norm_step")
        s_sq = sem("layer_norm_root")
        s_ss = sem("s_gathered")
        s_eaT = sem("features_transposed")
        s_eaTs = sem("features_stored")
        s_lrow = sem("lo_broadcast")
        s_enc = sem("edge_encoded")
        s_relu = sem("encoding_clipped")
        s_hd_ = sem("h_dst_looked_up")
        s_sde = sem("s_dst_copied")
        s_dot = sem("dot_taken")
        s_al = sem("alpha_step")
        s_alT = sem("alpha_transposed")
        s_alTs = sem("alpha_transpose_stored")
        s_end = sem("chunk_ends_moved")
        s_mx = sem("max_ready")
        s_ex = sem("exp_done")
        s_exT = sem("exp_transposed")
        s_exs = sem("exp_stored")
        s_val = sem("values_scaled")
        s_vx = sem("exp_column_copied")
        s_out = sem("out_stored")

        def nodes(t, cols=None):
            return t.rearrange("(w p) d -> p w d", p=P)

        def windows(engine, row, c, n):
            return nc.values_load_multi_w_load_instructions(
                row[0:1, bass.ds(c, n)], engines=(engine,), min_val=0, max_val=NW - 1,
                skip_runtime_bounds_check_because="a count of the USED windows, less one")[1]

        groups = EC // U

        def split(eng, parts, full, sem_, q):
            for i in range(3):
                nc.vector.tensor_copy(parts[i], full).then_inc(sem_, 1)
                eng.wait_ge(sem_, q + 2 * i + 1)
                if i < 2:
                    nc.vector.tensor_tensor(full, full, parts[i], ALU.subtract).then_inc(sem_, 1)
                    eng.wait_ge(sem_, q + 2 * i + 2)

        def turn(k):
            return k if k < HOPS else k + 1
        FULLW = N // P
        assert FULLW % 8 == 0 and FULLW * P < N

        zero_tile = ohlo[:, 0:NC * REC * 2 // P, :].bitcast(F32).rearrange("p a b -> p (a b)")

        STORED = 16 * NW // 2
        LN_STEPS = 3
        quads = [(b, min(4, NB - b)) for b in range(0, NB, 4)]
        AL_ENDS = 6
        AL_CARRY = 17
        dotT = dot[:, :, :].rearrange("p (b c) h -> p b (c h)", b=NB)
        sdeT = sde[:, :, :].rearrange("p (b c) h -> p b (c h)", b=NB)
        brk3 = brk.rearrange("p (b e) -> p b e", b=NB)

        block = ctx.enter_context(nc.Block())

        @block.sync
        def _(sp):
            sp.dma_start(src_i[0:EP, :], src.rearrange("(p c) -> p c", c=EC)).then_inc(s_in, 16)
            sp.dma_start(dst_i[0:EP, :], dst.rearrange("(p c) -> p c", c=EC)).then_inc(s_in, 16)
            sp.dma_start(w_in[0:EP, :], edge_weight.rearrange("(p c) -> p c", c=EC)).then_inc(s_in, 16)
            sp.dma_start(ea_in[0:EP, :, :], edge_attr.rearrange("(p c) k -> p c k", c=EC)).then_inc(s_in, 16)
            for k in range(HOPS):
                sp.dma_start(bias2[0:1, k, :], bn[k:k + 1, :]).then_inc(s_small, 16)
                sp.dma_start(bias2[1:2, k, :], bs[k:k + 1, :]).then_inc(s_small, 16)
            with nc.allow_non_contiguous_dma(reason="three short columns"):
                sp.dma_start(ew4[0:EF, :], edge_W.rearrange("o k -> k o")).then_inc(s_small, 16)
            sp.dma_start(ew4[EF:EF + 1, :], edge_b.rearrange("(a o) -> a o", a=1)).then_inc(s_small, 16)
            with nc.allow_non_contiguous_dma(reason="two short columns"):
                for i, v in enumerate((a_dst, a_src)):
                    sp.dma_start(a_cols[:, i, :], v.rearrange("(a h) d -> (h d) a", a=2)).then_inc(s_small, 16)
            sp.dma_start(bias_b[:, :], bias.rearrange("(a o) -> a o", a=1).broadcast_to([P, D])).then_inc(s_small, 16)
            def load_matrix(m):
                if m >= 1:
                    sp.wait_ge(s_wT_pe, m)
                mat = W if m == 2 * HOPS else (Wn, Ws)[m % 2][m // 2]
                sp.dma_start(wraw[:, :, :], mat.rearrange("(a p) k -> p a k", p=P)).then_inc(s_w, 16)
            EARLY = 4
            for m in range(EARLY):
                load_matrix(m)
            sp.wait_ge(s_fill, 1)
            for r in rows_dram:
                sp.dma_start(r.rearrange("(p c) k -> p (c k)", p=P), zero_tile).then_inc(s_fill, 16)
            sp.wait_ge(s_split, 6)
            for a in range(3):
                sp.dma_start(bias6[2 * a:2 * a + 2, :, :], b_parts[:, a, :, :]).then_inc(s_small, 16)
            sp.wait_ge(s_split, 11)
            for a in range(3):
                for b in range(3):
                    r0 = 4 * (3 * a + b)
                    sp.dma_start(ew36[r0:r0 + 4, :], ew_parts[:, b, :]).then_inc(s_small, 16)
            for m in range(EARLY, 2 * HOPS + 1):
                load_matrix(m)

            for q in s_scat:
                sp.wait_ge(q, 16 * EC)
            sp.wait_ge(s_tab, EC + 2)
            for k in range(2):
                sp.dma_start(recs[k][:, 0:NC, :], rows_dram[k].rearrange("(p c) k -> p c k", p=P)).then_inc(s_back[k], 16)
            sp.wait_ge(s_x0z, 2)
            for i, t in enumerate((hcur, x0)):
                loaded = 16 * (FULLW + 1) * i
                if i:
                    sp.wait_ge(s_x, loaded)
                sp.dma_start(t[0:N - FULLW * P, FULLW, 0:D], x[FULLW * P:N, :]).then_inc(s_x, 16)
                with sp.Fori(0, FULLW) as w:
                    sp.wait_ge(s_x, loaded + 16 * (w + 1))
                    sp.dma_start(t[:, bass.ds(w, 1), 0:D], nodes(x[0:FULLW * P, :])[:, bass.ds(w, 1), :]).then_inc(s_x, 16)
            for k in range(HOPS - 1):
                with sp.Fori(0, NW // 2) as t:
                    sp.wait_ge(s_new, NW * k + 2 * t + 2)
                    sp.dma_start(nodes(h_dram[k])[:, bass.ds(2 * t, 2), :],
                                 hcur[:, bass.ds(2 * t, 2), :]).then_inc(s_hst, 16)
            with sp.Fori(0, NW // 2) as t:
                sp.wait_ge(s_kept, 2 * t + 2)
                sp.dma_start(nodes(hh_dram)[:, bass.ds(2 * t, 2), :],
                             x0[:, bass.ds(2 * t, 2), 0:D]).then_inc(s_hst, 16)
            sp.wait_ge(s_kept, NW)
            sp.dma_start(nodes(ss_dram), s_src[:, :, :]).then_inc(s_hst, 16)
            sp.wait_ge(s_al, AL_ENDS)
            sp.dma_start(edge_dram, ends[:, :, :].rearrange("p b k -> p (b k)")).then_inc(s_end, 16)
            sp.wait_ge(s_end, 16)
            sp.dma_start(eh[:, :, :, :].rearrange("h c b k -> h c (b k)"),
                         edge_dram.rearrange("(c h) k -> h c k", h=HEADS)).then_inc(s_end, 16)
            sp.wait_ge(s_al, AL_CARRY)
            sp.dma_start(carry_dram.rearrange("(c h) x -> h c x", h=HEADS),
                         eo[:, :, :, :].rearrange("h c b k -> h c (b k)")).then_inc(s_end, 16)
            sp.wait_ge(s_end, 48)
            sp.dma_start(cin[:, :, :].rearrange("p b k -> p (b k)"), carry_dram).then_inc(s_end, 16)
            for i in range(FULLW // 8):
                sp.wait_ge(s_fin, 8 * i + 8)
                sp.dma_start(out[8 * i * P:(8 * i + 8) * P, :].rearrange("(w p) d -> p w d", p=P),
                             hcur[:, 8 * i:8 * i + 8, :]).then_inc(s_out, 16)
            sp.wait_ge(s_fin, FULLW + 1)
            sp.dma_start(out[FULLW * P:N, :], hcur[0:N - FULLW * P, FULLW, :]).then_inc(s_out, 16)
            sp.wait_ge(s_out, 16 * (FULLW // 8 + 1))

        @block.gpsimd
        def _(pool):
            pool.memset(identf[:, :], 0.0).then_inc(s_lane, 1)
            pool.memset(ones[:, :], 1.0).then_inc(s_lane, 1)
            pool.iota(iota_i[:, :], [[1, NC]], base=0, channel_multiplier=0).then_inc(s_lane, 1)
            pool.iota(lane_i[:, :], [[1, 1]], base=0, channel_multiplier=1).then_inc(s_lane, 1)
            pool.wait_ge(s_lane, 4)
            pool.affine_select(out=identf[:, :], in_=identf[:, :], compare_op=ALU.not_equal, fill=1.0, base=0,
                               pattern=[[-1, P]], channel_multiplier=1).then_inc(s_lane, 1)
            pool.affine_select(out=tri[:, :], in_=ones[:, :], compare_op=ALU.is_gt, fill=0.0, base=0,
                               pattern=[[-1, P]], channel_multiplier=1).then_inc(s_lane, 1)
            pool.affine_select(out=triu[:, :], in_=ones[:, :], compare_op=ALU.is_gt, fill=0.0, base=0,
                               pattern=[[1, P]], channel_multiplier=-1).then_inc(s_lane, 1)
            pool.wait_ge(s_fill, 1 + 32)
            pool.wait_ge(s_rec, 6)
            for k in range(2):
                with pool.Fori(0, groups // 2) as t:
                    for h in range(2):
                        g = 2 * t + h
                        pool.wait_ge(s_leave, g + groups * k + 1)
                        pool.wait_ge(s_pos, g + groups * k + 1)
                        pool.nop(nofuse=True)
                        for j in range(U):
                            pool.indirect_dma_start(
                                out=rows_dram[k],
                                in_=leaving[0:EP, h, j, :],
                                out_offset=bass.IndirectOffsetOnAxis(ap=place[0:EP, h, j:j + 1], axis=0),
                                in_offset=None).then_inc(s_scat[h], 16)

            def gather(p, t, table, ring, first):
                for j in range(U):
                    if ring is not None and not first:
                        pool.wait_ge(s_mm, ring * NC + (t - 1) * U + j + 1)
                        pool.nop(nofuse=True)
                    if j % 4 == 0:
                        pool.wait_ge(s_idx, p * (2 * NC // U + 2) + 2 * t + j // 4 + 1)
                        pool.nop(nofuse=True)
                    o = gath[:, j, :] if ring is not None else gath[:, j, 0:HEADS]
                    pool.indirect_dma_start(
                        out=o, out_offset=None, in_=table,
                        in_offset=bass.IndirectOffsetOnAxis(ap=idx[:, j:j + 1], axis=0)).then_inc(s_g[j], 16)

            for k in range(HOPS):
                if k >= 1:
                    pool.wait_ge(s_hst, STORED * k)
                gather(k, 0, x if k == 0 else h_dram[k - 1], k, k == 0)
                with pool.Fori(1, NC // U) as t:
                    gather(k, t, x if k == 0 else h_dram[k - 1], k, False)
            def part_2(w, s):
                pool.wait_ge(s_r2, w + 1)
                pool.nop(nofuse=True)
                nc.gpsimd.tensor_copy(h_parts[2][:, bass.ds(w, 1), :].rearrange("p c d -> p (c d)"),
                                      elu[:, s, 0:HX]).then_inc(s_p2, 1)
            with pool.Fori(0, NW // 2) as t:
                part_2(2 * t, 0)
                part_2(2 * t + 1, 1)
            pool.wait_ge(s_hst, STORED * HOPS + 16)
            pool.nop(nofuse=True)
            with pool.Fori(0, NC // U) as t:
                gather(HOPS, t, ss_dram, None, False)
            pool.wait_ge(s_stg, (HOPS + 1) * NW)
            nc.gpsimd.tensor_tensor(hcur[:, :, :], hcur[:, :, :], bias_b[:, :].unsqueeze(1).broadcast_to([P, NW, D]),
                                    ALU.add).then_inc(s_bias, 1)
            gather(HOPS + 1, 0, hh_dram, HOPS, False)
            pool.wait_ge(s_lo, 19)
            nc.gpsimd.memset(acc[:, :, :], 0.0).then_inc(s_clr, 1)
            with pool.Fori(1, NC // U) as t:
                gather(HOPS + 1, t, hh_dram, HOPS, False)
            with pool.Fori(0, NW) as w:
                h = hcur[:, bass.ds(w, 1), :].rearrange("p c d -> p (c d)")
                pool.wait_ge(s_div, w + 1)
                pool.nop(nofuse=True)
                nc.gpsimd.tensor_tensor(h, h, acc[:, bass.ds(w, 1), 0:D].rearrange("p c d -> p (c d)"),
                                        ALU.add).then_inc(s_res, 1)

        @block.tensor
        def _(pe):
            pe.wait_ge(s_const, 4)
            for m in range(2 * HOPS + 1):
                pe.wait_ge(s_w, 16 * (m + 1))
                if m >= 2:
                    pe.wait_ge(s_wT, m - 1)
                for a in range(2):
                    for b in range(2):
                        i = pe.transpose(bank[m % 2][:, b * D + a * P:b * D + (a + 1) * P],
                                         wraw[:, a, b * P:(b + 1) * P], identf[:, :])
                if m == 2 * HOPS:
                    pe.wait_ge(s_blk, 6)
                    for b in range(2):
                        for a in range(2):
                            i = pe.matmul(bank[2][:, 2 * HEADS * b:2 * HEADS * (b + 1)], wraw[:, a, b * P:(b + 1) * P],
                                          a_blocks[:, a, :], start=a == 0, stop=a == 1)
                i.then_inc(s_wT_pe, 1)

            def count(k, t, start=False, stop=False, parts=(0, 4)):
                pe.wait_ge(s_oh, k * groups + t + 2)
                for j in parts:
                    i = pe.matmul(bank[k][:, :], ohhi[0:EP, bass.ds(t * U + j, 4), :].rearrange("p c k -> p (c k)"),
                                  ohlo[0:EP, bass.ds(t * U + j, 4), :].rearrange("p c k -> p (c k)"),
                                  start=start and j == 0, stop=stop and j == U - 4, skip_group_check=True)
                return i

            pe.wait_ge(s_wT, 2 * HOPS + 2)
            count(0, 0, True)
            with pe.Fori(1, groups - 1) as t:
                count(0, t)
            count(0, groups - 1, stop=True).then_inc(s_hist, 1)
            for k in range(2):
                if k:
                    count(1, groups - 2)
                    count(1, groups - 1, stop=True).then_inc(s_hist, 1)
                    pe.wait_ge(s_rank, 2 * groups)
                totals = bank[1 - k]
                pe.wait_ge(s_part, 4 * k + 4)
                pe.matmul(totals[0:HI, 0:P], fold[:, :], blocks[:, :], start=True, stop=True).then_inc(s_sum, 1)
                pe.wait_ge(s_hd, 10 * k + 4)
                pe.matmul(totals[0:HI, 0:1], triu[0:HI, 0:HI], small[:, 2:3], start=True, stop=True).then_inc(s_cum, 1)
                pe.wait_ge(s_hd, 10 * k + 9)
                pe.matmul(totals[0:1, 0:NC], ones[0:USED, 0:1], started[0:USED, :], start=True,
                          stop=True).then_inc(s_win, 1)
                if k:
                    pe.wait_ge(s_tab, EC // 2 + 1)
                pe.matmul(bank[2][0:HI, 0:P], identf[0:HI, 0:HI], table0[:, :], start=True, stop=False,
                          skip_group_check=True).then_inc(s_seed, 1)

                def spread(t, s, n, cold):
                    h, rows = bank[3 + s][0:HI, :], bank[5 + s]
                    if not cold:
                        pe.wait_ge(s_hiTs, n - 1)
                    for j in range(4):
                        i = pe.matmul(h[:, j * EP:(j + 1) * EP],
                                      ohhi[0:EP, bass.ds(t * U + 4 * s + j, 1), :].rearrange("p c k -> p (c k)"),
                                      identb[0:EP, 0:EP], start=True, stop=True, skip_group_check=True)
                    i.then_inc(s_hiT, 1)
                    yield
                    if not cold:
                        pe.wait_ge(s_rank, n - 1)
                    pe.wait_ge(s_kst, n + 2 * k + 1)
                    for j in range(4):
                        i = pe.transpose(rows[0:EP, j * EP:(j + 1) * EP],
                                         kst[0:EP, 4 * s + j:4 * s + j + 1].broadcast_to([EP, EP]),
                                         identf[0:EP, 0:EP])
                    i.then_inc(s_row, 1)
                    yield

                def rank_step(t, first, last=False, counted=None):
                    for s in range(2):
                        n = 2 * (groups * k + t) + s
                        pe.wait_ge(s_hiTs, n + 1)
                        if not first:
                            pe.wait_ge(s_rank, n - 1)
                        ahead = iter(()) if last and s else spread(t + s, 1 - s, n + 1, first and s == 0)
                        for half in range(2):
                            pe.wait_ge(s_tab, (EC // 2 + 1) * k + U // 2 * t + 2 * s + half + 1)
                            for j in (2 * half, 2 * half + 1):
                                pe.matmul(bank[7 * s][0:EP, j * P:(j + 1) * P], ohhiT[:, 4 * s + j, :],
                                          table[:, half, :], start=True, stop=True,
                                          skip_group_check=True).then_inc(s_look, 1)
                            for j in (2 * half, 2 * half + 1):
                                c = t * U + 4 * s + j
                                i = pe.matmul(bank[2][0:HI, 0:P],
                                              ohhi[0:EP, bass.ds(c, 1), :].rearrange("p c k -> p (c k)"),
                                              ohlo[0:EP, bass.ds(c, 1), :].rearrange("p c k -> p (c k)"),
                                              start=False, stop=False, skip_group_check=True)
                            i.then_inc(s_upd, 1)
                            next(ahead, None)
                            if counted is not None and half == 0:
                                count(1, counted, isinstance(counted, int) and counted == 0, parts=(4 * s,))

                for _ in spread(0, 0, 2 * groups * k, k == 0):
                    pass
                if k:
                    pe.wait_ge(s_hd, 20)
                rank_step(0, k == 0)
                rank_step(1, False)
                rank_step(2, False, counted=0 if k == 0 else None)
                with pe.Fori(3, groups - 1) as t:
                    rank_step(t, False, counted=t - 2 if k == 0 else None)
                rank_step(groups - 1, False, True, groups - 3 if k == 0 else None)
            pe.wait_ge(s_rank, 4 * groups)

            def sum_chunks(k, t, first, side=None):
                for j in range(U):
                    if j == 4 and side is not None:
                        side()
                    n = k * NC + t * U + j
                    pe.wait_ge(s_g[j], 16 * (turn(k) * (NC // U) + t + 1))
                    pe.wait_ge(s_oneh, n + 1)
                    if not (first and j < 4):
                        pe.wait_ge(s_add, n - 3)
                    pe.matmul(bank[j % 4][:, 0:D], onehot[:, j % 4, :], gath[:, j, :], start=True,
                              stop=True).then_inc(s_mm, 1)

            def own_transpose(k, w, first):
                pe.wait_ge(s_ostg, k * NW + w + 1)
                if not first:
                    pe.wait_ge(s_oTs, k * NW + w)
                for q in range(2):
                    i = pe.transpose(bank[4][:, q * P:(q + 1) * P], stg[:, 0, q * P:(q + 1) * P], identf[:, :])
                i.then_inc(s_oT, 1)

            def own_multiply(k, w, first):
                pe.wait_ge(s_oTs, k * NW + w + 1)
                if not first:
                    pe.wait_ge(s_own, k * NW + w)
                for q in range(2):
                    pe.matmul(bank[6][:, 0:D], stgT[:, 0, q * P:(q + 1) * P], wT[:, 2 * k + 1, q, :],
                              start=q == 0, stop=False)
                pe.matmul(bank[6][:, 0:D], onesb[:, :], bias6[:, k, :], start=False, stop=True).then_inc(s_oL, 1)

            def hop(k, w, first):
                sum_chunks(k, 2 * w, first, lambda: own_transpose(k, w, first))
                sum_chunks(k, 2 * w + 1, False, lambda: own_multiply(k, w, first))

            def transpose(k, w, s, cold):
                n = k * NW + w
                pe.wait_ge(s_stg, n + 1)
                if not cold:
                    pe.wait_ge(s_stTs, n - 1)
                for q in range(2):
                    i = pe.transpose(bank[4 + s][:, q * P:(q + 1) * P], stg[:, s, q * P:(q + 1) * P], identf[:, :])
                i.then_inc(s_stT, 1)

            def multiply(k, w, s, cold):
                n = k * NW + w
                pe.wait_ge(s_stTs, n + 1)
                if k == HOPS and not (isinstance(w, int) and w < 2):
                    pe.wait_ge(s_kept, w - 1)
                elif not cold:
                    pe.wait_ge(s_z, n - 1)
                wide, m = (D, wT[:, 2 * k]) if k < HOPS else (D + 2 * HEADS, w1T)
                for q in range(2):
                    i = pe.matmul(bank[6 + s][:, 0:wide], stgT[:, s, q * P:(q + 1) * P], m[:, q, :],
                                  start=q == 0, stop=q == 1)
                i.then_inc(s_lin, 1)

            def dense(k):
                def pair(t, cold, last=False):
                    transpose(k, 2 * t + 1, 1, cold)
                    multiply(k, 2 * t, 0, cold)
                    if not last:
                        transpose(k, 2 * t + 2, 0, False)
                    multiply(k, 2 * t + 1, 1, cold)
                if k < HOPS:
                    pe.wait_ge(s_own, (k + 1) * NW)
                transpose(k, 0, 0, k == 0)
                pair(0, k == 0)
                with pe.Fori(1, NW // 2 - 1) as t:
                    pair(t, False)
                pair(NW // 2 - 1, False, True)

            pe.wait_ge(s_small, 16 * (2 * HOPS + 5 + 12))
            for k in range(HOPS):
                if k:
                    pe.wait_ge(s_stTs, k * NW)
                    pe.wait_ge(s_z, k * NW)
                hop(k, 0, k == 0)
                with pe.Fori(1, NW) as w:
                    hop(k, w, False)
                dense(k)
            dense(HOPS)

            def transpose_features(g, s):
                pe.wait_ge(s_fst, g + 1)
                pe.wait_ge(s_fsl, g + 1)
                pe.nop(nofuse=True)
                for j in range(4):
                    i = pe.transpose(bank[s][0:36, 0:2 * P].bitcast(BF16)[:, j * P:(j + 1) * P], fst[:, 4 * s + j, 0:36],
                                     identb[:, :])
                i.then_inc(s_eaT, 1)

            def score(t, first):
                ws = windows(mybir.EngineType.PE, win_next, t * U, U) if not first else (
                    (None, *windows(mybir.EngineType.PE, win_next, 1, U - 1)))
                for j in range(U):
                    n = t * U + j
                    if not (first and j < 2):
                        pe.wait_ge(s_oneh, HOPS * NC + n - 1)
                    pe.transpose(bank[2 + j % 2][:, 0:P // 2].bitcast(BF16), fst[:, j, 36:37].broadcast_to([P, P]),
                                 identb[:, :]).then_inc(s_lrow, 1)
                    if j % 4 == 0:
                        pe.wait_ge(s_eaTs, 2 * t + j // 4 + 1)
                    if not (first and j < 2):
                        pe.wait_ge(s_relu, n - 1)
                    pe.matmul(bank[4 + j % 2][:, 0:D], eaT[:, j // 4, (j % 4) * P:(j % 4 + 1) * P], ew36[:, :],
                              start=True, stop=True).then_inc(s_enc, 1)
                    if not (first and j == 0):
                        look_up(n - 1, (j - 1) % U, ws[j], first and 1 <= j < 3)
                    if j % 4 == 1:
                        transpose_features(2 * t + j // 4 + 1, 1 - j // 4)

            def look_up(n, j, w, cold):
                pe.wait_ge(s_oneh, HOPS * NC + n + 1)
                if not cold:
                    pe.wait_ge(s_em, (HOPS - 1) * NW + n - 1)
                    pe.wait_ge(s_sde, n - 1)
                for i in range(3):
                    mm = pe.matmul(bank[6 + j % 2][:, 0:HX], onehotb[:, j % 4, :],
                                   h_parts[i][:, bass.ds(w, 1), :].rearrange("p c k -> p (c k)"),
                                   start=i == 0, stop=i == 2)
                mm.then_inc(s_hd_, 1)
            pe.wait_ge(s_kept, NW)
            pe.wait_ge(s_p1, NW)
            pe.wait_ge(s_p2, NW)
            transpose_features(0, 0)
            score(0, True)
            with pe.Fori(1, NC // U) as t:
                score(t, False)
            look_up(NC - 1, U - 1, windows(mybir.EngineType.PE, win_next, NC, 1)[0], False)

            pe.wait_ge(s_al, 4)
            for i, (b, n) in enumerate(2 * quads):
                if i >= 2:
                    pe.wait_ge(s_alTs, i - 1)
                a = (s_sb if i < len(quads) else sde)[:, :, :].rearrange("p c h -> p (c h)")
                for q in range(n):
                    t = pe.transpose(bank[i % 2][:, q * P:(q + 1) * P], a[:, (b + q) * P:(b + q + 1) * P], identf[:, :])
                t.then_inc(s_alT, 1)
            for i, (b, n) in enumerate(quads):
                pe.wait_ge(s_ex, b + n)
                if i >= 2:
                    pe.wait_ge(s_exs, i - 1)
                for q in range(n):
                    t = pe.transpose(bank[2 + i % 2][:, q * P:(q + 1) * P], alT[:, b + q, :], identf[:, :])
                t.then_inc(s_exT, 1)

            def attend(t):
                for j in range(U):
                    n = HOPS * NC + t * U + j
                    pe.wait_ge(s_val, t * U + j + 1)
                    pe.wait_ge(s_vx, t * U + j + 1)
                    pe.wait_ge(s_oneh, NC + n + 1)
                    pe.wait_ge(s_add, n - 3)
                    pe.matmul(bank[4 + j % 4][:, 0:HX], onehot[:, j % 4, :], val[:, j % 4, :], start=True,
                              stop=True).then_inc(s_mm, 1)
            with pe.Fori(0, NC // U) as t:
                attend(t)

        @block.scalar
        def _(act):
            for m in range(2 * HOPS + 1):
                act.wait_ge(s_wT_pe, m + 1)
                o = wT[:, m, :, :] if m < 2 * HOPS else w1T[:, :, 0:D]
                nc.scalar.copy(o, bank[m % 2][:, :].rearrange("p (a o) -> p a o", a=2)).then_inc(s_wT, 1)
            nc.scalar.copy(w1T[:, :, D:], bank[2][:, 0:4 * HEADS].rearrange("p (a o) -> p a o", a=2)).then_inc(s_wT, 1)
            for k in range(2):
                act.wait_ge(s_seed, k + 1)
                nc.scalar.copy(table[:, 0, :], bank[2][0:HI, 0:P]).then_inc(s_tab, 1)

                def stage(c, j):
                    nc.scalar.copy(kst[0:EP, j:j + 4], key_f[0:EP, bass.ds(c, 4)]).then_inc(s_kst, 1)

                stage(0, 0)
                stage(4, 4)

                def store_hiT(g, s):
                    act.wait_ge(s_hiT, g + 1)
                    nc.scalar.copy(ohhiT[:, 4 * s:4 * s + 4, :],
                                   bank[3 + s][0:HI, 0:4 * EP].rearrange("p (a e) -> p a e", a=4)).then_inc(s_hiTs, 1)

                def step(t, last=False):
                    for j in range(U):
                        if j % 4 == 2:
                            act.wait_ge(s_eq, 5 * (2 * (groups * k + t) + j // 4) + 4)
                            act.nop(nofuse=True)
                            stage((t + 1) * U + j - 2, j - 2)
                        if j % 2:
                            act.wait_ge(s_upd, EC // 2 * k + U // 2 * t + j // 2 + 1)
                            nc.scalar.copy(table[:, (j // 2 + 1) % 2, :], bank[2][0:HI, 0:P]).then_inc(s_tab, 1)
                        if j % 4 == 1 and not (last and j == 5):
                            store_hiT(2 * (groups * k + t) + j // 4 + 1, 1 - j // 4)
                store_hiT(2 * groups * k, 0)
                step(0)
                with act.Fori(1, groups - 1) as t:
                    step(t)
                step(groups - 1, True)

            def hop(k, w):
                stage_idx(k, 2 * w + 1, 0)
                if k == 0:
                    act.wait_ge(s_x, 16 * (w + 2))
                if not (k == 0 and isinstance(w, int)):
                    act.wait_ge(s_oT, k * NW + w)
                act.nop(nofuse=True)
                h = hcur[:, bass.ds(w, 1), :].rearrange("p c d -> p (c d)")
                nc.scalar.copy(stg[:, 0, 0:D], h).then_inc(s_ostg, 1)
                stage_idx(k, 2 * w + 1, 1)
                act.wait_ge(s_oT, k * NW + w + 1)
                nc.scalar.copy(stgT[:, 0, 0:D], bank[4][:, 0:D]).then_inc(s_oTs, 1)
                stage_idx(k, 2 * w + 2, 0)
                act.wait_ge(s_oL, k * NW + w + 1)
                act.nop(nofuse=True)
                nc.scalar.copy(h, bank[6][:, 0:D]).then_inc(s_own, 1)
                stage_idx(k, 2 * w + 2, 1)

            def stage(k, w, s, cold=False):
                if not cold:
                    act.wait_ge(s_stT, k * NW + w - 1)
                if k == HOPS:
                    act.wait_ge(s_nrm, w + 1)
                act.nop(nofuse=True)
                nc.scalar.copy(stg[:, s, 0:D], (acc if k < HOPS else hcur)[:, bass.ds(w, 1), 0:D]
                               .rearrange("p c d -> p (c d)")).then_inc(s_stg, 1)

            def store_T(k, w, s, cold=False):
                n = k * NW + w
                act.wait_ge(s_stT, n + 1)
                if not cold:
                    act.wait_ge(s_lin, n - 1)
                nc.scalar.copy(stgT[:, s, 0:D], bank[4 + s][:, 0:D]).then_inc(s_stTs, 1)

            def dense(k):
                def step(w, s, cold, more=2):
                    if more > 0:
                        store_T(k, w + 1, 1 - s, cold)
                    if more > 1:
                        stage(k, w + 2, s)
                    if k < HOPS - 1:
                        act.wait_ge(s_z, k * NW + w + 1)
                        nc.scalar.activation(elu[:, s, D:2 * D], elu[:, s, 0:D], ACT.Exp).then_inc(s_ea, 1)
                    if k == HOPS:
                        keep(w, s)

                def keep(w, s):
                    act.wait_ge(s_lin, k * NW + w + 1)
                    act.nop(nofuse=True)
                    nc.scalar.copy(x0[:, bass.ds(w, 1), :].rearrange("p c d -> p (c d)"), bank[6 + s][:, 0:HX])
                    nc.scalar.copy(s_src[:, bass.ds(w, 1), :].rearrange("p c d -> p (c d)"),
                                   bank[6 + s][:, HX:HX + HEADS]).then_inc(s_kept, 1)

                if k < HOPS:
                    act.wait_ge(s_add, NC * (k + 1))
                stage(k, 0, 0, k == 0)
                stage(k, 1, 1, k == 0)
                store_T(k, 0, 0, k == 0)
                step(0, 0, k == 0)
                step(1, 1, False)
                with act.Fori(1, NW // 2 - 1) as t:
                    step(2 * t, 0, False)
                    step(2 * t + 1, 1, False)
                step(NW - 2, 0, False, 1)
                step(NW - 1, 1, False, 0)

            def stage_idx(p, t, h, first=False):
                if not (first and p == 0):
                    for j in range(4 * h, 4 * h + 4):
                        act.wait_ge(s_g[j], 16 * (p * (NC // U) + t))
                    act.nop(nofuse=True)
                if p == HOPS and not first:
                    nc.scalar.copy(s_sb[:, bass.ds((t - 1) * U + 4 * h, 4), :],
                                   gath[:, 4 * h:4 * h + 4, 0:HEADS]).then_inc(s_ss, 1)
                r, col = (recs[0], 1) if p < HOPS else (recs[1], 0)
                nc.scalar.copy(idx[:, 4 * h:4 * h + 4],
                               r[:, bass.ds(t * U + 4 * h, 4), col].bitcast(I32)).then_inc(s_idx, 1)

            act.wait_ge(s_back[0], 16)
            act.wait_ge(s_lo7, 2)
            for k in range(HOPS + 1):
                if k < HOPS:
                    stage_idx(k, 0, 0, True)
                    stage_idx(k, 0, 1, True)
                    if k:
                        act.wait_ge(s_hst, STORED * k)
                    hop(k, 0)
                    with act.Fori(1, NW) as w:
                        hop(k, w)
                dense(k)
                if k == HOPS - 1:
                    act.wait_ge(s_ln, 2)
                    nc.scalar.activation(stat[:, :, 2], stat[:, :, 1], ACT.Sqrt).then_inc(s_sq, 1)

            act.wait_ge(s_lo7, 3)
            act.wait_ge(s_p2, NW)

            def stage_recs(c, j):
                e = recs[1][:, bass.ds(c, 4), 2:8].bitcast(BF16)
                nc.scalar.copy(fst[:, j:j + 4, 36], lo_s[:, bass.ds(c, 4)]).then_inc(s_fsl, 1)
                for a in range(3):
                    i = nc.scalar.copy(fst[:, j:j + 4, 12 * a:12 * a + 12].rearrange("p c (b f) -> p c b f", b=3),
                                       e[:, :, 4 * a:4 * a + 4].unsqueeze(2).broadcast_to([P, 4, 3, 4]))
                i.then_inc(s_fst, 1)

            stage_recs(0, 0)
            stage_recs(4, 4)
            stage_idx(HOPS, 0, 0, True)
            stage_idx(HOPS, 0, 1, True)

            def keep_s_dst(n, j):
                act.wait_ge(s_hd_, n + 1)
                act.nop(nofuse=True)
                nc.scalar.copy(sde[:, bass.ds(n, 1), :].rearrange("p c h -> p (c h)"),
                               bank[6 + j % 2][:, D:HX]).then_inc(s_sde, 1)

            def store_features(g, s):
                act.wait_ge(s_eaT, g + 1)
                nc.scalar.copy(eaT[:, s, :], bank[s][0:36, 0:2 * P].bitcast(BF16)).then_inc(s_eaTs, 1)

            def score(t):
                for j in range(U):
                    n = t * U + j
                    act.wait_ge(s_enc, n + 1)
                    if not (isinstance(t, int) and j < 4):
                        act.wait_ge(s_em, (HOPS - 1) * NW + n - 3)
                    nc.scalar.activation(encr[:, j % 4, :], bank[4 + j % 2][:, 0:D], ACT.Relu).then_inc(s_relu, 1)
                    if not (isinstance(t, int) and j == 0):
                        keep_s_dst(n - 1, (j - 1) % U)
                    if j % 4 == 2:
                        store_features(2 * t + j // 4 + 1, 1 - j // 4)
                    if j % 4 == 3:
                        stage_recs((t + 1) * U + j - 3, j - 3)
                        stage_idx(HOPS, t + 1, j // 4)
            store_features(0, 0)
            score(0)
            with act.Fori(1, NC // U) as t:
                score(t)
            keep_s_dst(NC - 1, U - 1)
            act.wait_ge(s_idx, (HOPS + 1) * (2 * NC // U + 2))
            stage_idx(HOPS + 1, 0, 0)
            stage_idx(HOPS + 1, 0, 1)
            for i, (b, n) in enumerate(2 * quads):
                act.wait_ge(s_alT, i + 1)
                nc.scalar.copy((alT if i < len(quads) else dotT)[:, b:b + n, :],
                               bank[i % 2][:, 0:n * P].rearrange("p (b e) -> p b e", b=n)).then_inc(s_alTs, 1)
            for b in range(NB):
                act.wait_ge(s_mx, b + 1)
                nc.scalar.activation(alT[:, b, :], alT[:, b, :], ACT.Exp).then_inc(s_ex, 1)
            for i, (b, n) in enumerate(quads):
                act.wait_ge(s_exT, i + 1)
                nc.scalar.copy(s_sb[:, 16 * b:16 * (b + n), :].rearrange("p c h -> p (c h)"),
                               bank[2 + i % 2][:, 0:n * P]).then_inc(s_exs, 1)
            act.wait_ge(s_exs, len(quads))

            def attend(t):
                for j in range(U):
                    n = t * U + j
                    act.wait_ge(s_mm, HOPS * NC + n - 3)
                    act.nop(nofuse=True)
                    nc.scalar.copy(val[:, j % 4, D:HX], s_sb[:, bass.ds(n, 1), :].rearrange("p c h -> p (c h)")
                                   ).then_inc(s_vx, 1)
                    if j % 4 == 3:
                        stage_idx(HOPS + 1, t + 1, j // 4)
            attend(0)
            with act.Fori(1, NC // U) as t:
                attend(t)
            act.wait_ge(s_ln, LN_STEPS + 2 + 2)
            nc.scalar.activation(stat[:, :, 2], stat[:, :, 1], ACT.Sqrt).then_inc(s_sq, 1)


        @block.vector
        def _(dve):
            v = nc.vector
            v.memset(zero_tile, 0.0).then_inc(s_fill, 1)
            dve.wait_ge(s_lane, 7)
            v.tensor_copy(iota_f[:, :], iota_i[:, :]).then_inc(s_const, 1)
            v.tensor_copy(iota_b[:, :], iota_i[:, 0:P]).then_inc(s_const, 1)
            v.tensor_copy(lane_f[:, :], lane_i[:, :]).then_inc(s_const, 1)
            v.tensor_copy(identb[:, :], identf[:, :]).then_inc(s_const, 1)
            v.memset(key_f[0:EP, EC:EC + U], 0.0).then_inc(s_const, 1)
            v.tensor_reduce(fold[:, :], identf[:, :].rearrange("p (b i) -> p i b", i=HI), X, ALU.add).then_inc(s_const, 1)
            v.memset(earlier[0:EP, 0:EP], 1.0).then_inc(s_const, 1)
            v.tensor_copy(earlier[0:EP, EP:2 * EP], tri[0:EP, 0:EP]).then_inc(s_const, 1)
            dve.wait_ge(s_small, 16 * (2 * HOPS + 5))
            split(dve, [b_parts[:, i, :, :] for i in range(3)], bias2, s_split, 0)
            v.memset(onesb[:, :], 1.0).then_inc(s_split, 1)
            split(dve, [ew_parts[:, i, :] for i in range(3)], ew4, s_split, 6)
            v.tensor_reduce(headmask[:, :], identf[:, :].rearrange("p (b i) -> p b i", i=HD), X, ALU.add).then_inc(s_blk, 1)
            v.memset(a_blocks[:, :, :], 0.0).then_inc(s_blk, 1)
            dve.wait_ge(s_blk, 2)
            for i in range(2):
                for a in range(2):
                    c = HEADS * i + HEADS // 2 * a
                    v.tensor_scalar(a_blocks[:, a, c:c + HEADS // 2], headmask[:, :], a_cols[:, i, a:a + 1], None,
                                    ALU.mult).then_inc(s_blk, 1)
            dve.wait_ge(s_in, 64)
            rec_i = rec[:, :, :].bitcast(I32)
            v.tensor_copy(rec_i[0:EP, :, 0], src_i[0:EP, :]).then_inc(s_rec, 1)
            v.tensor_copy(rec_i[0:EP, :, 1], dst_i[0:EP, :]).then_inc(s_rec, 1)
            v.tensor_copy(rec[0:EP, :, 2], w_in[0:EP, :]).then_inc(s_rec, 1)
            v.tensor_copy(rec[0:EP, :, 3:6], ea_in[0:EP, :, :]).then_inc(s_rec, 1)
            v.memset(rec[0:EP, :, 6], 1.0).then_inc(s_rec, 1)
            v.memset(rec[0:EP, :, 7], 0.0).then_inc(s_rec, 1)
            dve.wait_ge(s_rec, 6)

            def split_key(key, q):
                v.tensor_scalar(lo_i[0:EP, :], key[0:EP, :], P - 1, None, ALU.bitwise_and).then_inc(s_keys, 1)
                dve.wait_ge(s_keys, q + 1)
                v.tensor_copy(lo_f[0:EP, :], lo_i[0:EP, :]).then_inc(s_keys, 1)
                dve.wait_ge(s_keys, q + 2)
                v.tensor_scalar(lo_i[0:EP, :], key[0:EP, :], SHIFT, None, ALU.logical_shift_right).then_inc(s_keys, 1)
                dve.wait_ge(s_keys, q + 3)
                v.tensor_copy(hi_f[0:EP, :], lo_i[0:EP, :]).then_inc(s_keys, 1)
                dve.wait_ge(s_keys, q + 4)

            def build_hi(c, n):
                return v.tensor_tensor(ohhi[0:EP, bass.ds(c, n), :],
                                       hi_f[0:EP, bass.ds(c, n)].unsqueeze(2).broadcast_to([EP, n, HI]),
                                       iota_f[0:EP, 0:HI].unsqueeze(1).broadcast_to([EP, n, HI]), ALU.is_equal)

            def build_lo(t):
                v.tensor_tensor(ohlo[0:EP, bass.ds(t * U, U), :],
                                lo_f[0:EP, bass.ds(t * U, U)].unsqueeze(2).broadcast_to([EP, U, P]),
                                iota_b[0:EP, :].unsqueeze(1).broadcast_to([EP, U, P]), ALU.is_equal).then_inc(s_oh, 1)

            def rebuild(t):
                dve.wait_ge(s_upd, U // 2 * (t + 1))
                build_hi(t * U, U)
                build_lo(t)

            for k in range(2):
                if k == 0:
                    v.tensor_copy(key_f[0:EP, 0:EC], src_i[0:EP, :]).then_inc(s_keys, 1)
                    split_key(src_i, 1)
                    build_hi(0, EC).then_inc(s_oh, 1)
                    dve.wait_ge(s_fill, 33)
                    dve.wait_ge(s_small, 16 * (2 * HOPS + 5 + 12))
                    with dve.Fori(0, groups) as t:
                        build_lo(t)
                    dve.wait_ge(s_oh, 1 + groups)
                    split_key(dst_i, 5)
                else:
                    dve.wait_ge(s_row, 2 * groups)
                    v.tensor_copy(key_f[0:EP, 0:EC], dst_i[0:EP, :]).then_inc(s_keys, 1)
                    rebuild(groups - 1)
                q = 10 * k
                dve.wait_ge(s_hist, k + 1)
                for j in range(4):
                    v.tensor_copy(blocks[j * HI:(j + 1) * HI, :],
                                  bank[k][j * HI:(j + 1) * HI, j * P:(j + 1) * P]).then_inc(s_part, 1)
                dve.wait_ge(s_sum, k + 1)
                v.tensor_copy(hist[:, :], bank[1 - k][0:HI, 0:P]).then_inc(s_hd, 1)
                dve.wait_ge(s_hd, q + 1)
                v.tensor_reduce(small[:, 0:1], hist[:, :], X, ALU.add).then_inc(s_hd, 1)
                dve.wait_ge(s_hd, q + 2)
                v.tensor_scalar(small_i[:, 0:1], small[:, 0:1], float(P - 1), None, ALU.add).then_inc(s_hd, 1)
                dve.wait_ge(s_hd, q + 3)
                v.tensor_scalar(small_i[:, 1:2], small_i[:, 0:1], SHIFT, None,
                                ALU.logical_shift_right).then_inc(s_base, 1)
                dve.wait_ge(s_base, k + 1)
                v.tensor_copy(small[:, 2:3], small_i[:, 1:2]).then_inc(s_hd, 1)
                dve.wait_ge(s_cum, k + 1)
                v.tensor_copy(small[:, 3:4], bank[1 - k][0:HI, 0:1]).then_inc(s_hd, 1)
                dve.wait_ge(s_hd, q + 5)
                v.tensor_scalar(small[:, 4:5], small[:, 3:4], float(P), None, ALU.mult).then_inc(s_hd, 1)
                dve.wait_ge(s_hd, q + 6)
                v.tensor_tensor_scan(table0[:, :], ones[0:HI, :], hist[:, :], small[:, 4:5], ALU.mult,
                                     ALU.add).then_inc(s_hd, 1)
                dve.wait_ge(s_hd, q + 7)
                v.tensor_tensor(table0[:, :], table0[:, :], hist[:, :], ALU.subtract).then_inc(s_hd, 1)
                v.tensor_scalar(started[:, :], iota_f[0:HI, :], small[:, 3:4], None, ALU.is_ge).then_inc(s_hd, 1)
                dve.wait_ge(s_win, k + 1)
                if k:
                    v.tensor_scalar(win_next[:, 1:NC + 1], bank[1 - k][0:1, 0:NC], -1.0, None, ALU.add).then_inc(s_base, 1)
                v.tensor_scalar(win_late[k][:, LAG:NC + LAG], bank[1 - k][0:1, 0:NC], -1.0, None,
                                ALU.add).then_inc(s_hd, 1)

                def ranks(pair, h, first, old=None):
                    t = 2 * pair + h
                    g = groups * k + t
                    for q in range(2):
                        tm = terms[0:EP, :, :]
                        if not (first and h == 0 and q == 0):
                            dve.wait_ge(s_rank, 2 * g + q)
                        dve.wait_ge(s_row, 2 * g + q + 1)
                        for j in range(4):
                            wide = (j % 2 + 1) * EP
                            v.scalar_tensor_tensor(out=tm[:, j, 0:wide],
                                                   in0=bank[5 + q][0:EP, j // 2 * 2 * EP:j // 2 * 2 * EP + wide],
                                                   scalar=kst[0:EP, 4 * q + j:4 * q + j + 1],
                                                   in1=earlier[0:EP, 2 * EP - wide:2 * EP], op0=ALU.is_equal, op1=ALU.mult,
                                                   accum_out=tm[:, j, TERMS - 1:TERMS]).then_inc(s_eq, 1)
                        if old is not None and q == 0:
                            rebuild(old)
                        dve.wait_ge(s_look, EC * k + t * U + 4 * q + 4)
                        v.tensor_tensor(tm[:, :, 2 * EP:2 * EP + P],
                                        bank[7 * q][0:EP, :].rearrange("p (c n) -> p c n", c=4),
                                        ohlo[0:EP, bass.ds(t * U + 4 * q, 4), :], ALU.mult).then_inc(s_eq, 1)
                        dve.wait_ge(s_eq, 5 * (2 * g + q + 1))
                        v.tensor_reduce(rank[0:EP, 4 * q:4 * q + 4], tm[:, :, 2 * EP:TERMS], X,
                                        ALU.add).then_inc(s_rank, 1)
                    dve.wait_ge(s_rank, 2 * g + 2)
                    v.tensor_copy(pos_i[0:EP, 0, :], rank[0:EP, :]).then_inc(s_d, 1)
                    dve.wait_ge(s_d, 3 * g + 1)
                    v.tensor_scalar(pos_i[0:EP, 1, :], pos_i[0:EP, 0, :], P - 1, None,
                                    ALU.bitwise_and).then_inc(s_d, 1)
                    v.tensor_scalar(pos_i[0:EP, 2, :], pos_i[0:EP, 0, :], SHIFT, None,
                                    ALU.logical_shift_right).then_inc(s_d, 1)
                    dve.wait_ge(s_d, 3 * g + 3)
                    if not first:
                        dve.wait_ge(s_scat[h], 16 * U * (groups // 2 * k + pair))
                    v.tensor_copy(leaving[0:EP, h, :, :], rec[0:EP, bass.ds(t * U, U), :]).then_inc(s_leave, 1)
                    v.scalar_tensor_tensor(out=place[0:EP, h, :], in0=pos_i[0:EP, 1, :], scalar=float(NC),
                                           in1=pos_i[0:EP, 2, :], op0=ALU.mult, op1=ALU.add).then_inc(s_pos, 1)
                ranks(0, 0, k == 0)
                ranks(0, 1, k == 0, 0 if k == 0 else None)
                with dve.Fori(1, groups // 2) as t:
                    for h in range(2):
                        ranks(t, h, False, 2 * t + h - 1 if k == 0 else None)

            def los(k):
                dve.wait_ge(s_back[k], 16)
                ri = recs[k][:, 0:NC, :].bitcast(I32)
                q = 4 * k
                v.tensor_scalar(lo_si[:, :], ri[:, :, k], P - 1, None, ALU.bitwise_and).then_inc(s_lo, 1)
                dve.wait_ge(s_lo, q + 1)
                v.tensor_copy(lo_s[:, 0:NC], lo_si[:, :]).then_inc(s_lo, 1)
                dve.wait_ge(s_lo, q + 2)
                filled = recs[0][:, 0:NC, 6] if k == 0 else recs[1][:, 0:NC, 3:4].bitcast(BF16)[:, :, 1]
                v.scalar_tensor_tensor(out=lo_s[:, 0:NC], in0=lo_s[:, 0:NC], scalar=1.0, in1=filled,
                                       op0=ALU.add, op1=ALU.mult).then_inc(s_lo, 1)
                dve.wait_ge(s_lo, q + 3)
                v.tensor_scalar(lo_s[:, 0:NC], lo_s[:, 0:NC], -1.0, None, ALU.add).then_inc(s_lo, 1)
                dve.wait_ge(s_lo, q + 4)

            for q in s_scat:
                dve.wait_ge(q, 16 * EC)
            dve.wait_ge(s_tab, EC + 2)
            for k in range(2):
                v.memset(recs[k][:, NC:NC + U, :], 0.0).then_inc(s_lo7, 1)
            v.memset(x0[:, FULLW:NW, :], 0.0).then_inc(s_x0z, 1)
            v.memset(hcur[:, FULLW:NW, :], 0.0).then_inc(s_x0z, 1)
            v.memset(acc[:, :, :], 0.0).then_inc(s_clr, 1)
            los(0)

            def sum_chunks(k, t):
                row = win_late[0 if k < HOPS else 1]
                if isinstance(t, int):
                    ws = [None] * LAG + list(windows(mybir.EngineType.DVE, row, LAG, U - LAG))
                else:
                    ws = windows(mybir.EngineType.DVE, row, t * U, U)
                for j in range(U):
                    n = k * NC + t * U + j
                    c = t * U + j
                    cold = isinstance(t, int) and k == 0
                    m = n if k < HOPS else n + NC
                    if not (cold and j < 4):
                        dve.wait_ge(s_mm, n - 3)
                    if k < HOPS:
                        v.tensor_scalar(onehot[:, j % 4, :], iota_f[:, 0:P], lo_s[:, bass.ds(c, 1)],
                                        recs[0][:, bass.ds(c, 1), 2], ALU.is_equal, ALU.mult).then_inc(s_oneh, 1)
                    else:
                        v.tensor_scalar(onehot[:, j % 4, :], iota_f[:, 0:P], lo_s[:, bass.ds(c, 1)], None,
                                        ALU.is_equal).then_inc(s_oneh, 1)
                        dve.wait_ge(s_g[j], 16 * (turn(k) * (NC // U) + t + 1))
                        v.tensor_tensor(val[:, j % 4, 0:D].rearrange("p (h d) -> p h d", h=HEADS),
                                        gath[:, j, :].rearrange("p (h d) -> p h d", h=HEADS),
                                        s_sb[:, bass.ds(c, 1), :].rearrange("p c h -> p (c h)").unsqueeze(2)
                                        .broadcast_to([P, HEADS, HD]), ALU.mult).then_inc(s_val, 1)
                    if not (isinstance(t, int) and j < LAG):
                        add(k, n - LAG, (j - LAG) % U, ws[j])

            def add(k, n, j, w):
                wide = D if k < HOPS else HX
                b = bank[j % 4] if k < HOPS else bank[4 + j % 4]
                dve.wait_ge(s_mm, n + 1)
                dve.wait_ge(s_add, n) if not (isinstance(n, int) and n == 0) else None
                a = acc[:, bass.ds(w, 1), 0:wide].rearrange("p c d -> p (c d)")
                v.tensor_tensor(a, a, b[:, 0:wide], ALU.add).then_inc(s_add, 1)

            def dense(k):
                def at(t, w):
                    return t[:, bass.ds(w, 1), 0:D].rearrange("p c d -> p (c d)")

                def total(w, s, cold):
                    n = k * NW + w
                    dve.wait_ge(s_lin, n + 1)
                    if not cold:
                        dve.wait_ge(s_new, n - 1)
                    v.tensor_tensor(elu[:, s, 0:D], bank[6 + s][:, 0:D], at(hcur, w), ALU.add).then_inc(s_z, 1)

                def finish(w, s):
                    n = k * NW + w
                    if k == HOPS - 1:
                        dve.wait_ge(s_z, n + 1)
                        v.tensor_tensor(at(hcur, w), elu[:, s, 0:D], at(x0, w), ALU.add).then_inc(s_new, 1)
                        return
                    dve.wait_ge(s_ea, n + 1)
                    v.tensor_scalar(elu[:, s, D:2 * D], elu[:, s, D:2 * D], 1.0, -1.0, ALU.min, ALU.add).then_inc(s_em, 1)
                    dve.wait_ge(s_em, n + 1)
                    v.scalar_tensor_tensor(out=at(hcur, w), in0=elu[:, s, 0:D], scalar=0.0, in1=elu[:, s, D:2 * D],
                                           op0=ALU.max, op1=ALU.add).then_inc(s_new, 1)

                def stats(w):
                    if k == HOPS - 1:
                        dve.wait_ge(s_new, k * NW + w + 1)
                        v.bn_stats(s_src[:, bass.ds(w, 1), 0:6].rearrange("p c d -> p (c d)"), at(hcur, w)).then_inc(s_bn, 1)

                dve.wait_ge(s_own, (k + 1) * NW)
                if k == HOPS - 1:
                    dve.wait_ge(s_x, 32 * (FULLW + 1))
                total(0, 0, k == 0)
                total(1, 1, k == 0)
                finish(0, 0)
                with dve.Fori(1, NW // 2) as t:
                    total(2 * t, 0, False)
                    finish(2 * t - 1, 1)
                    stats(2 * t - 2)
                    total(2 * t + 1, 1, False)
                    finish(2 * t, 0)
                    stats(2 * t - 1)
                finish(NW - 1, 1)
                stats(NW - 2)
                stats(NW - 1)

            def normalise(w, done):
                h = hcur[:, bass.ds(w, 1), :].rearrange("p c d -> p (c d)")
                v.tensor_scalar(h, h, stat[:, bass.ds(w, 1), 0], stat[:, bass.ds(w, 1), 3], ALU.subtract,
                                ALU.mult).then_inc(done, 1)

            def deviations(q, m, sums):
                dve.wait_ge(s_bn, NW * (m + 1))
                for w in range(NW):
                    ins = v.bn_aggr(stat[:, w, 0:2], sums[:, w, 0:6])
                ins.then_inc(s_ln, 1)
                dve.wait_ge(s_ln, q + 1)
                v.tensor_scalar(stat[:, :, 1], stat[:, :, 1], EPS, None, ALU.add).then_inc(s_ln, 1)
                dve.wait_ge(s_sq, m + 1)
                v.reciprocal(stat[:, :, 3], stat[:, :, 2]).then_inc(s_ln, 1)
                dve.wait_ge(s_ln, q + 3)

            def split_h():
                def parts(t, cold):
                    def at(x, s):
                        return x[:, bass.ds(2 * t + s, 1), 0:HX].rearrange("p c d -> p (c d)")
                    dve.wait_ge(s_kept, 2 * t + 2)
                    for s in range(2):
                        v.tensor_copy(at(h_parts[0], s), at(x0, s)).then_inc(s_p0, 1)
                    for s in range(2):
                        dve.wait_ge(s_p0, 2 * t + s + 1)
                        if not cold:
                            dve.wait_ge(s_p2, 2 * t + s - 1)
                        v.tensor_tensor(elu[:, s, 0:HX], at(x0, s), at(h_parts[0], s), ALU.subtract).then_inc(s_r1, 1)
                    for s in range(2):
                        dve.wait_ge(s_r1, 2 * t + s + 1)
                        v.tensor_copy(at(h_parts[1], s), elu[:, s, 0:HX]).then_inc(s_p1, 1)
                    for s in range(2):
                        dve.wait_ge(s_p1, 2 * t + s + 1)
                        v.tensor_tensor(elu[:, s, 0:HX], elu[:, s, 0:HX], at(h_parts[1], s), ALU.subtract).then_inc(s_r2, 1)
                for w in range(6):
                    normalise(w, s_nrm)
                parts(0, True)
                with dve.Fori(1, NW // 2 - 2) as t:
                    normalise(2 * t + 4, s_nrm)
                    normalise(2 * t + 5, s_nrm)
                    parts(t, False)
                parts(NW // 2 - 2, False)
                parts(NW // 2 - 1, False)

            def split_features():
                dve.wait_ge(s_back[1], 16)
                full = dot[:, 0:NC // 2, :].rearrange("p c (a f) -> p (c a) f", f=4)
                v.tensor_copy(full, recs[1][:, 0:NC, 3:7]).then_inc(s_split, 1)
                dve.wait_ge(s_split, 12)
                rb = recs[1][:, 0:NC, 2:8].bitcast(BF16)
                split(dve, [rb[:, :, 4 * i:4 * i + 4] for i in range(3)], full, s_split, 12)

            for k in range(HOPS):
                if k:
                    dve.wait_ge(s_stg, NW * k)
                    v.memset(acc[:, :, :], 0.0).then_inc(s_clr, 1)
                dve.wait_ge(s_clr, k + 1)
                sum_chunks(k, 0)
                if k == 1:
                    split_features()
                with dve.Fori(1, NC // U) as t:
                    sum_chunks(k, t)
                ws = windows(mybir.EngineType.DVE, win_late[0], NC, LAG)
                for n in range(LAG):
                    add(k, k * NC + NC - LAG + n, U - LAG + n, ws[n])
                dve.wait_ge(s_add, NC * (k + 1))
                dense(k)
            los(1)
            deviations(0, 0, s_src)
            split_h()
            v.tensor_copy(lo_s[:, NC:NC + U], lo_s[:, NC - U:NC]).then_inc(s_lo7, 1)
            dve.wait_ge(s_lo7, 3)

            def score(t):
                for j in range(U):
                    n = t * U + j
                    cold = isinstance(t, int)
                    dve.wait_ge(s_lrow, n + 1)
                    if not (cold and j < 4):
                        dve.wait_ge(s_hd_, n - 3)
                    v.tensor_scalar(onehotb[:, j % 4, :], bank[2 + j % 2][:, 0:P // 2].bitcast(BF16), lane_f[:, 0:1], None,
                                    ALU.is_equal).then_inc(s_oneh, 1)
                    if not (cold and j < 2):
                        multiply(n - 2, (j - 2) % U)
                    if not (cold and j < 3):
                        take_dot(n - 3, (j - 3) % U)

            def multiply(n, j):
                dve.wait_ge(s_relu, n + 1)
                dve.wait_ge(s_sde, n + 1)
                v.tensor_tensor(prod[:, j % 4, :], encr[:, j % 4, :], bank[6 + j % 2][:, 0:D],
                                ALU.mult).then_inc(s_em, 1)

            def take_dot(n, j):
                dve.wait_ge(s_em, (HOPS - 1) * NW + n + 1)
                v.tensor_reduce(dot[:, bass.ds(n, 1), :].rearrange("p c h -> p (c h)"),
                                prod[:, j % 4, :].rearrange("p (h d) -> p h d", h=HEADS), X, ALU.add).then_inc(s_dot, 1)

            score(0)
            with dve.Fori(1, NC // U) as t:
                score(t)
            take_dot(NC - 3, (NC - 3) % U)
            for n in range(NC - 2, NC):
                multiply(n, n % U)
                take_dot(n, n % U)

            dve.wait_ge(s_dot, NC)
            dve.wait_ge(s_sde, NC)
            dve.wait_ge(s_ss, 2 * NC // U)
            al, do, sd = (z[:, :, :].rearrange("p c h -> p (c h)") for z in (s_sb, dot, sde))
            v.tensor_tensor(al, al, sd, ALU.add).then_inc(s_al, 1)
            dve.wait_ge(s_al, 1)
            v.tensor_tensor(al, al, do, ALU.add).then_inc(s_al, 1)
            dve.wait_ge(s_al, 2)
            v.scalar_tensor_tensor(out=al, in0=al, scalar=0.2, in1=al, op0=ALU.mult, op1=ALU.max).then_inc(s_al, 1)
            v.tensor_copy(lo_s[:, 0:NC], recs[1][:, 0:NC, :].bitcast(I32)[:, :, 1]).then_inc(s_lo, 1)
            dve.wait_ge(s_lo, 9)
            v.scalar_tensor_tensor(out=lo_si[:, :].bitcast(F32), in0=lo_s[:, 0:NC], scalar=1.0, in1=recs[1][:, 0:NC, 3:4].bitcast(BF16)[:, :, 1],
                                   op0=ALU.add, op1=ALU.mult).then_inc(s_lo, 1)
            dve.wait_ge(s_lo, 10)
            v.tensor_copy(sde[:, :, :], lo_si[:, :].bitcast(F32).unsqueeze(2).broadcast_to([P, NC, HEADS])).then_inc(s_al, 1)

            K = dotT
            v.memset(brk3[:, :, 0:P + 1:P], 0.0).then_inc(s_lo, 1)
            dve.wait_ge(s_alTs, 2 * len(quads))
            v.tensor_tensor(brk3[:, :, 1:P], K[:, :, 1:P], K[:, :, 0:P - 1], ALU.not_equal).then_inc(s_lo, 1)
            dve.wait_ge(s_lo, 12)
            v.tensor_scalar(brk, brk, -BIG, None, ALU.mult).then_inc(s_lo, 1)
            dve.wait_ge(s_lo, 13)
            for b in range(NB):
                ins = v.tensor_tensor_scan(sdeT[:, b, :], brk3[:, b, 0:P], alT[:, b, :], -BIG, ALU.add, ALU.max)
            ins.then_inc(s_lo, 1)
            dve.wait_ge(s_lo, 14)
            v.tensor_copy(ends[:, :, 0], sdeT[:, :, P - 1]).then_inc(s_lo, 1)
            v.tensor_copy(ends[:, :, 2], K[:, :, 0]).then_inc(s_lo, 1)
            v.tensor_copy(ends[:, :, 3], K[:, :, P - 1]).then_inc(s_lo, 1)
            dve.wait_ge(s_lo, 17)
            for b in range(NB):
                ins = v.tensor_tensor_scan(dotT[:, b, ::-1], brk3[:, b, 1:P + 1][:, ::-1], sdeT[:, b, ::-1], -BIG,
                                           ALU.add, ALU.max)
            ins.then_inc(s_al, 1)
            dve.wait_ge(s_al, 5)
            v.tensor_copy(ends[:, :, 1], dotT[:, :, 0]).then_inc(s_al, 1)
            dve.wait_ge(s_end, 32)
            for i in range(4):
                ins = v.tensor_copy(el[:, i, :].rearrange("h (b c) -> h c b", c=16), eh[:, :, :, i])
            ins.then_inc(s_al, 1)
            dve.wait_ge(s_al, 7)
            last, firstm, k0, k1, cont, sing, p_, o_ = (el[:, i, :] for i in range(8))
            v.memset(cont, 1.0).then_inc(s_al, 1)
            dve.wait_ge(s_al, 8)
            v.tensor_tensor(cont[:, 1:NC], k0[:, 1:NC], k1[:, 0:NC - 1], ALU.not_equal).then_inc(s_al, 1)
            v.tensor_tensor(sing, k0, k1, ALU.not_equal).then_inc(s_al, 1)
            dve.wait_ge(s_al, 10)
            v.tensor_tensor(p_, cont, sing, ALU.max).then_inc(s_al, 1)
            dve.wait_ge(s_al, 11)
            v.tensor_scalar(p_, p_, -BIG, None, ALU.mult).then_inc(s_al, 1)
            dve.wait_ge(s_al, 12)
            v.tensor_tensor_scan(o_, p_, last, -BIG, ALU.add, ALU.max).then_inc(s_al, 1)
            v.memset(k0, 1.0).then_inc(s_al, 1)
            dve.wait_ge(s_al, 14)
            v.tensor_copy(k0[:, 0:NC - 1], cont[:, 1:NC]).then_inc(s_al, 1)
            dve.wait_ge(s_al, 15)
            v.tensor_tensor(k1, k0, sing, ALU.max).then_inc(s_x0z, 1)
            dve.wait_ge(s_x0z, 3)
            v.tensor_scalar(k1, k1, -BIG, None, ALU.mult).then_inc(s_x0z, 1)
            dve.wait_ge(s_x0z, 4)
            v.tensor_tensor_scan(sing[:, ::-1], k1[:, ::-1], firstm[:, ::-1], -BIG, ALU.add, ALU.max).then_inc(s_x0z, 1)
            v.tensor_scalar(cont, cont, -BIG, None, ALU.mult).then_inc(s_x0z, 1)
            v.tensor_scalar(k0, k0, -BIG, None, ALU.mult).then_inc(s_x0z, 1)
            v.memset(last, 0.0).then_inc(s_x0z, 1)
            dve.wait_ge(s_x0z, 8)
            v.tensor_tensor(last[:, 1:NC], cont[:, 1:NC], o_[:, 0:NC - 1], ALU.add).then_inc(s_x0z, 1)
            v.tensor_scalar(last[:, 0:1], cont[:, 0:1], 1.0, None, ALU.mult).then_inc(s_x0z, 1)
            v.tensor_tensor(p_[:, 0:NC - 1], k0[:, 0:NC - 1], sing[:, 1:NC], ALU.add).then_inc(s_x0z, 1)
            v.tensor_scalar(p_[:, NC - 1:NC], k0[:, NC - 1:NC], 1.0, None, ALU.mult).then_inc(s_x0z, 1)
            dve.wait_ge(s_x0z, 12)
            v.tensor_copy(eo[:, :, :, 0], last.rearrange("h (b c) -> h c b", c=16)).then_inc(s_al, 1)
            v.tensor_copy(eo[:, :, :, 1], p_.rearrange("h (b c) -> h c b", c=16)).then_inc(s_al, 1)
            dve.wait_ge(s_end, 64)
            for b in range(NB):
                ins = v.tensor_tensor_scan(sdeT[:, b, :], brk3[:, b, 0:P], alT[:, b, :], cin[:, b, 0:1],
                                           ALU.add, ALU.max)
            ins.then_inc(s_lo, 1)
            dve.wait_ge(s_lo, 18)
            for b in range(NB):
                ins = v.tensor_tensor_scan(dotT[:, b, ::-1], brk3[:, b, 1:P + 1][:, ::-1], sdeT[:, b, ::-1],
                                           cin[:, b, 1:2], ALU.add, ALU.max)
            ins.then_inc(s_lo, 1)
            dve.wait_ge(s_lo, 19)
            for b in range(NB):
                v.tensor_tensor(alT[:, b, :], alT[:, b, :], dotT[:, b, :], ALU.subtract).then_inc(s_mx, 1)

            v.tensor_scalar(lo_si[:, :], recs[1][:, 0:NC, :].bitcast(I32)[:, :, 1], P - 1, None,
                            ALU.bitwise_and).then_inc(s_lo, 1)
            dve.wait_ge(s_lo, 20)
            v.tensor_copy(lo_s[:, 0:NC], lo_si[:, :]).then_inc(s_lo, 1)
            dve.wait_ge(s_lo, 21)
            v.scalar_tensor_tensor(out=lo_s[:, 0:NC], in0=lo_s[:, 0:NC], scalar=1.0, in1=recs[1][:, 0:NC, 3:4].bitcast(BF16)[:, :, 1],
                                   op0=ALU.add, op1=ALU.mult).then_inc(s_lo, 1)
            dve.wait_ge(s_lo, 22)
            v.tensor_scalar(lo_s[:, 0:NC], lo_s[:, 0:NC], -1.0, None, ALU.add).then_inc(s_lo, 1)
            dve.wait_ge(s_lo, 23)
            dve.wait_ge(s_clr, HOPS + 1)
            dve.wait_ge(s_exs, len(quads))
            sum_chunks(HOPS, 0)
            with dve.Fori(1, NC // U) as t:
                sum_chunks(HOPS, t)
            ws = windows(mybir.EngineType.DVE, win_late[1], NC, LAG)
            for n in range(LAG):
                add(HOPS, HOPS * NC + NC - LAG + n, U - LAG + n, ws[n])
            dve.wait_ge(s_add, NC * (HOPS + 1))
            q = LN_STEPS
            v.tensor_scalar(x0[:, :, D:HX], acc[:, :, D:HX], 1e-10, None, ALU.max).then_inc(s_ln, 1)
            dve.wait_ge(s_ln, q + 1)
            v.reciprocal(s_src[:, :, :], x0[:, :, D:HX]).then_inc(s_ln, 1)
            dve.wait_ge(s_ln, q + 2)

            def divide(w):
                a = acc[:, bass.ds(w, 1), 0:D].rearrange("p c (h d) -> p (c h) d", h=HEADS)
                v.tensor_tensor(a, a, s_src[:, bass.ds(w, 1), :].rearrange("p c h -> p (c h)").unsqueeze(2)
                                .broadcast_to([P, HEADS, HD]), ALU.mult).then_inc(s_div, 1)

            def stats(w):
                dve.wait_ge(s_res, w + 1)
                v.bn_stats(x0[:, bass.ds(w, 1), 0:6].rearrange("p c d -> p (c d)"),
                           hcur[:, bass.ds(w, 1), :].rearrange("p c d -> p (c d)")).then_inc(s_bn, 1)

            for w in range(3):
                divide(w)
            with dve.Fori(3, NW) as w:
                divide(w)
                stats(w - 3)
            for w in range(NW - 3, NW):
                stats(w)
            deviations(q + 2, 1, x0)
            for w in range(FULLW + 1):
                normalise(w, s_fin)


_INS = ['x', 'src', 'dst', 'edge_attr_3', 'edge_weight', 'L0_gnn_Wn', 'L0_gnn_bn', 'L0_gnn_Ws', 'L0_gnn_bs',
        'L1_gnn_W', 'L1_gnn_a_src', 'L1_gnn_a_dst', 'L1_gnn_edge_W', 'L1_gnn_edge_b', 'L1_gnn_bias']


def kernel(**inputs):
    import concourse.bacc as bacc
    from concourse.bass_utils import run_bass_kernel_spmd

    nc = bacc.Bacc("TRN2", target_bir_lowering=False, num_devices=1)
    arrays, args = {}, []
    for name in _INS:
        a = np.ascontiguousarray(inputs[name])
        arrays[f"in_{name}"] = a
        args.append(nc.dram_tensor(f"in_{name}", a.shape, mybir.dt.from_np(a.dtype), kind="ExternalInput").ap())
    out = nc.dram_tensor("out_0", (N, D), F32, kind="ExternalOutput").ap()
    build(nc, *args, out)
    r = run_bass_kernel_spmd(nc, [arrays], core_ids=[0])
    return r.results[0]["out_0"]
```
